# Optimizing a Trainium2 kernel written in Bass

```python
import numpy as np
import jax
import jax.numpy as jnp

def _softmax(x, axis=-1):
    return jax.nn.softmax(x, axis=axis)

def _gelu(x):
    return jax.nn.gelu(x, approximate=True)

def _silu(x):
    return jax.nn.silu(x)

def _sigmoid(x):
    return jax.nn.sigmoid(x)

def _layernorm(x, axis=-1, eps=1e-05):
    m = jnp.mean(x, axis=axis, keepdims=True)
    v = jnp.var(x, axis=axis, keepdims=True)
    return (x - m) / jnp.sqrt(v + eps)

def _scatter_add(tgt, idx, src, axis=0):
    return tgt.at[idx].add(src)

def _segment_sum(src, seg, n):
    return jax.ops.segment_sum(src, seg, n)
kernel_name = 'mk_recurrent_d4_jaxref_r8_e27625'

def setup_inputs(seed: int=0):
    np.random.seed(seed)
    _w = jnp.asarray

    def _L0_attn_setup():
        import jax, jax.numpy as jnp
        import numpy as np
        B, T, D = (2, 256, 512)
        H = 32
        HKV = 1
        HD = D // H
        key = jax.random.key(seed)
        ks = jax.random.split(key, 9)
        s = lambda fan_in: 1.0 / np.sqrt(fan_in)
        return {'x': jax.random.normal(ks[0], (B, T, D), dtype=jnp.float32), 'wq_w': jax.random.normal(ks[1], (H * HD, D), dtype=jnp.float32) * s(D), 'wq_b': jax.random.normal(ks[2], (H * HD,), dtype=jnp.float32) * 0.02, 'wk_w': jax.random.normal(ks[3], (HKV * HD, D), dtype=jnp.float32) * s(D), 'wk_b': jax.random.normal(ks[4], (HKV * HD,), dtype=jnp.float32) * 0.02, 'wv_w': jax.random.normal(ks[5], (HKV * HD, D), dtype=jnp.float32) * s(D), 'wv_b': jax.random.normal(ks[6], (HKV * HD,), dtype=jnp.float32) * 0.02, 'wo_w': jax.random.normal(ks[7], (D, H * HD), dtype=jnp.float32) * s(H * HD), 'wo_b': jax.random.normal(ks[8], (D,), dtype=jnp.float32) * 0.02}
    _L0_attn_in = _L0_attn_setup()

    def _L0_ffn_setup():
        import jax, jax.numpy as jnp
        import numpy as np
        B, S, H, I, R = (4, 32, 512, 1792, 4)

        def _anemll_linear(x, w, su, sv):
            w_eff = w * (su @ sv)
            return jnp.einsum('bsh,oh->bso', x, w_eff)
        key = jax.random.key(seed)
        ks = jax.random.split(key, 10)
        sd = 0.02
        return {'x': jax.random.normal(ks[0], (B, S, H), dtype=jnp.float32), 'gate_w': jax.random.normal(ks[1], (I, H), dtype=jnp.float32) * sd, 'gate_su': jax.random.normal(ks[2], (I, R), dtype=jnp.float32) * 0.5, 'gate_sv': jax.random.normal(ks[3], (R, H), dtype=jnp.float32) * 0.5, 'up_w': jax.random.normal(ks[4], (I, H), dtype=jnp.float32) * sd, 'up_su': jax.random.normal(ks[5], (I, R), dtype=jnp.float32) * 0.5, 'up_sv': jax.random.normal(ks[6], (R, H), dtype=jnp.float32) * 0.5, 'down_w': jax.random.normal(ks[7], (H, I), dtype=jnp.float32) * sd, 'down_su': jax.random.normal(ks[8], (H, R), dtype=jnp.float32) * 0.5, 'down_sv': jax.random.normal(ks[9], (R, I), dtype=jnp.float32) * 0.5}
    _L0_ffn_in = _L0_ffn_setup()

    def _L1_attn_setup():
        import jax, jax.numpy as jnp
        import numpy as np
        B, S, HIDDEN = (2, 256, 512)
        TP = 2
        PART = HIDDEN // TP
        NUM_HEADS = 16 // TP
        HEAD_DIM = PART // NUM_HEADS
        MASKED_BIAS = -10000.0
        key = jax.random.key(seed)
        k_x, k_wq, k_bq, k_wo, k_bo = jax.random.split(key, 5)
        x = jax.random.normal(k_x, (B, S, HIDDEN), dtype=jnp.float32)
        w_qkv = jax.random.normal(k_wq, (3 * PART, HIDDEN), dtype=jnp.float32) * 0.02
        b_qkv = jax.random.normal(k_bq, (3 * PART,), dtype=jnp.float32) * 0.02
        w_o = jax.random.normal(k_wo, (HIDDEN, PART), dtype=jnp.float32) * 0.02
        b_o = jax.random.normal(k_bo, (HIDDEN,), dtype=jnp.float32) * 0.02
        return {'x': x, 'w_qkv': w_qkv, 'b_qkv': b_qkv, 'w_o': w_o, 'b_o': b_o}
    _L1_attn_in = _L1_attn_setup()

    def _L1_ffn_setup():
        import jax, jax.numpy as jnp
        import numpy as np
        N_STREAMS = 4
        DIM = 128
        SINKHORN_ITERS = 50
        SINKHORN_TAU = 0.1
        RMS_EPS = 1.1920929e-07

        def sinkhorn_log(logits, num_iters=SINKHORN_ITERS, tau=SINKHORN_TAU):
            Z = logits / tau
            u0 = jnp.zeros(Z.shape[:-1], Z.dtype)
            v0 = jnp.zeros_like(u0)

            def step(carry, _):
                u, v = carry
                u = -jax.nn.logsumexp(Z + v[..., None, :], axis=-1)
                v = -jax.nn.logsumexp(Z + u[..., :, None], axis=-2)
                return ((u, v), None)
            (u, v), _ = jax.lax.scan(step, (u0, v0), None, length=num_iters)
            return jnp.exp(Z + u[..., :, None] + v[..., None, :])
        key = jax.random.key(seed)
        ks = jax.random.split(key, 6)
        B, T = (4, 256)
        n, C = (N_STREAMS, DIM)
        wd = n * C
        x = jax.random.normal(ks[0], (B, T, wd), dtype=jnp.float32)
        W_res = 0.01 * jax.random.normal(ks[1], (n * n, wd), dtype=jnp.float32)
        W_pre = 0.01 * jax.random.normal(ks[2], (n, wd), dtype=jnp.float32)
        W_post = 0.01 * jax.random.normal(ks[3], (n, wd), dtype=jnp.float32)
        H_res_base = jnp.full((n, n), -0.5, dtype=jnp.float32)
        H_res_base = H_res_base.at[jnp.arange(n), jnp.arange(n)].set(0.0)
        H_pre_base = jnp.zeros((n,), dtype=jnp.float32).at[0].set(1.0)
        H_post_base = jnp.zeros((n,), dtype=jnp.float32)
        gate = jnp.array([5.0], dtype=jnp.float32)
        W_branch = 1.0 / np.sqrt(C) * jax.random.normal(ks[4], (C, C), dtype=jnp.float32)
        return {'x': x, 'W_res': W_res, 'W_pre': W_pre, 'W_post': W_post, 'H_res_base': H_res_base, 'H_pre_base': H_pre_base, 'H_post_base': H_post_base, 'gate': gate, 'W_branch': W_branch}
    _L1_ffn_in = _L1_ffn_setup()

    def _L2_attn_setup():
        import jax, jax.numpy as jnp
        import numpy as np
        HIDDEN = 512
        N_HEADS = 32
        N_KV_HEADS = 8
        HEAD_DIM = HIDDEN // N_HEADS
        N_REP = N_HEADS // N_KV_HEADS
        KV_DIM = N_KV_HEADS * HEAD_DIM

        def _kaiming_uniform(key, out_f, in_f):
            bound = 1.0 / np.sqrt(in_f)
            return jax.random.uniform(key, (out_f, in_f), jnp.float32, -bound, bound)

        def bitnet_linear(x, weight, scale_param):
            s = jnp.maximum(jnp.mean(jnp.abs(weight), axis=1), 1e-08)
            binary_w = jnp.sign(weight / s[:, None])
            y = jnp.einsum('bsi,oi->bso', x, binary_w)
            y = y * (s * scale_param)[None, None, :]
            return jnp.nan_to_num(y, nan=0.0, posinf=1000000.0, neginf=-1000000.0)
        key = jax.random.key(seed)
        ks = jax.random.split(key, 5)
        return {'hidden_states': jax.random.normal(ks[0], (1, 256, HIDDEN), jnp.float32), 'q_weight': _kaiming_uniform(ks[1], HIDDEN, HIDDEN), 'q_scale': jnp.ones((HIDDEN,), jnp.float32), 'k_weight': _kaiming_uniform(ks[2], KV_DIM, HIDDEN), 'k_scale': jnp.ones((KV_DIM,), jnp.float32), 'v_weight': _kaiming_uniform(ks[3], KV_DIM, HIDDEN), 'v_scale': jnp.ones((KV_DIM,), jnp.float32), 'o_weight': _kaiming_uniform(ks[4], HIDDEN, HIDDEN), 'o_scale': jnp.ones((HIDDEN,), jnp.float32)}
    _L2_attn_in = _L2_attn_setup()

    def _L2_ffn_setup():
        import jax, jax.numpy as jnp
        import numpy as np
        R = 16
        LORA_ALPHA = 16
        SCALING = LORA_ALPHA / R
        key = jax.random.key(seed)
        kx, kr, ka = jax.random.split(key, 3)
        B, S, D, DO, E = (4, 256, 512, 512, 8)
        x = jax.random.normal(kx, (B, S, D), dtype=jnp.float32)
        bound_r = 1.0 / np.sqrt(D)
        route_w = jax.random.uniform(kr, (E, D), jnp.float32, -bound_r, bound_r)
        bound_a = 1.0 / np.sqrt(D)
        A = jax.random.uniform(ka, (E, R, D), jnp.float32, -bound_a, bound_a)
        kb = jax.random.fold_in(key, 7)
        Bw = jax.random.normal(kb, (E, DO, R), dtype=jnp.float32) * 0.02
        return {'x': x, 'route_w': route_w, 'A': A, 'Bw': Bw}
    _L2_ffn_in = _L2_ffn_setup()

    def _L3_attn_setup():
        import jax, jax.numpy as jnp
        import numpy as np
        B, S, E, H = (2, 256, 512, 32)
        D = E // H
        ROPE_BASE = 10000.0
        MASK_VAL = -66504.0

        def _rope(x, cos, sin):
            x1, x2 = jnp.split(x, 2, axis=-1)
            return jnp.concatenate([x1 * cos - x2 * sin, x2 * cos + x1 * sin], axis=-1)
        key = jax.random.key(seed)
        k1, k2, k3, k4, k5 = jax.random.split(key, 5)
        return {'hidden_states': jax.random.normal(k1, (B, S, E), dtype=jnp.float32), 'qkv_w': jax.random.normal(k2, (E, 3 * E), dtype=jnp.float32) * 0.02, 'qkv_b': jax.random.normal(k3, (3 * E,), dtype=jnp.float32) * 0.02, 'out_w': jax.random.normal(k4, (E, E), dtype=jnp.float32) * 0.02, 'out_b': jax.random.normal(k5, (E,), dtype=jnp.float32) * 0.02}
    _L3_attn_in = _L3_attn_setup()

    def _L3_ffn_setup():
        import jax, jax.numpy as jnp
        import numpy as np
        B, S, D, O, E, R = (2, 512, 512, 512, 8, 16)
        TOP_K = 2
        SCALING = 32.0 / 16.0
        key = jax.random.key(seed)
        k = jax.random.split(key, 6)
        x = jax.random.normal(k[0], (B, S, D), dtype=jnp.float32)
        W_base = jax.random.normal(k[1], (O, D), dtype=jnp.float32) * 0.02
        b_base = jax.random.normal(k[2], (O,), dtype=jnp.float32) * 0.02
        W_router = jax.random.normal(k[3], (E, D), dtype=jnp.float32) * 0.01
        lora_A = jax.random.normal(k[4], (E, R, D), dtype=jnp.float32) * (1.0 / np.sqrt(D))
        lora_B = jax.random.normal(k[5], (E, O, R), dtype=jnp.float32) * 0.02
        return {'x': x, 'W_base': W_base, 'b_base': b_base, 'W_router': W_router, 'lora_A': lora_A, 'lora_B': lora_B}
    _L3_ffn_in = _L3_ffn_setup()
    _d = {'L0_attn_x': _L0_attn_in['x'], 'L0_attn_wq_w': _L0_attn_in['wq_w'], 'L0_attn_wq_b': _L0_attn_in['wq_b'], 'L0_attn_wk_w': _L0_attn_in['wk_w'], 'L0_attn_wk_b': _L0_attn_in['wk_b'], 'L0_attn_wv_w': _L0_attn_in['wv_w'], 'L0_attn_wv_b': _L0_attn_in['wv_b'], 'L0_attn_wo_w': _L0_attn_in['wo_w'], 'L0_attn_wo_b': _L0_attn_in['wo_b'], 'L0_ffn_gate_w': _L0_ffn_in['gate_w'], 'L0_ffn_gate_su': _L0_ffn_in['gate_su'], 'L0_ffn_gate_sv': _L0_ffn_in['gate_sv'], 'L0_ffn_up_w': _L0_ffn_in['up_w'], 'L0_ffn_up_su': _L0_ffn_in['up_su'], 'L0_ffn_up_sv': _L0_ffn_in['up_sv'], 'L0_ffn_down_w': _L0_ffn_in['down_w'], 'L0_ffn_down_su': _L0_ffn_in['down_su'], 'L0_ffn_down_sv': _L0_ffn_in['down_sv'], 'L1_attn_w_qkv': _L1_attn_in['w_qkv'], 'L1_attn_b_qkv': _L1_attn_in['b_qkv'], 'L1_attn_w_o': _L1_attn_in['w_o'], 'L1_attn_b_o': _L1_attn_in['b_o'], 'L1_ffn_W_res': _L1_ffn_in['W_res'], 'L1_ffn_W_pre': _L1_ffn_in['W_pre'], 'L1_ffn_W_post': _L1_ffn_in['W_post'], 'L1_ffn_H_res_base': _L1_ffn_in['H_res_base'], 'L1_ffn_H_pre_base': _L1_ffn_in['H_pre_base'], 'L1_ffn_H_post_base': _L1_ffn_in['H_post_base'], 'L1_ffn_gate': _L1_ffn_in['gate'], 'L1_ffn_W_branch': _L1_ffn_in['W_branch'], 'L2_attn_q_weight': _L2_attn_in['q_weight'], 'L2_attn_q_scale': _L2_attn_in['q_scale'], 'L2_attn_k_weight': _L2_attn_in['k_weight'], 'L2_attn_k_scale': _L2_attn_in['k_scale'], 'L2_attn_v_weight': _L2_attn_in['v_weight'], 'L2_attn_v_scale': _L2_attn_in['v_scale'], 'L2_attn_o_weight': _L2_attn_in['o_weight'], 'L2_attn_o_scale': _L2_attn_in['o_scale'], 'L2_ffn_route_w': _L2_ffn_in['route_w'], 'L2_ffn_A': _L2_ffn_in['A'], 'L2_ffn_Bw': _L2_ffn_in['Bw'], 'L3_attn_qkv_w': _L3_attn_in['qkv_w'], 'L3_attn_qkv_b': _L3_attn_in['qkv_b'], 'L3_attn_out_w': _L3_attn_in['out_w'], 'L3_attn_out_b': _L3_attn_in['out_b'], 'L3_ffn_W_base': _L3_ffn_in['W_base'], 'L3_ffn_b_base': _L3_ffn_in['b_base'], 'L3_ffn_W_router': _L3_ffn_in['W_router'], 'L3_ffn_lora_A': _L3_ffn_in['lora_A'], 'L3_ffn_lora_B': _L3_ffn_in['lora_B']}
    _x0 = _d['L0_attn_x']
    _d['L0_attn_x'] = jax.random.normal(jax.random.fold_in(jax.random.key(seed), 1), (2, 512, 512), dtype=_x0.dtype)
    del _x0
    return _d

def reference(L0_attn_x, L0_attn_wq_w, L0_attn_wq_b, L0_attn_wk_w, L0_attn_wk_b, L0_attn_wv_w, L0_attn_wv_b, L0_attn_wo_w, L0_attn_wo_b, L0_ffn_gate_w, L0_ffn_gate_su, L0_ffn_gate_sv, L0_ffn_up_w, L0_ffn_up_su, L0_ffn_up_sv, L0_ffn_down_w, L0_ffn_down_su, L0_ffn_down_sv, L1_attn_w_qkv, L1_attn_b_qkv, L1_attn_w_o, L1_attn_b_o, L1_ffn_W_res, L1_ffn_W_pre, L1_ffn_W_post, L1_ffn_H_res_base, L1_ffn_H_pre_base, L1_ffn_H_post_base, L1_ffn_gate, L1_ffn_W_branch, L2_attn_q_weight, L2_attn_q_scale, L2_attn_k_weight, L2_attn_k_scale, L2_attn_v_weight, L2_attn_v_scale, L2_attn_o_weight, L2_attn_o_scale, L2_ffn_route_w, L2_ffn_A, L2_ffn_Bw, L3_attn_qkv_w, L3_attn_qkv_b, L3_attn_out_w, L3_attn_out_b, L3_ffn_W_base, L3_ffn_b_base, L3_ffn_W_router, L3_ffn_lora_A, L3_ffn_lora_B):

    def _L0_attn_ref(x, wq_w, wq_b, wk_w, wk_b, wv_w, wv_b, wo_w, wo_b):
        import jax, jax.numpy as jnp
        import numpy as np
        B, T, D = (2, 256, 512)
        H = 32
        HKV = 1
        HD = D // H
        b, t, d = x.shape
        q = (x @ wq_w.T + wq_b).reshape(b, t, H, HD)
        k = (x @ wk_w.T + wk_b).reshape(b, t, HKV, HD)
        v = (x @ wv_w.T + wv_b).reshape(b, t, HKV, HD)
        k1 = k[:, :, 0, :]
        v1 = v[:, :, 0, :]
        scores = jnp.einsum('bqhd,bkd->bhqk', q, k1) / jnp.sqrt(jnp.float32(HD))
        causal = jnp.tril(jnp.ones((t, t), dtype=bool))
        scores = jnp.where(causal, scores, -jnp.inf)
        weights = jax.nn.softmax(scores, axis=-1)
        attn = jnp.einsum('bhqk,bkd->bqhd', weights, v1)
        attn = attn.reshape(b, t, H * HD)
        return attn @ wo_w.T + wo_b

    def _L0_ffn_ref(x, gate_w, gate_su, gate_sv, up_w, up_su, up_sv, down_w, down_su, down_sv):
        import jax, jax.numpy as jnp
        import numpy as np
        B, S, H, I, R = (4, 32, 512, 1792, 4)

        def _anemll_linear(x, w, su, sv):
            w_eff = w * (su @ sv)
            return jnp.einsum('bsh,oh->bso', x, w_eff)
        a = _anemll_linear(x, gate_w, gate_su, gate_sv)
        b = _anemll_linear(x, up_w, up_su, up_sv)
        d = jax.nn.silu(a) * b
        return _anemll_linear(d, down_w, down_su, down_sv)

    def _L1_attn_ref(x, w_qkv, b_qkv, w_o, b_o):
        import jax, jax.numpy as jnp
        import numpy as np
        B, S, HIDDEN = (2, 256, 512)
        TP = 2
        PART = HIDDEN // TP
        NUM_HEADS = 16 // TP
        HEAD_DIM = PART // NUM_HEADS
        MASKED_BIAS = -10000.0
        b, s, _ = x.shape
        qkv = x @ w_qkv.T + b_qkv
        q, k, v = jnp.split(qkv, 3, axis=-1)

        def to_heads(a):
            return a.reshape(b, s, NUM_HEADS, HEAD_DIM).transpose(0, 2, 1, 3)
        q, k, v = (to_heads(q), to_heads(k), to_heads(v))
        scores = jnp.einsum('bhfc,bhtc->bhft', k, q)
        causal = jnp.triu(jnp.ones((s, s), dtype=bool))
        scores = jnp.where(causal[None, None], scores, MASKED_BIAS)
        attn = jax.nn.softmax(scores, axis=-2)
        vals = jnp.einsum('bhft,bhfc->bhtc', attn, v)
        vals = vals.transpose(0, 2, 1, 3).reshape(b, s, PART)
        out = vals @ w_o.T + b_o
        return out

    def _L1_ffn_ref(x, W_res, W_pre, W_post, H_res_base, H_pre_base, H_post_base, gate, W_branch):
        import jax, jax.numpy as jnp
        import numpy as np
        N_STREAMS = 4
        DIM = 128
        SINKHORN_ITERS = 50
        SINKHORN_TAU = 0.1
        RMS_EPS = 1.1920929e-07

        def sinkhorn_log(logits, num_iters=SINKHORN_ITERS, tau=SINKHORN_TAU):
            Z = logits / tau
            u0 = jnp.zeros(Z.shape[:-1], Z.dtype)
            v0 = jnp.zeros_like(u0)

            def step(carry, _):
                u, v = carry
                u = -jax.nn.logsumexp(Z + v[..., None, :], axis=-1)
                v = -jax.nn.logsumexp(Z + u[..., :, None], axis=-2)
                return ((u, v), None)
            (u, v), _ = jax.lax.scan(step, (u0, v0), None, length=num_iters)
            return jnp.exp(Z + u[..., :, None] + v[..., None, :])
        B, T, nC = x.shape
        n = N_STREAMS
        C = nC // n
        x_norm = x * jax.lax.rsqrt(jnp.mean(x * x, axis=-1, keepdims=True) + RMS_EPS)
        H_res_logits = (x_norm @ W_res.T).reshape(B, T, n, n) + H_res_base
        H_pre_logits = x_norm @ W_pre.T + H_pre_base
        H_post_logits = x_norm @ W_post.T + H_post_base
        H_res = sinkhorn_log(H_res_logits)
        H_pre = jax.nn.softmax(H_pre_logits, axis=-1)
        H_post = jax.nn.softmax(H_post_logits, axis=-1)
        g = jax.nn.sigmoid(gate)[0]
        I = jnp.eye(n, dtype=H_res.dtype)
        H_res = (1.0 - g) * I + g * H_res
        x_streams = x.reshape(B, T, n, C)
        x_pre = jnp.einsum('btnc,btn->btc', x_streams, H_pre)
        y = x_pre @ W_branch
        x_mixed = jnp.einsum('btij,btjc->btic', H_res, x_streams)
        y_distributed = jnp.einsum('btc,btn->btnc', y, H_post)
        return (x_mixed + y_distributed).reshape(B, T, nC)

    def _L2_attn_ref(hidden_states, q_weight, q_scale, k_weight, k_scale, v_weight, v_scale, o_weight, o_scale):
        import jax, jax.numpy as jnp
        import numpy as np
        HIDDEN = 512
        N_HEADS = 32
        N_KV_HEADS = 8
        HEAD_DIM = HIDDEN // N_HEADS
        N_REP = N_HEADS // N_KV_HEADS
        KV_DIM = N_KV_HEADS * HEAD_DIM

        def _kaiming_uniform(key, out_f, in_f):
            bound = 1.0 / np.sqrt(in_f)
            return jax.random.uniform(key, (out_f, in_f), jnp.float32, -bound, bound)

        def bitnet_linear(x, weight, scale_param):
            s = jnp.maximum(jnp.mean(jnp.abs(weight), axis=1), 1e-08)
            binary_w = jnp.sign(weight / s[:, None])
            y = jnp.einsum('bsi,oi->bso', x, binary_w)
            y = y * (s * scale_param)[None, None, :]
            return jnp.nan_to_num(y, nan=0.0, posinf=1000000.0, neginf=-1000000.0)
        b, s, _ = hidden_states.shape
        q = bitnet_linear(hidden_states, q_weight, q_scale)
        k = bitnet_linear(hidden_states, k_weight, k_scale)
        v = bitnet_linear(hidden_states, v_weight, v_scale)
        q = q.reshape(b, s, N_HEADS, HEAD_DIM).transpose(0, 2, 1, 3)
        k = k.reshape(b, s, N_KV_HEADS, HEAD_DIM).transpose(0, 2, 1, 3)
        v = v.reshape(b, s, N_KV_HEADS, HEAD_DIM).transpose(0, 2, 1, 3)
        k = jnp.repeat(k, N_REP, axis=1)
        v = jnp.repeat(v, N_REP, axis=1)
        scores = jnp.einsum('bhqd,bhkd->bhqk', q, k) / np.sqrt(HEAD_DIM)
        attn = jax.nn.softmax(scores, axis=-1)
        out = jnp.einsum('bhqk,bhkd->bhqd', attn, v)
        out = out.transpose(0, 2, 1, 3).reshape(b, s, HIDDEN)
        return bitnet_linear(out, o_weight, o_scale)

    def _L2_ffn_ref(x, route_w, A, Bw):
        import jax, jax.numpy as jnp
        import numpy as np
        R = 16
        LORA_ALPHA = 16
        SCALING = LORA_ALPHA / R
        logits = jnp.einsum('bsd,ed->bse', x, route_w)
        topk_v, topk_idx = jax.lax.top_k(logits, 1)
        E = logits.shape[-1]
        route_weight = jax.nn.one_hot(topk_idx[..., 0], E, dtype=logits.dtype) * topk_v
        h = jnp.einsum('bsd,erd->bser', x, A)
        wh = route_weight[..., None] * h
        out = jnp.einsum('bser,eor->bso', wh, Bw) * SCALING
        return out

    def _L3_attn_ref(hidden_states, qkv_w, qkv_b, out_w, out_b):
        import jax, jax.numpy as jnp
        import numpy as np
        B, S, E, H = (2, 256, 512, 32)
        D = E // H
        ROPE_BASE = 10000.0
        MASK_VAL = -66504.0

        def _rope(x, cos, sin):
            x1, x2 = jnp.split(x, 2, axis=-1)
            return jnp.concatenate([x1 * cos - x2 * sin, x2 * cos + x1 * sin], axis=-1)
        b, s, e = hidden_states.shape
        qkv = hidden_states @ qkv_w + qkv_b
        q, k, v = jnp.split(qkv, 3, axis=-1)
        q = q.reshape(b, s, H, D)
        k = k.reshape(b, s, H, D)
        v = v.reshape(b, s, H, D)
        half = D // 2
        inv_freq = 1.0 / ROPE_BASE ** (jnp.arange(0, half, dtype=jnp.float32) / half)
        ang = jnp.arange(s, dtype=jnp.float32)[:, None] * inv_freq[None, :]
        cos = jnp.cos(ang)[None, :, None, :]
        sin = jnp.sin(ang)[None, :, None, :]
        q = _rope(q, cos, sin)
        k = _rope(k, cos, sin)
        scale = 1.0 / jnp.sqrt(jnp.asarray(D, dtype=hidden_states.dtype))
        scores = jnp.einsum('bqhd,bkhd->bhqk', q, k) * scale
        causal = jnp.tril(jnp.ones((s, s), dtype=scores.dtype))
        scores = scores + (1.0 - causal) * MASK_VAL
        probs = jax.nn.softmax(scores, axis=-1)
        ctx = jnp.einsum('bhqk,bkhd->bqhd', probs, v).reshape(b, s, e)
        return ctx @ out_w + out_b

    def _L3_ffn_ref(x, W_base, b_base, W_router, lora_A, lora_B):
        import jax, jax.numpy as jnp
        import numpy as np
        B, S, D, O, E, R = (2, 512, 512, 512, 8, 16)
        TOP_K = 2
        SCALING = 32.0 / 16.0
        d = x.shape[-1]
        n_experts = W_router.shape[0]
        xf = x.reshape(-1, d)
        logits = xf @ W_router.T
        probs = jax.nn.softmax(logits, axis=-1)
        topk_p, topk_i = jax.lax.top_k(probs, TOP_K)
        topk_p = topk_p / jnp.sum(topk_p, axis=-1, keepdims=True)
        w = jnp.sum(jax.nn.one_hot(topk_i, n_experts, dtype=xf.dtype) * topk_p[..., None], axis=1)
        h = jnp.einsum('td,erd->ter', xf, lora_A)
        lora_out = jnp.einsum('ter,eor,te->to', h, lora_B, w) * SCALING
        base = x @ W_base.T + b_base
        return base + lora_out.reshape(x.shape[:-1] + (W_base.shape[0],))
    x = L0_attn_x
    xn = _layernorm(x, axis=-1)
    s = _L0_attn_ref(xn, L0_attn_wq_w, L0_attn_wq_b, L0_attn_wk_w, L0_attn_wk_b, L0_attn_wv_w, L0_attn_wv_b, L0_attn_wo_w, L0_attn_wo_b)
    g = _silu(_L0_ffn_ref(xn, L0_ffn_gate_w, L0_ffn_gate_su, L0_ffn_gate_sv, L0_ffn_up_w, L0_ffn_up_su, L0_ffn_up_sv, L0_ffn_down_w, L0_ffn_down_su, L0_ffn_down_sv))
    x = x + s * g
    xn = _layernorm(x, axis=-1)
    s = _L1_attn_ref(xn, L1_attn_w_qkv, L1_attn_b_qkv, L1_attn_w_o, L1_attn_b_o)
    g = _silu(_L1_ffn_ref(xn, L1_ffn_W_res, L1_ffn_W_pre, L1_ffn_W_post, L1_ffn_H_res_base, L1_ffn_H_pre_base, L1_ffn_H_post_base, L1_ffn_gate, L1_ffn_W_branch))
    x = x + s * g
    xn = _layernorm(x, axis=-1)
    s = _L2_attn_ref(xn, L2_attn_q_weight, L2_attn_q_scale, L2_attn_k_weight, L2_attn_k_scale, L2_attn_v_weight, L2_attn_v_scale, L2_attn_o_weight, L2_attn_o_scale)
    g = _silu(_L2_ffn_ref(xn, L2_ffn_route_w, L2_ffn_A, L2_ffn_Bw))
    x = x + s * g
    xn = _layernorm(x, axis=-1)
    s = _L3_attn_ref(xn, L3_attn_qkv_w, L3_attn_qkv_b, L3_attn_out_w, L3_attn_out_b)
    g = _silu(_L3_ffn_ref(xn, L3_ffn_W_base, L3_ffn_b_base, L3_ffn_W_router, L3_ffn_lora_A, L3_ffn_lora_B))
    x = x + s * g
    return x

_drawn_inputs = setup_inputs


def setup_inputs(seed=0):
    import zlib

    import numpy as np

    out = dict(_drawn_inputs(seed))
    spreads = {'L1_ffn_H_post_base': (0.0, 0.1),
     'L2_attn_q_scale': (1.0, 0.2),
     'L2_attn_k_scale': (1.0, 0.2),
     'L2_attn_v_scale': (1.0, 0.2),
     'L2_attn_o_scale': (1.0, 0.2)}
    factors = {}
    for name, (base, spread) in spreads.items():
        noise = np.random.default_rng([zlib.crc32(name.encode()), seed]).standard_normal(out[name].shape)
        drawn = base * np.exp(spread * noise) if base else spread * noise
        out[name] = jnp.asarray(drawn.astype(out[name].dtype))
    for name, factor in factors.items():
        out[name] = (out[name] * factor).astype(out[name].dtype)
    return out
```

```python
from contextlib import ExitStack

import numpy as np

import concourse.bass as bass
from concourse import mybir

ALU = mybir.AluOpType
ACT = mybir.ActivationFunctionType
AX = mybir.AxisListType
F32 = mybir.dt.float32
F16 = mybir.dt.float16
BF16 = mybir.dt.bfloat16
ds = bass.ds

P = 128
D = 512
KC = D // P
NB = 2
T = 512
NI = T // P
NT = NB * NI
BANK = 512
PRODUCTS = ((0, 0), (1, 0), (0, 1))
MASKED = -1.0e30
LN_EPS = 1e-5


def wait_pos(eng, sem, value):
    if isinstance(value, int) and value <= 0:
        return
    eng.wait_ge(sem, value)


class Phase:

    held = []

    def __init__(self, nc, tag, names):
        self.nc, self.tag, self.names, self.stack = nc, tag, names.split(), ExitStack()

    def __enter__(self):
        sems = [self.nc.alloc_semaphore(f"{self.tag}_{n}") for n in self.names]
        Phase.held += sems
        return (self.stack.enter_context(self.nc.Block()), *sems)

    def __exit__(self, *exc):
        return self.stack.__exit__(*exc)


def product(pe, out, left, right, chunks, pairs=PRODUCTS, first=True, last=True):
    n = len(pairs) * len(chunks)
    k = 0
    for c in chunks:
        for a, b in pairs:
            mm = pe.matmul(out, left(a, c), right(b, c), start=first and k == 0, stop=last and k == n - 1)
            k += 1
    return mm


def load_constants(nc, g, ins):
    with Phase(nc, "const", "ident_here zeroed masked") as (block, ident_here, zeroed, masked):
        @block.sync
        def _(sp):
            sp.dma_start(g.ident[:, :], ins["ident"]).then_inc(ident_here, 16)
            sp.wait_ge(ident_here, 16)

        @block.vector
        def _(dve):
            dve.memset(g.ones[:, :], 1.0)
            dve.wait_ge(ident_here, 16)
            dve.tensor_copy(g.ident_b[:, :], g.ident[:, :])

        @block.gpsimd
        def _(pool):
            pool.memset(g.mask_qk[:, :], 0.0).then_inc(zeroed, 1)
            pool.memset(g.mask_kq[:, :], 0.0).then_inc(zeroed, 1)
            pool.wait_ge(zeroed, 2)
            pool.affine_select(out=g.mask_qk[:, :], in_=g.mask_qk[:, :], compare_op=ALU.is_ge, fill=MASKED,
                               base=0, pattern=[[-1, P]], channel_multiplier=1).then_inc(masked, 1)
            pool.affine_select(out=g.mask_kq[:, :], in_=g.mask_kq[:, :], compare_op=ALU.is_ge, fill=MASKED,
                               base=0, pattern=[[1, P]], channel_multiplier=-1).then_inc(masked, 1)
            pool.wait_ge(masked, 2)


def norm_and_split(nc, tag, g, weights, x_in=None, small=()):
    with Phase(nc, tag, "x_here stats aggr var std rstd normed turned hi lo w_hi w_lo small_here "
               + " ".join(f"w_here{i}" for i in range(len(weights)))) as (
            block, x_here, stats, aggr, var, std, rstd, normed, turned, hi, lo, w_hi, w_lo, small_here, *w_here), \
            nc.psum_tensor(f"{tag}_pt", [P, 8, BANK], F32) as pt, \
            nc.sbuf_tensor(f"{tag}_st", [P, NT, 6], F32) as st, \
            nc.sbuf_tensor(f"{tag}_mv", [P, NT, 2], F32) as mv, \
            nc.sbuf_tensor(f"{tag}_sd", [P, 3, NT], F32) as sd:
        splits = [(here, *part) for (_, _, parts), here in zip(weights, w_here) for part in parts]

        @block.sync
        def _(sp):
            if x_in is not None:
                sp.dma_start(g.x_res[:, :, :], x_in).then_inc(x_here, 16)
            for (dram, stage, _), here in zip(weights, w_here):
                sp.dma_start(stage, dram).then_inc(here, 16)
            for dst, src in small:
                sp.dma_start(dst, src).then_inc(small_here, 16)
            if small:
                sp.wait_ge(small_here, 16 * len(small))

        @block.vector
        def _(dve):
            if x_in is not None:
                dve.wait_ge(x_here, 16)
            for t in range(NT):
                dve.bn_stats(st[:, t, :], g.x_res[:, t, :]).then_inc(stats, 1)
            dve.wait_ge(stats, NT)
            for t in range(NT):
                dve.bn_aggr(mv[:, t, :], st[:, t, :]).then_inc(aggr, 1)
            dve.wait_ge(aggr, NT)
            dve.tensor_scalar(sd[:, 0, :], mv[:, :, 1], LN_EPS, None, ALU.add).then_inc(var, 1)
            dve.wait_ge(std, 1)
            dve.reciprocal(sd[:, 2, :], sd[:, 1, :]).then_inc(rstd, 1)
            dve.wait_ge(rstd, 1)
            for t in range(NT):
                dve.tensor_scalar(g.xn[:, t, :], g.x_res[:, t, :], mv[:, t, 0:1], sd[:, 2, t:t + 1],
                                  ALU.subtract, ALU.mult).then_inc(normed, 1)
            for n in range(NB * KC):
                b, c = divmod(n, KC)
                dve.wait_ge(hi, n + 1)
                dve.tensor_tensor(g.xt[:, 1, c, b * T:(b + 1) * T], pt[:, n, :], g.xt[:, 0, c, b * T:(b + 1) * T],
                                  ALU.subtract).then_inc(lo, 1)
            for k, (_, staged, h, l) in enumerate(splits):
                if k % 2 == 0:
                    dve.wait_ge(w_hi, k + 1)
                    dve.tensor_tensor(l, staged, h, ALU.subtract).then_inc(w_lo, 1)

        @block.gpsimd
        def _(pool):
            for k, (_, staged, h, l) in enumerate(splits):
                if k % 2:
                    pool.wait_ge(w_hi, k + 1)
                    pool.tensor_tensor(l, staged, h, ALU.subtract).then_inc(w_lo, 1)

        @block.tensor
        def _(pe):
            for n in range(NB * KC):
                b, c = divmod(n, KC)
                pe.wait_ge(normed, NI * (b + 1))
                for i in range(NI):
                    mm = pe.transpose(pt[:, n, i * P:(i + 1) * P], g.xn[:, b * NI + i, c * P:(c + 1) * P],
                                      g.ident[:, :])
                mm.then_inc(turned, 1)

        @block.scalar
        def _(act):
            act.wait_ge(var, 1)
            act.activation(sd[:, 1, :], sd[:, 0, :], ACT.Sqrt).then_inc(std, 1)
            for n in range(NB * KC):
                b, c = divmod(n, KC)
                act.wait_ge(turned, n + 1)
                act.activation(g.xt[:, 0, c, b * T:(b + 1) * T], pt[:, n, :], ACT.Copy).then_inc(hi, 1)
            for here, staged, h, l in splits:
                act.wait_ge(here, 16)
                act.activation(h, staged, ACT.Copy).then_inc(w_hi, 1)


def binary_weights(nc, tag, g, w_view, stage, sign, n_qk, n_v, n_o, cols, cols_src, rows, rows_src):
    nch, n_row = n_qk // P, n_v + n_o
    with Phase(nc, tag, "w_here small_here signed absd col_sum row_sum part") as (
            block, w_here, small_here, signed, absd, col_sum, row_sum, part), \
            nc.psum_tensor(f"{tag}_pc", [P, BANK], F32) as pc, \
            nc.psum_tensor(f"{tag}_pr", [P, 2, BANK], F32) as pr, \
            nc.sbuf_tensor(f"{tag}_cs", [P, nch], F32) as cs, \
            nc.sbuf_tensor(f"{tag}_rs", [P, n_row], F32) as rs:

        @block.sync
        def _(sp):
            for c in range(KC):
                sp.dma_start(stage[:, c, :], w_view[:, c, :]).then_inc(w_here, 16)
            sp.dma_start(cs[:, :], cols_src).then_inc(small_here, 16)
            sp.dma_start(rs[:, :], rows_src.partition_broadcast(P)).then_inc(small_here, 16)

        @block.scalar
        def _(act):
            act.wait_ge(w_here, 16 * KC)
            for c in range(KC):
                act.activation(sign[:, 0, c, :], stage[:, c, :], ACT.Sign).then_inc(signed, 1)
            for c in range(KC):
                act.wait_ge(signed, c + 1)
                act.activation(stage[:, c, :], stage[:, c, :], ACT.Abs).then_inc(absd, 1)

        @block.tensor
        def _(pe):
            pe.wait_ge(absd, KC)
            for j in range(nch):
                for c in range(KC):
                    mm = pe.matmul(pc[:, j:j + 1], stage[:, c, j * P:(j + 1) * P], g.ones[:, 0:1],
                                   start=c == 0, stop=c == KC - 1)
            mm.then_inc(col_sum, 1)
            for k, (a, n) in enumerate(((n_qk, n_v), (n_qk + n_v, n_o))):
                for c in range(KC):
                    mm = pe.matmul(pr[:, k, 0:n], g.ones[:, :], stage[:, c, a:a + n], start=c == 0, stop=c == KC - 1)
            mm.then_inc(row_sum, 1)

        @block.vector
        def _(dve):
            dve.wait_ge(small_here, 32)
            dve.wait_ge(col_sum, 1)
            dve.tensor_scalar(cols[:, :], pc[:, 0:nch], 1.0 / D, 1e-8, ALU.mult, ALU.max).then_inc(part, 1)
            dve.wait_ge(row_sum, 1)
            for k, (a, n) in enumerate(((0, n_v), (n_v, n_o))):
                dve.tensor_scalar(rows[:, a:a + n], pr[:, k, 0:n], 1.0 / D, 1e-8, ALU.mult, ALU.max).then_inc(part, 1)
            dve.wait_ge(part, 3)
            dve.tensor_tensor(cols[:, :], cols[:, :], cs[:, :], ALU.mult).then_inc(part, 1)
            dve.tensor_tensor(rows[:, :], rows[:, :], rs[:, :], ALU.mult).then_inc(part, 1)


def project(nc, tag, g, a, w, vz, col, v_row):
    full, left = divmod(a.n_qk, P)
    nch = full + (left > 0)
    op = ALU.mult if a.binary else ALU.add
    w_pairs = ((0, 0), (0, 1)) if a.binary else PRODUCTS
    x_pairs = ((0, 0), (1, 0)) if a.binary else PRODUCTS
    with Phase(nc, tag, "qk_made hi lo stored v_made v_out padded ones_set") as (
            block, qk_made, hi, lo, stored, v_made, v_out, padded, ones_set), \
            nc.psum_tensor(f"{tag}_pq", [P, 3, BANK], F32) as pq, \
            nc.psum_tensor(f"{tag}_pv", [P, 2, BANK], F32) as pv, \
            nc.sbuf_tensor(f"{tag}_qk", [P, NB * nch, 2, T], F16) as qk:

        def chunks(eng, step):
            for b in range(NB):
                with eng.Fori(0, full // 2) as jj:
                    for u in range(2):
                        j = eng.snap(jj * 2 + u)
                        step(b, j, eng.snap(j + b * nch), u, P)
                if left:
                    step(b, full, b * nch + full, 2, left)
                elif full % 2:
                    step(b, full - 1, b * nch + full - 1, 2, P)

        @block.tensor
        def _(pe):
            def step(b, j, n, u, rows):
                pe.wait_ge(lo, n + 1)
                product(pe, pq[0:rows, u, :], lambda part, c: w[:, part, c, ds(j * P, rows)],
                        lambda part, c: g.xt[:, part, c, b * T:(b + 1) * T], range(KC), w_pairs)\
                    .then_inc(qk_made, 1)
            chunks(pe, step)
            with pe.Fori(0, NT // 2) as tt:
                for u in range(2):
                    t = pe.snap(tt * 2 + u)
                    pe.wait_ge(v_out, t + 1)
                    product(pe, pv[:, u, 0:a.n_v], lambda part, c: g.xt[:, part, c, ds(t * P, P)],
                            lambda part, c: w[:, part, c, a.n_qk:a.n_qk + a.n_v], range(KC), x_pairs)\
                        .then_inc(v_made, 1)

        @block.scalar
        def _(act):
            def step(b, j, n, u, rows):
                act.wait_ge(qk_made, n + 1)
                out = qk[0:rows, ds(n, 1), 0, :]
                if a.binary:
                    act.activation(out, pq[0:rows, u:u + 1, :], ACT.Identity, scale=col[0:rows, ds(j, 1)]).then_inc(hi, 1)
                else:
                    act.activation(out, pq[0:rows, u:u + 1, :], ACT.Identity, bias=col[0:rows, ds(j, 1)]).then_inc(hi, 1)
            chunks(act, step)

        @block.gpsimd
        def _(pool):
            pool.memset(vz[:, :, :, :], 0.0).then_inc(padded, 1)
            pool.wait_ge(padded, 1)
            pool.memset(vz[:, :, :, a.hd:a.hd + 1], 1.0).then_inc(ones_set, 1)

        @block.vector
        def _(dve):
            dve.sem_inc(lo, 2)
            dve.sem_inc(v_out, 2)

            def step(b, j, n, u, rows):
                dve.wait_ge(hi, n + 1)
                dve.scalar_tensor_tensor(out=qk[0:rows, ds(n, 1), 1, :], in0=pq[0:rows, u:u + 1, :],
                                         scalar=col[0:rows, ds(j, 1)], in1=qk[0:rows, ds(n, 1), 0, :],
                                         op0=op, op1=ALU.subtract).then_inc(lo, 1)
            chunks(dve, step)
            dve.wait_ge(ones_set, 1)
            with dve.Fori(0, NT // 2) as tt:
                for u in range(2):
                    t = dve.snap(tt * 2 + u)
                    dve.wait_ge(v_made, t + 1)
                    dve.tensor_tensor(vz[:, ds(t, 1), :, 0:a.hd].rearrange("p o h d -> p (o h) d"),
                                      pv[:, u, 0:a.n_v].rearrange("p (h d) -> p h d", d=a.hd),
                                      v_row.rearrange("p (h d) -> p h d", d=a.hd), op).then_inc(v_out, 1)

        @block.sync
        def _(sp):
            def step(b, j, n, u, rows):
                sp.wait_ge(lo, n + 3)
                sp.dma_start(g.qk_dram[b, :, ds(j * P, rows), :].rearrange("two p t -> p two t"),
                             qk[0:rows, ds(n, 1), :, :].rearrange("p o two t -> p (o two) t")).then_inc(stored, 16)
            chunks(sp, step)
            sp.wait_ge(stored, 16 * NB * nch)


def row_maxima(nc, tag, g, a, b, qs, ks):
    rows = 3 * a.hd
    if a.causal:
        units = [(0, 0, 4, P), (1, 0, 4, 2 * P), (2, 0, 2, 3 * P), (2, 2, 2, 3 * P), (3, 0, 2, 4 * P), (3, 2, 2, 4 * P)]
        slots = 3
    else:
        units = [(i, h, 2, T) for i in range(NI) for h in (0, 2)]
        slots = 2
    with Phase(nc, tag, "filled stacked scored maxed turned neg_hi neg_lo placed") as (
            block, filled, stacked, scored, maxed, turned, neg_hi, neg_lo, placed), \
            nc.psum_tensor(f"{tag}_ps", [P, 3, 2 * BANK], F32) as ps, \
            nc.psum_tensor(f"{tag}_pm", [P, BANK], F32) as pm, \
            nc.sbuf_tensor(f"{tag}_mx", [P, NI, a.h], F32) as mx, \
            nc.sbuf_tensor(f"{tag}_mn", [a.h, 2, T], F16) as mn:
        ngroups = a.h // 4

        def region(n, u):
            i, _, heads, keys = units[u]
            s = u % slots
            if keys == 3 * P:
                return ps[:, s, :].rearrange("p (h k) -> p h k", k=BANK)[:, 0:heads, 0:keys]
            return ps[:, s, 0:heads * keys].rearrange("p (h k) -> p h k", k=keys)

        @block.gpsimd
        def _(pool):
            pool.memset(qs[:, :, :].bitcast(F32), 0.0).then_inc(filled, 1)

        @block.vector
        def _(dve):
            dve.memset(ks[:, :, :], 1.0).then_inc(filled, 1)
            dve.sem_inc(maxed, slots)
            with dve.Fori(0, ngroups) as gr:
                for u, (i, h0, heads, keys) in enumerate(units):
                    n = gr * len(units) + u
                    dve.wait_ge(scored, n + 1)
                    dve.tensor_reduce(mx[:, i, ds(gr * 4 + h0, heads)], region(n, u), AX.X, ALU.max).then_inc(maxed, 1)
            dve.wait_ge(neg_hi, 1)
            dve.scalar_tensor_tensor(out=mn[:, 1, :], in0=pm[0:a.h, :], scalar=-1.0, in1=mn[:, 0, :],
                                     op0=ALU.mult, op1=ALU.subtract).then_inc(neg_lo, 1)

        @block.sync
        def _(sp):
            sp.wait_ge(filled, 2)
            for r, (qp, kp) in enumerate(PRODUCTS):
                sp.dma_start(qs[r * a.hd:(r + 1) * a.hd, :, :],
                             g.qk_dram[b, qp, 0:a.n_q, :].rearrange("(h d) t -> d h t", d=a.hd)).then_inc(stacked, 16)
                sp.dma_start(ks[r * a.hd:(r + 1) * a.hd, :, :],
                             g.qk_dram[b, kp, a.n_q:a.n_qk, :].rearrange("(h d) t -> d h t", d=a.hd)).then_inc(stacked, 16)
            sp.wait_ge(neg_lo, 1)
            for part in range(2):
                sp.dma_start(qs[rows + part:rows + part + 1, :, :], mn[:, part:part + 1, :]).then_inc(placed, 16)
            sp.wait_ge(placed, 32)

        @block.tensor
        def _(pe):
            pe.wait_ge(stacked, 16 * 2 * len(PRODUCTS))
            with pe.Fori(0, ngroups) as gr:
                for u, (i, h0, heads, keys) in enumerate(units):
                    pe.wait_ge(maxed, gr * len(units) + u + 1)
                    out = region(None, u)
                    for k in range(heads):
                        h = pe.snap(gr * 4 + h0 + k)
                        kv = (0 if a.kv == 1 else gr) if a.kv < a.h else h
                        mm = pe.matmul(out[:, k, :], qs[:, ds(h, 1), i * P:(i + 1) * P].rearrange("p o q -> p (o q)"),
                                       ks[:, ds(kv, 1), 0:keys].rearrange("p o k -> p (o k)"),
                                       start=True, stop=not a.causal)
                        if a.causal:
                            mm = pe.matmul(out[:, k, keys - P:keys], g.ident_b[:, :], g.mask_qk[:, :],
                                           start=False, stop=True)
                    mm.then_inc(scored, 1)
            pe.wait_ge(maxed, slots + ngroups * len(units))
            for i in range(NI):
                mm = pe.transpose(pm[0:a.h, i * P:(i + 1) * P], mx[:, i, :], g.ident[:, :])
            mm.then_inc(turned, 1)

        @block.scalar
        def _(act):
            act.wait_ge(turned, 1)
            act.activation(mn[:, 0, :], pm[0:a.h, :], ACT.Copy, scale=-1.0).then_inc(neg_hi, 1)


def attend(nc, tag, g, a, b, qs, ks, vz, on):
    if a.causal:
        units = [[(0, 0), (1, 512), (3, 512 + 384), (2, 1024)]]
    else:
        units = [[(0, 0), (1, 512)], [(2, 0), (3, 512)]]
    n_u = len(units)
    width = 1280 if a.causal else 1024
    body = 8
    n_body = a.h // body
    hb = P // a.sw
    og_n = body // hb
    vh = 4 // (a.h // a.kv) if a.h // a.kv < 4 else 1
    staged_v = n_body > 1 and a.kv > 1
    with Phase(nc, tag, "scored exped summed taken turned inverted normed staged") as (
            block, scored, exped, summed, taken, turned, inverted, normed, staged), \
            nc.psum_tensor(f"{tag}_ps", [P, 2, 3 * BANK], F32) as ps, \
            nc.psum_tensor(f"{tag}_po", [P, BANK], F32) as po, \
            nc.psum_tensor(f"{tag}_pt", [P, BANK], F32) as pt, \
            nc.sbuf_tensor(f"{tag}_pr", [P, 4 * n_u, width], F32) as pr, \
            nc.sbuf_tensor(f"{tag}_vs", [P, 2, NI, vh, a.sw], F32) as vs, \
            nc.sbuf_tensor(f"{tag}_ou", [P, 2, BANK], F32) as ou, \
            nc.sbuf_tensor(f"{tag}_ri", [P, 2, NI, hb], F32) as ri:

        def place(j):
            for w, unit in enumerate(units):
                for jj, at in unit:
                    if jj == j:
                        return w, at

        def passes(eng, step):
            for k in range(body):
                step(0, k)
            if n_body > 1:
                with eng.Fori(1, n_body) as n:
                    for k in range(body):
                        step(n, k)

        def back(n, k, lag, fn):
            if k >= lag:
                fn(n, k - lag)
            elif not (isinstance(n, int) and n == 0):
                fn(n - 1, k - lag + body)

        def group_of(fn):
            return lambda n, k: fn(n, k // hb) if k % hb == hb - 1 else None

        def drain(*fns):
            for past in range(max(lag for lag, _ in fns)):
                for lag, fn in fns:
                    if past < lag:
                        fn(n_body - 1, body - lag + past)

        def kv_of(eng, n, k):
            rep = a.h // a.kv
            if a.kv == 1:
                return 0
            return n * (body // rep) + k // rep if isinstance(n, int) else eng.snap(n * (body // rep) + k // rep)

        @block.gpsimd
        def _(pool):
            def step(n, k):
                if k % 4 == 0:
                    group = n * 2 + k // 4
                    wait_pos(pool, summed, (group - 1) * 4)
                    src = vz[:, b * NI:(b + 1) * NI, ds(kv_of(pool, n, k), vh), :]
                    pool.tensor_copy(vs[:, k // 4].rearrange("p j h d -> p j (h d)"),
                                     src.rearrange("p j h d -> p j (h d)")).then_inc(staged, 1)
            if staged_v:
                passes(pool, step)

        @block.tensor
        def _(pe):
            def scores(n, k):
                kv = kv_of(pe, n, k)
                h = n * body + k if isinstance(n, int) else pe.snap(n * body + k)
                for w, unit in enumerate(units):
                    slot = (k * n_u + w) % 2
                    wait_pos(pe, exped, (n * body + k) * n_u + w - 1)
                    for j, at in unit:
                        q0 = j * P if a.causal else 0
                        mm = pe.matmul(ps[:, slot, at:at + T - q0],
                                       ks[:, ds(kv, 1), j * P:(j + 1) * P].rearrange("p o k -> p (o k)"),
                                       qs[:, ds(h, 1), q0:T].rearrange("p o q -> p (o q)"),
                                       start=True, stop=not a.causal)
                        if a.causal:
                            mm = pe.matmul(ps[:, slot, at:at + P], g.ident_b[:, :], g.mask_kq[:, :],
                                           start=False, stop=True)
                    mm.then_inc(scored, 1)

            def values(n, k):
                h = n * body + k
                pe.wait_ge(exped, (h + 1) * n_u)
                if k % hb == 0:
                    wait_pos(pe, taken, n * og_n + k // hb)
                if staged_v and k % 4 == 0:
                    pe.wait_ge(staged, n * 2 + k // 4 + 1)
                s = k % hb
                out = po[s * a.sw:(s + 1) * a.sw, :]
                for j in range(NI):
                    w, at = place(j)
                    q0 = j * P if a.causal else 0
                    if staged_v:
                        v = vs[:, k // 4, j, k % 4 if vh == 4 else 0, :]
                    else:
                        v = vz[:, b * NI + j, kv_of(pe, n, k) if n_body == 1 else 0, :]
                    mm = pe.matmul(out[:, q0:T], v, pr[:, (k % 4) * n_u + w, at:at + T - q0],
                                   start=j == 0, stop=j == NI - 1)
                mm.then_inc(summed, 1)

            def turn(n, group):
                og = n * og_n + group
                pe.wait_ge(taken, og + 1)
                wait_pos(pe, normed, og)
                for i in range(NI):
                    mm = pe.transpose(pt[:, i * P:(i + 1) * P], ou[:, group % 2, i * P:(i + 1) * P], g.ident[:, :])
                mm.then_inc(turned, 1)

            def step(n, k):
                scores(n, k)
                back(n, k, 2, values)
                back(n, k, 3, group_of(turn))

            passes(pe, step)
            drain((2, values), (3, group_of(turn)))

        @block.scalar
        def _(act):
            def exp_unit(n, k, w):
                u = (n * body + k) * n_u + w
                slot = (k * n_u + w) % 2
                act.wait_ge(scored, u + 1)
                if w == 0:
                    wait_pos(act, summed, n * body + k - 3)
                act.activation(pr[:, (k % 4) * n_u + w, :], ps[:, slot, 0:width], ACT.Exp, scale=a.scale).then_inc(exped, 1)

            def step(n, k):
                for w in range(n_u):
                    exp_unit(n, k, w)
            passes(act, step)

        @block.vector
        def _(dve):
            def take(n, group):
                og = n * og_n + group
                dve.wait_ge(summed, (og + 1) * hb)
                wait_pos(dve, turned, og - 1)
                dve.tensor_copy(ou[:, group % 2, :], po[:, :]).then_inc(taken, 1)

            def normalise(n, group):
                og = n * og_n + group
                dve.wait_ge(turned, og + 1)
                out = pt[:, :].rearrange("p (i h d) -> p i h d", i=NI, d=a.sw)
                r = ri[:, group % 2, :, :]
                dve.reciprocal(r, out[:, :, :, a.hd]).then_inc(inverted, 1)
                dve.wait_ge(inverted, og + 1)
                dst = on[:, :, ds((n * og_n + group) * hb * a.hd, hb * a.hd)].rearrange("p i (h d) -> p i h d", d=a.hd)
                dve.tensor_tensor(dst, out[:, :, :, 0:a.hd], r.unsqueeze(3).to_broadcast([P, NI, hb, a.hd]),
                                  ALU.mult).then_inc(normed, 1)


            def step(n, k):
                back(n, k, 2, group_of(take))
                back(n, k, 3, group_of(normalise))
            passes(dve, step)
            drain((2, group_of(take)), (3, group_of(normalise)))


def project_out(nc, tag, g, a, b, on, wo, row):
    kc = a.n_q // P
    pairs = ((0, 0), (1, 0)) if a.binary else PRODUCTS
    with Phase(nc, tag, "turned hi lo made out") as (block, turned, hi, lo, made, out), \
            nc.psum_tensor(f"{tag}_pt", [P, kc, BANK], F32) as pt, \
            nc.psum_tensor(f"{tag}_po", [P, NI, BANK], F32) as po, \
            nc.sbuf_tensor(f"{tag}_ot", [P, 2, kc, T], F16) as ot:

        @block.tensor
        def _(pe):
            for c in range(kc):
                for i in range(NI):
                    mm = pe.transpose(pt[:, c, i * P:(i + 1) * P], on[:, i, c * P:(c + 1) * P], g.ident[:, :])
                mm.then_inc(turned, 1)
            pe.wait_ge(lo, kc)
            for i in range(NI):
                product(pe, po[:, i, :], lambda part, c: ot[:, part, c, i * P:(i + 1) * P],
                        lambda part, c: wo[:, part, c, :], range(kc), pairs).then_inc(made, 1)

        @block.scalar
        def _(act):
            for c in range(kc):
                act.wait_ge(turned, c + 1)
                act.activation(ot[:, 0, c, :], pt[:, c, :], ACT.Copy).then_inc(hi, 1)

        @block.vector
        def _(dve):
            for c in range(kc):
                dve.wait_ge(hi, c + 1)
                dve.tensor_tensor(ot[:, 1, c, :], pt[:, c, :], ot[:, 0, c, :], ALU.subtract).then_inc(lo, 1)
            for i in range(NI):
                dve.wait_ge(made, i + 1)
                dve.tensor_tensor(g.att[:, b * NI + i, :], po[:, i, :], row,
                                  ALU.mult if a.binary else ALU.add).then_inc(out, 1)


def attention(nc, tag, g, a, vz, wo, o_row):
    with nc.sbuf_tensor(f"{tag}_qs", [P, a.h, T], F16) as qs, \
            nc.sbuf_tensor(f"{tag}_ks", [P, a.kv, T], F16) as ks, \
            nc.sbuf_tensor(f"{tag}_on", [P, NI, a.n_q], F32) as on:
        for b in range(NB):
            row_maxima(nc, f"{tag}m{b}", g, a, b, qs, ks)
            attend(nc, f"{tag}a{b}", g, a, b, qs, ks, vz, on)
            project_out(nc, f"{tag}o{b}", g, a, b, on, wo, o_row)


def clear_semaphores(nc):
    nc.clear_and_free_semaphores(Phase.held)
    nc.all_engine_barrier()
    Phase.held = []


class Heads:

    def __init__(self, h, kv, hd, causal, scale, binary=False):
        self.h, self.kv, self.hd, self.causal, self.scale, self.binary = h, kv, hd, causal, scale, binary
        self.n_q, self.n_v = h * hd, kv * hd
        self.sw = 32 if hd < 32 else 64
        self.n_qk = self.n_q + kv * hd
        self.n_all = self.n_qk + self.n_v


def project_rotary(nc, tag, g, a, w, vz, brow, cos, sin):
    half = a.hd // 2
    with Phase(nc, tag, "made biased sined cosed rotated turned hi lo v_out padded ones_set stored") as (
            block, made, biased, sined, cosed, rotated, turned, hi, lo, v_out, padded, ones_set, stored), \
            nc.psum_tensor(f"{tag}_pq", [P, 3, BANK], F32) as pq, \
            nc.psum_tensor(f"{tag}_pt", [P, 2, BANK], F32) as pt, \
            nc.sbuf_tensor(f"{tag}_qb", [P, 2, a.n_q], F32) as qb, \
            nc.sbuf_tensor(f"{tag}_qc", [P, 2, a.n_q], F32) as qc, \
            nc.sbuf_tensor(f"{tag}_qsn", [P, 2, a.n_q], F32) as qsn, \
            nc.sbuf_tensor(f"{tag}_rot", [P, 2, a.n_q], F32) as rot, \
            nc.sbuf_tensor(f"{tag}_qk", [P, 2, KC, 2, NT * P], F16) as qk:

        def heads(ap):
            return ap.rearrange("p (h d) -> p h d", d=a.hd)

        def table(tab, t):
            return tab[:, ds(t, 1), :].to_broadcast([P, a.h, a.hd])

        def tiles(eng, step):
            with eng.Fori(0, NT) as t:
                step(eng.snap(t))

        @block.tensor
        def _(pe):
            pe.sem_inc(turned, 2)

            def step(t):
                for m in range(3):
                    if m < 2:
                        pe.wait_ge(biased, t * 2 + m + 1)
                    else:
                        pe.wait_ge(v_out, t + 1)
                    product(pe, pq[:, m, :], lambda part, c: g.xt[:, part, c, ds(t * P, P)],
                            lambda part, c: w[:, part, c, m * a.n_q:(m + 1) * a.n_q], range(KC)).then_inc(made, 1)
                for m in range(2):
                    pe.wait_ge(rotated, t * 4 + 2 * m + 6)
                    pe.wait_ge(lo, t * 2 + m + 1)
                    for c in range(KC):
                        mm = pe.transpose(pt[:, m, c * P:(c + 1) * P], rot[:, m, c * P:(c + 1) * P], g.ident[:, :])
                    mm.then_inc(turned, 1)
            tiles(pe, step)

        @block.vector
        def _(dve):
            dve.sem_inc(biased, 2)
            dve.sem_inc(rotated, 4)
            dve.sem_inc(lo, 2)
            dve.sem_inc(v_out, 1)
            dve.wait_ge(ones_set, 1)

            def step(t):
                for m in range(2):
                    dve.wait_ge(made, t * 3 + m + 1)
                    dve.tensor_tensor(qb[:, m, :], pq[:, m, :], brow[:, m * a.n_q:(m + 1) * a.n_q],
                                      ALU.add).then_inc(biased, 1)
                    dve.wait_ge(biased, t * 2 + m + 3)
                    dve.tensor_tensor(heads(qc[:, m, :]), heads(qb[:, m, :]), table(cos, t), ALU.mult).then_inc(cosed, 1)
                    dve.wait_ge(cosed, t * 2 + m + 1)
                    dve.wait_ge(sined, t * 2 + m + 1)
                    dve.wait_ge(turned, t * 2 + m + 1)
                    out, c_, s_ = heads(rot[:, m, :]), heads(qc[:, m, :]), heads(qsn[:, m, :])
                    dve.tensor_tensor(out[:, :, 0:half], c_[:, :, 0:half], s_[:, :, half:], ALU.subtract).then_inc(rotated, 1)
                    dve.tensor_tensor(out[:, :, half:], c_[:, :, half:], s_[:, :, 0:half], ALU.add).then_inc(rotated, 1)
                dve.wait_ge(made, t * 3 + 3)
                dve.tensor_tensor(vz[:, ds(t, 1), :, 0:a.hd].rearrange("p o h d -> p (o h) d"), heads(pq[:, 2, :]),
                                  heads(brow[:, 2 * a.n_q:3 * a.n_q]), ALU.add).then_inc(v_out, 1)
                for m in range(2):
                    dve.wait_ge(hi, t * 2 + m + 1)
                    dve.tensor_tensor(qk[:, m, :, 1, ds(t * P, P)], pt[:, m, :].rearrange("p (c t) -> p c t", t=P),
                                      qk[:, m, :, 0, ds(t * P, P)], ALU.subtract).then_inc(lo, 1)
            tiles(dve, step)

        @block.gpsimd
        def _(pool):
            pool.memset(vz[:, :, :, :], 0.0).then_inc(padded, 1)
            pool.wait_ge(padded, 1)
            pool.memset(vz[:, :, :, a.hd:a.hd + 1], 1.0).then_inc(ones_set, 1)

            def step(t):
                for m in range(2):
                    pool.wait_ge(biased, t * 2 + m + 3)
                    pool.wait_ge(rotated, t * 4 + 2 * m + 2)
                    pool.tensor_tensor(heads(qsn[:, m, :]), heads(qb[:, m, :]), table(sin, t), ALU.mult).then_inc(sined, 1)
            for t in range(NT):
                step(t)

        @block.scalar
        def _(act):
            def step(t):
                for m in range(2):
                    act.wait_ge(turned, t * 2 + m + 3)
                    act.activation(qk[:, m, :, 0, ds(t * P, P)], pt[:, m, :].rearrange("p (c t) -> p c t", t=P),
                                   ACT.Copy).then_inc(hi, 1)
            tiles(act, step)

        @block.sync
        def _(sp):
            for b in range(NB):
                sp.wait_ge(lo, 2 * NI * (b + 1) + 2)
                for m in range(2):
                    for c in range(KC):
                        sp.dma_start(g.qk_dram[b, :, m * a.n_q + c * P:m * a.n_q + (c + 1) * P, :]
                                     .rearrange("two p t -> p two t"), qk[:, m, c, :, b * T:(b + 1) * T]).then_inc(stored, 16)
            sp.wait_ge(stored, 16 * NB * 2 * KC)


def gated_residual(nc, tag, g, multiply, row=None):
    with Phase(nc, tag, "made free biased silued gated added") as (block, made, free, biased, silued, gated, added), \
            nc.psum_tensor(f"{tag}_pf", [P, 2, BANK], F32) as pf, \
            nc.sbuf_tensor(f"{tag}_gl", [P, 2, D], F32) as gl:

        def tiles(eng, step):
            with eng.Fori(0, NT // 2) as tt:
                for u in range(2):
                    step(eng.snap(tt * 2 + u), u)

        @block.tensor
        def _(pe):
            def step(t, u):
                pe.wait_ge(free, t + 1)
                multiply(pe, pf[:, u, :], t).then_inc(made, 1)
            tiles(pe, step)

        @block.scalar
        def _(act):
            def step(t, u):
                if row is None:
                    act.wait_ge(added, t + 1)
                    act.wait_ge(made, t + 1)
                    act.activation(gl[:, u, :], pf[:, u, :], ACT.Silu).then_inc(silued, 1)
                else:
                    act.wait_ge(biased, t + 1)
                    act.activation(gl[:, u, :], gl[:, u, :], ACT.Silu).then_inc(silued, 1)
            tiles(act, step)

        @block.vector
        def _(dve):
            dve.sem_inc(added, 2)
            dve.sem_inc(free, 2)

            def step(t, u):
                if row is not None:
                    dve.wait_ge(added, t + 1)
                    dve.wait_ge(made, t + 1)
                    dve.tensor_tensor(gl[:, u, :], pf[:, u, :], row, ALU.add).then_inc(biased, 1)
                dve.wait_ge(silued, t + 1)
                dve.sem_inc(free, 1)
                dve.tensor_tensor(gl[:, u, :], gl[:, u, :], g.att[:, ds(t, 1), :].rearrange("p o d -> p (o d)"),
                                  ALU.mult).then_inc(gated, 1)
                dve.wait_ge(gated, t + 1)
                x = g.x_res[:, ds(t, 1), :].rearrange("p o d -> p (o d)")
                dve.tensor_tensor(x, x, gl[:, u, :], ALU.add).then_inc(added, 1)
            tiles(dve, step)



def swiglu_low_rank(nc, g, ins):
    rank, width = ins["L0_sv_d"].shape
    n_i = width // P
    gu = KC * 2 * P
    down = D
    with nc.sbuf_tensor("f0_dt", [P, 2, n_i, NT * P], F16) as dt, \
            nc.sbuf_tensor("f0_wd", [P, 2, n_i, D], F16) as wd:
        with nc.sbuf_tensor("f0_ws", [P, 2, gu + down], F32) as ws, \
                nc.sbuf_tensor("f0_wgu", [P, 2, 2, gu], F16) as wgu, \
                nc.sbuf_tensor("f0_sd", [P, NB, T], F32) as sd, \
                nc.sbuf_tensor("f0_svg", [rank, 2, D], F32) as svg, \
                nc.sbuf_tensor("f0_sug", [rank, n_i, 2, P], F32) as sug, \
                nc.sbuf_tensor("f0_svd", [rank, 2, P], F32) as svd, \
                nc.sbuf_tensor("f0_sud", [rank, D], F32) as sud, \
                nc.psum_tensor("f0_pr", [P, 3 * BANK], F32) as pr, \
                nc.psum_tensor("f0_pp", [P, NB, 2, BANK], F32) as pp, \
                Phase(nc, "f0", "small_here w_here0 w_here1 low weffed hi lo paired silued gated d_hi d_lo") as (
                block, small_here, w_here0, w_here1, low, weffed, hi, lo, paired, silued, gated, d_hi, d_lo):
            w_here = (w_here0, w_here1)

            def pipeline(eng, prepare, use):
                prepare(0, 0, 0)
                for i in range(2):
                    prepare(i + 1, (i + 1) % 2, (i + 1) // 2)
                    use(i, i)
                with eng.Fori(1, n_i // 2 - 1) as ii:
                    i = eng.snap(ii * 2)
                    after = eng.snap(ii * 2 + 1)
                    prepare(after, 1, ii)
                    use(i, 0)
                    prepare(eng.snap(ii * 2 + 2), 0, ii + 1)
                    use(after, 1)
                prepare(n_i - 1, 1, n_i // 2 - 1)
                use(n_i - 2, 0)
                use(n_i - 1, 1)

            @block.sync
            def _(sp):
                for dst, name in ((svg, "L0_sv_gu"), (sug, "L0_su_gu"), (sud, "L0_su_d")):
                    sp.dma_start(dst[:], ins[name]).then_inc(small_here, 16)

                def load(i, u, k):
                    wait_pos(sp, lo, i - 1)
                    sp.dma_start(ws[:, u, 0:gu].rearrange("p (c n) -> p c n", c=KC),
                                 ins["L0_gu"][:, ds(i * KC * 2 * P, KC * 2 * P)].rearrange("p (c n) -> p c n", c=KC))\
                        .then_inc(w_here[u], 16)
                    sp.dma_start(ws[:, u, gu:gu + down], ins["L0_down"][:, ds(i * D, D)]).then_inc(w_here[u], 16)
                    sp.dma_start(svd[:, u, :], ins["L0_sv_d"][:, ds(i * P, P)]).then_inc(w_here[u], 16)
                pipeline(sp, load, lambda i, u: None)

            @block.tensor
            def _(pe):
                pe.wait_ge(small_here, 48)

                def low_rank(i, u, k):
                    wait_pos(pe, weffed, i)
                    pe.wait_ge(w_here[u], (k + 1) * 48)
                    for c in range(KC):
                        for m in range(2):
                            at = (c * 2 + m) * P
                            pe.matmul(pr[:, at:at + P], svg[:, m, c * P:(c + 1) * P],
                                      sug[:, ds(i, 1), m, :].rearrange("r o n -> r (o n)"), start=True, stop=True)
                    pe.matmul(pr[:, gu:gu + down], svd[:, u, :], sud[:, :], start=True, stop=True).then_inc(low, 1)

                def gate_and_up(i, u):
                    pe.wait_ge(lo, i + 1)
                    for b in range(NB):
                        wait_pos(pe, gated, i * 2 - 1 + b)
                        for m in range(2):
                            mm = product(pe, pp[:, b, m, :],
                                         lambda part, c: wgu[:, u, part, (c * 2 + m) * P:(c * 2 + m + 1) * P],
                                         lambda part, c: g.xt[:, part, c, b * T:(b + 1) * T], range(KC))
                        mm.then_inc(paired, 1)
                pipeline(pe, low_rank, gate_and_up)

            @block.vector
            def _(dve):
                def effective(i, u, k):
                    dve.wait_ge(low, i + 1)
                    dve.wait_ge(w_here[u], (k + 1) * 48)
                    dve.tensor_tensor(ws[:, u, :], ws[:, u, :], pr[:, :], ALU.mult).then_inc(weffed, 1)

                def gate(i, u):
                    for b in range(NB):
                        dve.wait_ge(silued, i * 2 + b + 1)
                        dve.tensor_tensor(sd[:, b, :], sd[:, b, :], pp[:, b, 1, :], ALU.mult).then_inc(gated, 1)
                pipeline(dve, effective, gate)

            @block.scalar
            def _(act):
                def high(i, u, k):
                    act.wait_ge(weffed, i + 1)
                    wait_pos(act, paired, (i - 1) * 2)
                    act.activation(wgu[:, u, 0, :], ws[:, u, 0:gu], ACT.Copy).then_inc(hi, 1)
                    act.activation(wd[:, 0, ds(i, 1), :], ws[:, u:u + 1, gu:gu + down], ACT.Copy).then_inc(hi, 1)

                def silu(i, u):
                    for b in range(NB):
                        wait_pos(act, d_lo, i * 2 - 1 + b)
                        act.wait_ge(paired, i * 2 + b + 1)
                        act.activation(sd[:, b, :], pp[:, b, 0, :], ACT.Silu).then_inc(silued, 1)
                        act.wait_ge(gated, i * 2 + b + 1)
                        act.activation(dt[:, 0, ds(i, 1), b * T:(b + 1) * T], sd[:, b:b + 1, :], ACT.Copy).then_inc(d_hi, 1)
                pipeline(act, high, silu)

            @block.gpsimd
            def _(pool):
                def low_part(i, u, k):
                    pool.wait_ge(hi, (i + 1) * 2)
                    pool.tensor_tensor(wd[:, 1, ds(i, 1), :], ws[:, u:u + 1, gu:gu + down], wd[:, 0, ds(i, 1), :],
                                       ALU.subtract)
                    pool.tensor_tensor(wgu[:, u, 1, :], ws[:, u, 0:gu], wgu[:, u, 0, :], ALU.subtract).then_inc(lo, 1)

                def gated_low(i, u):
                    for b in range(NB):
                        pool.wait_ge(d_hi, i * 2 + b + 1)
                        pool.tensor_tensor(dt[:, 1, ds(i, 1), b * T:(b + 1) * T], sd[:, b:b + 1, :],
                                           dt[:, 0, ds(i, 1), b * T:(b + 1) * T], ALU.subtract).then_inc(d_lo, 1)
                pipeline(pool, low_part, gated_low)

        gated_residual(nc, "g0", g, lambda pe, out, t: product(
            pe, out, lambda part, j: dt[:, part, j, ds(t * P, P)], lambda part, j: wd[:, part, j, :], range(n_i)))


def hyper_connections(nc, g, ins, w24, wb, base, gate):
    n, iters, inv_tau, eps = 4, 50, 10.0, 1.1920929e-07
    nl = n * n + 2 * n
    with nc.sbuf_tensor("h_mix", [P, NT, n * n], F32) as mix, \
            nc.sbuf_tensor("h_pp", [P, NT, 2 * n], F32) as pp:
        with nc.psum_tensor("h_pl", [P, NT * nl], F32) as pl, \
                nc.sbuf_tensor("h_sq", [P, 2, D], F32) as sq, \
                nc.sbuf_tensor("h_ss", [P, NT], F32) as ss, \
                nc.sbuf_tensor("h_rr", [P, NT], F32) as rr, \
                nc.sbuf_tensor("h_lg", [P, NT, nl], F32) as lg, \
                nc.sbuf_tensor("h_m4", [P, NT * n], F32) as m4, \
                nc.sbuf_tensor("h_i4", [P, NT * n], F32) as i4, \
                nc.sbuf_tensor("h_m2", [P, NT, 2], F32) as m2, \
                nc.sbuf_tensor("h_i2", [P, NT * 2], F32) as i2, \
                nc.sbuf_tensor("h_gt", [P, 3], F32) as gt, \
                Phase(nc, "hs", "made squared meaned rooted centred exped gate_exped done balanced") as (
                block, made, squared, meaned, rooted, centred, exped, gate_exped, done, balanced):

            @block.tensor
            def _(pe):
                for t in range(NT):
                    mm = product(pe, pl[:, t * nl:(t + 1) * nl], lambda part, c: g.xt[:, part, c, t * P:(t + 1) * P],
                                 lambda part, c: w24[:, part, c, :], range(KC))
                mm.then_inc(made, 1)

            @block.scalar
            def _(act):
                for t in range(NT):
                    wait_pos(act, squared, t - 1)
                    act.activation(sq[:, t % 2, :], g.xn[:, t, :], ACT.Square, accum_out=ss[:, t:t + 1]).then_inc(squared, 1)
                act.activation(gt[:, 0:1], gate[:, :], ACT.Exp, scale=-1.0).then_inc(gate_exped, 1)
                act.wait_ge(meaned, 1)
                act.activation(ss[:, :], ss[:, :], ACT.Sqrt).then_inc(rooted, 1)
                act.wait_ge(centred, 2)
                act.activation(mix[:, :, :], mix[:, :, :], ACT.Exp, scale=inv_tau).then_inc(exped, 1)
                act.activation(pp[:, :, :], pp[:, :, :], ACT.Exp).then_inc(exped, 1)

            @block.vector
            def _(dve):
                count = 0

                def chain(ins_):
                    nonlocal count
                    count += 1
                    ins_.then_inc(done, 1)
                    dve.wait_ge(done, count)

                dve.wait_ge(squared, NT)
                dve.tensor_scalar(ss[:, :], ss[:, :], 1.0 / D, eps, ALU.mult, ALU.add).then_inc(meaned, 1)
                dve.wait_ge(rooted, 1)
                chain(dve.reciprocal(rr[:, :], ss[:, :]))
                dve.wait_ge(made, 1)
                chain(dve.tensor_tensor(lg[:, :, :], pl.rearrange("p (t n) -> p t n", n=nl),
                                        rr[:, :].unsqueeze(2).to_broadcast([P, NT, nl]), ALU.mult))
                chain(dve.tensor_tensor(lg[:, :, :], lg[:, :, :], base[:, :].unsqueeze(1).to_broadcast([P, NT, nl]), ALU.add))
                res = lg[:, :, 0:n * n].rearrange("p t (i j) -> p t i j", j=n)
                two = lg[:, :, n * n:].rearrange("p t (i j) -> p t i j", j=n)
                chain(dve.tensor_reduce(m4[:, :], res, AX.X, ALU.max))
                chain(dve.tensor_reduce(m2[:, :, :], two, AX.X, ALU.max))
                rows = mix[:, :, :].rearrange("p t (i j) -> p (t i) j", j=n)
                cols = mix[:, :, :].rearrange("p t (i j) -> p t j i", j=n)
                two_p = pp[:, :, :].rearrange("p t (i j) -> p (t i) j", j=n)
                dve.tensor_tensor(mix[:, :, :].rearrange("p t (i j) -> p t i j", j=n), res,
                                  m4[:, :].rearrange("p (t i) -> p t i", i=n).unsqueeze(3).to_broadcast([P, NT, n, n]),
                                  ALU.subtract).then_inc(centred, 1)
                dve.tensor_tensor(pp[:, :, :].rearrange("p t (i j) -> p t i j", j=n), two,
                                  m2[:, :, :].unsqueeze(3).to_broadcast([P, NT, 2, n]), ALU.subtract).then_inc(centred, 1)
                dve.wait_ge(exped, 2)
                chain(dve.tensor_reduce(m2[:, :, :].rearrange("p t i -> p (t i)"), two_p, AX.X, ALU.add))
                chain(dve.reciprocal(i2[:, :], m2[:, :, :].rearrange("p t i -> p (t i)")))
                chain(dve.tensor_tensor(two_p, two_p, i2[:, :].unsqueeze(2).to_broadcast([P, NT * 2, n]), ALU.mult))
                with dve.Fori(0, iters) as it:
                    dve.tensor_reduce(m4[:, :], rows, AX.X, ALU.add).then_inc(balanced, 1)
                    dve.wait_ge(balanced, it * 6 + 1)
                    dve.reciprocal(i4[:, :], m4[:, :]).then_inc(balanced, 1)
                    dve.wait_ge(balanced, it * 6 + 2)
                    dve.tensor_tensor(rows, rows, i4[:, :].unsqueeze(2).to_broadcast([P, NT * n, n]), ALU.mult)\
                        .then_inc(balanced, 1)
                    dve.wait_ge(balanced, it * 6 + 3)
                    dve.tensor_reduce(m4[:, :].rearrange("p (t j) -> p t j", j=n), cols, AX.X, ALU.add).then_inc(balanced, 1)
                    dve.wait_ge(balanced, it * 6 + 4)
                    dve.reciprocal(i4[:, :], m4[:, :]).then_inc(balanced, 1)
                    dve.wait_ge(balanced, it * 6 + 5)
                    dve.tensor_tensor(cols, cols, i4[:, :].rearrange("p (t j) -> p t j", j=n).unsqueeze(3)
                                      .to_broadcast([P, NT, n, n]), ALU.mult).then_inc(balanced, 1)
                    dve.wait_ge(balanced, it * 6 + 6)
                dve.wait_ge(gate_exped, 1)
                chain(dve.tensor_scalar(gt[:, 0:1], gt[:, 0:1], 1.0, None, ALU.add))
                chain(dve.reciprocal(gt[:, 1:2], gt[:, 0:1]))
                chain(dve.tensor_scalar(gt[:, 2:3], gt[:, 1:2], -1.0, 1.0, ALU.mult, ALU.add))
                chain(dve.tensor_scalar(mix[:, :, :], mix[:, :, :], gt[:, 1:2], None, ALU.mult))
                chain(dve.tensor_scalar(mix[:, :, 0:n * n:n + 1], mix[:, :, 0:n * n:n + 1], gt[:, 2:3], None, ALU.add))

        with nc.sbuf_tensor("h_xp", [P, NT, P], F32) as xp, \
                nc.sbuf_tensor("h_xpt", [P, 2, NT * P], F16) as xpt, \
                nc.sbuf_tensor("h_om", [P, 2, D], F32) as om, \
                nc.psum_tensor("h_pt", [P, 2, BANK], F32) as pt, \
                nc.psum_tensor("h_py", [P, NT, P], F32) as py, \
                Phase(nc, "hm", "pre turned hi lo branched mixed silued gated added") as (
                block, pre, turned, hi, lo, branched, mixed, silued, gated, added):

            @block.vector
            def _(dve):
                for s in range(n):
                    for t in range(NT):
                        x_s = g.xn[:, t, s * P:(s + 1) * P]
                        if s == 0:
                            dve.tensor_scalar(xp[:, t, :], x_s, pp[:, t, 0:1], None, ALU.mult).then_inc(pre, 1)
                        else:
                            dve.wait_ge(pre, (s - 1) * NT + t + 1)
                            dve.scalar_tensor_tensor(out=xp[:, t, :], in0=x_s, scalar=pp[:, t, s:s + 1], in1=xp[:, t, :],
                                                     op0=ALU.mult, op1=ALU.add).then_inc(pre, 1)
                for k in range(2):
                    dve.wait_ge(hi, k + 1)
                    dve.tensor_tensor(xpt[:, 1, k * BANK:(k + 1) * BANK], pt[:, k, :], xpt[:, 0, k * BANK:(k + 1) * BANK],
                                      ALU.subtract).then_inc(lo, 1)
                dve.wait_ge(branched, 1)
                dve.sem_inc(added, 2)
                with dve.Fori(0, NT // 2) as tt:
                    for u in range(2):
                        t = dve.snap(tt * 2 + u)
                        dve.wait_ge(added, t + 1)
                        xt_ = g.xn[:, ds(t, 1), :].rearrange("p o d -> p (o d)")
                        y = py[:, ds(t, 1), :].rearrange("p o d -> p (o d)")
                        h_ = mix[:, ds(t, 1), :].rearrange("p o d -> p (o d)")
                        w_ = pp[:, ds(t, 1), :].rearrange("p o d -> p (o d)")
                        for i in range(n):
                            dve.tensor_scalar(om[:, u, i * P:(i + 1) * P], y, w_[:, n + i:n + i + 1], None, ALU.mult)\
                                .then_inc(mixed, 1)
                        for j in range(n):
                            for i in range(n):
                                o = om[:, u, i * P:(i + 1) * P]
                                dve.wait_ge(mixed, t * (n * n + n) + j * n + i + 1)
                                dve.scalar_tensor_tensor(out=o, in0=xt_[:, j * P:(j + 1) * P],
                                                         scalar=h_[:, i * n + j:i * n + j + 1], in1=o,
                                                         op0=ALU.mult, op1=ALU.add).then_inc(mixed, 1)
                        dve.wait_ge(silued, t + 1)
                        dve.tensor_tensor(om[:, u, :], om[:, u, :], g.att[:, ds(t, 1), :].rearrange("p o d -> p (o d)"),
                                          ALU.mult).then_inc(gated, 1)
                        dve.wait_ge(gated, t + 1)
                        x = g.x_res[:, ds(t, 1), :].rearrange("p o d -> p (o d)")
                        dve.tensor_tensor(x, x, om[:, u, :], ALU.add).then_inc(added, 1)

            @block.tensor
            def _(pe):
                for t in range(NT):
                    pe.wait_ge(pre, (n - 1) * NT + t + 1)
                    pe.transpose(pt[:, t // NI, (t % NI) * P:(t % NI + 1) * P], xp[:, t, :], g.ident[:, :]).then_inc(turned, 1)
                pe.wait_ge(lo, 2)
                for t in range(NT):
                    mm = product(pe, py[:, t, :], lambda part, c: xpt[:, part, t * P:(t + 1) * P],
                                 lambda part, c: wb[:, part, :], range(1))
                mm.then_inc(branched, 1)

            @block.scalar
            def _(act):
                for k in range(2):
                    act.wait_ge(turned, (k + 1) * NI)
                    act.activation(xpt[:, 0, k * BANK:(k + 1) * BANK], pt[:, k, :], ACT.Copy).then_inc(hi, 1)
                with act.Fori(0, NT // 2) as tt:
                    for u in range(2):
                        t = act.snap(tt * 2 + u)
                        act.wait_ge(mixed, (t + 1) * (n * n + n))
                        act.activation(om[:, u, :], om[:, u, :], ACT.Silu).then_inc(silued, 1)


def routed_lora(nc, tag, g, w_ra, top, wt, e, r):
    er = e * r
    with nc.psum_tensor(f"{tag}_ph", [P, 2, BANK], F32) as ph, \
            nc.psum_tensor(f"{tag}_pt", [P, 2, BANK], F32) as pt, \
            nc.sbuf_tensor(f"{tag}_lg", [P, NT, e], F32) as lg, \
            nc.sbuf_tensor(f"{tag}_hh", [P, NT, er], F32) as hh, \
            nc.sbuf_tensor(f"{tag}_m", [P, NT], F32) as m, \
            nc.sbuf_tensor(f"{tag}_s", [P, NT], F32) as s, \
            nc.sbuf_tensor(f"{tag}_e", [P, NT, e], F32) as eq, \
            nc.sbuf_tensor(f"{tag}_o", [P, 2, NT, e], F32) as one, \
            nc.sbuf_tensor(f"{tag}_p", [P, NT, e], F32) as pb, \
            nc.sbuf_tensor(f"{tag}_w", [P, NT, e], F32) as wgt, \
            Phase(nc, tag, "made h_out l_out centred exped done weighted turned hi lo") as (
            block, made, h_out, l_out, centred, exped, done, weighted, turned, hi, lo):

        @block.tensor
        def _(pe):
            with pe.Fori(0, NT // 2) as tt:
                for u in range(2):
                    t = pe.snap(tt * 2 + u)
                    pe.wait_ge(l_out, t + 1)
                    pe.wait_ge(h_out, t + 1)
                    product(pe, ph[:, u, 0:e + er], lambda part, c: g.xt[:, part, c, ds(t * P, P)],
                            lambda part, c: w_ra[:, part, c, :], range(KC)).then_inc(made, 1)
            pe.wait_ge(weighted, 1)
            for t in range(NT):
                pe.transpose(pt[:, t // NI, (t % NI) * P:(t % NI + 1) * P], hh[:, t, :], g.ident[:, :]).then_inc(turned, 1)

        @block.scalar
        def _(act):
            act.sem_inc(h_out, 2)
            with act.Fori(0, NT // 2) as tt:
                for u in range(2):
                    t = act.snap(tt * 2 + u)
                    act.wait_ge(made, t + 1)
                    act.wait_ge(l_out, t + 3)
                    act.activation(hh[:, ds(t, 1), :], ph[:, u:u + 1, e:e + er], ACT.Copy).then_inc(h_out, 1)
            if top == 2:
                act.wait_ge(centred, 1)
                act.activation(pb[:, :, :], pb[:, :, :], ACT.Exp).then_inc(exped, 1)
            for k in range(2):
                act.wait_ge(turned, (k + 1) * NI)
                act.activation(wt[:, 0, k * BANK:(k + 1) * BANK], pt[:, k, :], ACT.Copy).then_inc(hi, 1)

        @block.vector
        def _(dve):
            count = 0

            def chain(ins_):
                nonlocal count
                count += 1
                ins_.then_inc(done, 1)
                dve.wait_ge(done, count)

            def over(v):
                return v.unsqueeze(2).to_broadcast([P, NT, e])

            def largest(values, mark):
                chain(dve.tensor_reduce(m[:, :], values, AX.X, ALU.max))
                chain(dve.tensor_tensor(eq[:, :, :], values, over(m[:, :]), ALU.is_equal))
                chain(dve.tensor_tensor(eq[:, :, :], eq[:, :, :], g.rank[:, :].unsqueeze(1).to_broadcast([P, NT, e]), ALU.mult))
                chain(dve.tensor_reduce(s[:, :], eq[:, :, :], AX.X, ALU.max))
                chain(dve.tensor_tensor(mark, eq[:, :, :], over(s[:, :]), ALU.is_equal))

            dve.sem_inc(l_out, 2)
            with dve.Fori(0, NT // 2) as tt:
                for u in range(2):
                    t = dve.snap(tt * 2 + u)
                    dve.wait_ge(made, t + 1)
                    dve.tensor_copy(lg[:, ds(t, 1), :], ph[:, u:u + 1, 0:e]).then_inc(l_out, 1)
            dve.wait_ge(l_out, NT + 2)
            if top == 1:
                largest(lg[:, :, :], one[:, 0, :, :])
                chain(dve.tensor_tensor(wgt[:, :, :], one[:, 0, :, :], over(m[:, :]), ALU.mult))
            else:
                chain(dve.tensor_reduce(m[:, :], lg[:, :, :], AX.X, ALU.max))
                dve.tensor_tensor(pb[:, :, :], lg[:, :, :], over(m[:, :]), ALU.subtract).then_inc(centred, 1)
                dve.wait_ge(exped, 1)
                chain(dve.tensor_reduce(s[:, :], pb[:, :, :], AX.X, ALU.add))
                chain(dve.reciprocal(m[:, :], s[:, :]))
                chain(dve.tensor_tensor(pb[:, :, :], pb[:, :, :], over(m[:, :]), ALU.mult))
                largest(pb[:, :, :], one[:, 0, :, :])
                chain(dve.scalar_tensor_tensor(out=lg[:, :, :], in0=one[:, 0, :, :], scalar=-2.0, in1=pb[:, :, :],
                                               op0=ALU.mult, op1=ALU.add))
                largest(lg[:, :, :], one[:, 1, :, :])
                chain(dve.tensor_tensor(eq[:, :, :], one[:, 0, :, :], one[:, 1, :, :], ALU.add))
                chain(dve.tensor_tensor(wgt[:, :, :], pb[:, :, :], eq[:, :, :], ALU.mult))
                chain(dve.tensor_reduce(s[:, :], wgt[:, :, :], AX.X, ALU.add))
                chain(dve.reciprocal(m[:, :], s[:, :]))
                chain(dve.tensor_tensor(wgt[:, :, :], wgt[:, :, :], over(m[:, :]), ALU.mult))
                chain(dve.tensor_scalar(wgt[:, :, :], wgt[:, :, :], 2.0, None, ALU.mult))
            dve.wait_ge(h_out, NT + 2)
            h4 = hh[:, :, :].rearrange("p t (e r) -> p (t e) r", r=r)
            dve.tensor_tensor(h4, h4, wgt[:, :, :].rearrange("p t e -> p (t e)").unsqueeze(2)
                              .to_broadcast([P, NT * e, r]), ALU.mult).then_inc(weighted, 1)
            for k in range(2):
                dve.wait_ge(hi, k + 1)
                dve.tensor_tensor(wt[:, 1, k * BANK:(k + 1) * BANK], pt[:, k, :], wt[:, 0, k * BANK:(k + 1) * BANK],
                                  ALU.subtract).then_inc(lo, 1)


class Shared:
    pass


def split_weight(stage, parts, chunks):
    return [(stage[:, c, :], parts[:, 0, c, :], parts[:, 1, c, :]) for c in range(chunks)]


def build(nc, ins, out, layers=4):
    g = Shared()
    Phase.held = []
    with ExitStack() as top:
        def sb(name, shape, dtype, stack=top):
            return stack.enter_context(nc.sbuf_tensor(name, shape, dtype))

        g.ident = sb("ident", [P, P], F32)
        g.ident_b = sb("ident_b", [P, P], BF16)
        g.mask_qk = sb("mask_qk", [P, P], BF16)
        g.mask_kq = sb("mask_kq", [P, P], BF16)
        g.ones = sb("ones", [P, P], F32)
        g.x_res = sb("x_res", [P, NT, D], F32)
        g.att = sb("att", [P, NT, D], F32)
        g.xt = sb("xt", [P, 2, KC, NT * P], F16)
        g.qk_dram = nc.dram_tensor("qk_scratch", [NB, 2, 2 * D, T], F16).ap()
        load_constants(nc, g, ins)

        def by_chunk(name, chunks=KC):
            return ins[name].rearrange("(c p) n -> p c n", c=chunks)

        x_tiles = ins["x"].rearrange("b (i p) d -> p (b i) d", p=P)
        for layer in range(layers):
            with ExitStack() as st:
                def lsb(name, shape, dtype, st=st):
                    return sb(f"l{layer}_{name}", shape, dtype, st)

                if layer == 0:
                    a = Heads(32, 1, 16, True, 0.25)
                elif layer == 1:
                    a = Heads(8, 8, 32, True, 1.0)
                elif layer == 2:
                    a = Heads(32, 8, 16, False, 0.25, binary=True)
                else:
                    a = Heads(32, 32, 16, True, 0.25)
                nch = -(-a.n_qk // P)
                kc_o = a.n_q // P
                if layer == 1:
                    g.xn = lsb("xn", [P, NT, D], F32)
                    w24 = lsb("w24", [P, 2, KC, 24], F16)
                    wb = lsb("wb", [P, 2, P], F16)
                    base = lsb("base", [P, 24], F32)
                    gate = lsb("gate", [P, 1], F32)
                if layer >= 2:
                    w_ra = lsb("w_ra", [P, 2, KC, 8 + P], F16)
                    w_b = lsb("w_b", [P, 2, 1, D], F16)
                    g.rank = lsb("rank", [P, 8], F32)
                if layer == 3:
                    w_base = lsb("w_base", [P, 2, KC, D], F16)
                    base_row = lsb("base_row", [P, D], F32)
                with ExitStack() as at:
                    def asb(name, shape, dtype, at=at):
                        return sb(f"a{layer}_{name}", shape, dtype, at)
                    pj = at.enter_context(ExitStack())

                    def psb(name, shape, dtype, pj=pj):
                        return sb(f"p{layer}_{name}", shape, dtype, pj)
                    vz = asb("vz", [P, NT, a.kv, a.sw], F32)
                    o_row = asb("o_row", [P, D], F32)
                    wts, small = [], []
                    if a.binary:
                        sign = asb("sign", [P, 1, KC, a.n_all + D], F16)
                        w, wo = sign, sign[:, :, :, a.n_all:]
                        col = asb("col", [P, nch], F32)
                        rows = asb("rows", [P, a.n_v + D], F32)
                        v_row, o_row = rows[:, 0:a.n_v], rows[:, a.n_v:]
                    else:
                        wo = asb("wo", [P, 2, kc_o, D], F16)
                        w = psb("w", [P, 2, KC, a.n_all], F16)
                        small.append((o_row[:, :], ins[f"L{layer}_o_bias"].partition_broadcast(P)))
                        if layer == 3:
                            v_row = psb("qkv_row", [P, a.n_all], F32)
                            small.append((v_row[:, :], ins["L3_qkv_bias"].partition_broadcast(P)))
                            cos = psb("cos", [P, NT, a.hd], F32)
                            sin = psb("sin", [P, NT, a.hd], F32)
                            small += [(cos[:, :, :], ins["cos"]), (sin[:, :, :], ins["sin"])]
                            col = None
                        else:
                            v_row = psb("v_row", [P, a.n_v], F32)
                            col = psb("col", [P, nch], F32)
                            small += [(col[:, :], ins[f"L{layer}_qk_bias"]),
                                      (v_row[:, :], ins[f"L{layer}_v_bias"].partition_broadcast(P))]
                            col, v_row = col[:, :], v_row[:, :]
                        o_row = o_row[:, :]
                    if layer == 1:
                        small += [(base[:, :], ins["L1_base"].partition_broadcast(P)),
                                  (gate[:, :], ins["L1_gate"].partition_broadcast(P))]
                    if layer >= 2:
                        small.append((g.rank[:, :], ins["rank"].partition_broadcast(P)))
                    if layer == 3:
                        small.append((base_row[:, :], ins["L3_base_bias"].partition_broadcast(P)))
                    with ExitStack() as stg:
                        def ssb(name, shape, stg=stg):
                            return sb(f"s{layer}_{name}", shape, F32, stg)
                        if not a.binary:
                            for nm, parts, chunks, n in (("w", w, KC, a.n_all), ("wo", wo, kc_o, D)):
                                s_ = ssb(nm, [P, chunks, n])
                                wts.append((by_chunk(f"L{layer}_{nm}", chunks), s_[:, :, :], split_weight(s_, parts, chunks)))
                        if layer == 1:
                            s_ = ssb("w24", [P, KC, 24])
                            wts.append((by_chunk("L1_w24"), s_[:, :, :],
                                        [(s_[:, :, :], w24[:, 0], w24[:, 1])]))
                            s_ = ssb("wb", [P, P])
                            wts.append((ins["L1_wb"], s_[:, :], [(s_[:, :], wb[:, 0], wb[:, 1])]))
                        if layer >= 2:
                            s_ = ssb("w_ra", [P, KC, 8 + P])
                            wts.append((by_chunk(f"L{layer}_w_ra"), s_[:, :, :], [(s_[:, :, :], w_ra[:, 0], w_ra[:, 1])]))
                            s_ = ssb("w_b", [P, 1, D])
                            wts.append((by_chunk(f"L{layer}_w_b", 1), s_[:, :, :], [(s_[:, :, :], w_b[:, 0], w_b[:, 1])]))
                        if layer == 3:
                            s_ = ssb("w_base", [P, KC, D])
                            wts.append((by_chunk("L3_w_base"), s_[:, :, :], split_weight(s_, w_base, KC)))
                        if layer != 1:
                            g.xn = ssb("xn", [P, NT, D])
                        norm_and_split(nc, f"n{layer}", g, wts, x_in=x_tiles if layer == 0 else None, small=small)
                    if a.binary:
                        with nc.sbuf_tensor("s2_all", [P, KC, a.n_all + D], F32) as stage:
                            binary_weights(nc, "bw", g, by_chunk("L2_w"), stage, sign, a.n_qk, a.n_v, D,
                                           col, ins["L2_qk_scale"], rows, ins["L2_row_scale"])
                        col, v_row, o_row = col[:, :], v_row, o_row
                    if layer == 3:
                        project_rotary(nc, "p3", g, a, w, vz, v_row[:, :], cos, sin)
                    else:
                        project(nc, f"p{layer}", g, a, w, vz, col, v_row)
                    pj.close()
                    attention(nc, f"a{layer}", g, a, vz, wo, o_row)
                if layer == 0:
                    swiglu_low_rank(nc, g, ins)
                elif layer == 1:
                    hyper_connections(nc, g, ins, w24, wb, base, gate)
                else:
                    wt = lsb("wt", [P, 2, NT * P], F16)
                    routed_lora(nc, f"r{layer}", g, w_ra, layer - 1, wt, 8, 16)

                    def multiply(pe, psum, t):
                        if layer == 3:
                            product(pe, psum, lambda part, c: g.xt[:, part, c, ds(t * P, P)],
                                    lambda part, c: w_base[:, part, c, :], range(KC), last=False)
                        return product(pe, psum, lambda part, c: wt[:, part, ds(t * P, P)],
                                       lambda part, c: w_b[:, part, 0, :], range(1), first=layer != 3)
                    gated_residual(nc, f"g{layer}", g, multiply, base_row[:, :] if layer == 3 else None)

            clear_semaphores(nc)

        with Phase(nc, "store", "stored") as (block, stored):
            @block.sync
            def _(sp):
                sp.dma_start(out.rearrange("b (i p) d -> p (b i) d", p=P), g.x_res[:, :, :]).then_inc(stored, 16)
                sp.wait_ge(stored, 16)


def lay_out(v):
    c = np.ascontiguousarray
    f = np.float32

    def by_column(bias):
        n = -(-bias.shape[0] // P)
        full = np.zeros((n * P,), f)
        full[:bias.shape[0]] = bias
        return c(full.reshape(n, P).T)

    cat = np.concatenate
    out = {"x": v["L0_attn_x"], "ident": np.eye(P, dtype=f), "rank": np.arange(8, 0, -1).astype(f)}
    out["L0_w"] = c(cat([v["L0_attn_wq_w"], v["L0_attn_wk_w"], v["L0_attn_wv_w"]]).T)
    out["L0_wo"] = c(v["L0_attn_wo_w"].T)
    out["L0_qk_bias"] = by_column(cat([v["L0_attn_wq_b"], v["L0_attn_wk_b"]]))
    out["L0_v_bias"] = v["L0_attn_wv_b"]
    out["L0_o_bias"] = v["L0_attn_wo_b"]
    gate, up, down = v["L0_ffn_gate_w"], v["L0_ffn_up_w"], v["L0_ffn_down_w"]
    width = gate.shape[0]
    n_i = width // P
    gu = np.stack([gate, up]).reshape(2, n_i, P, KC, P).transpose(4, 1, 3, 0, 2)
    out["L0_gu"] = c(gu.reshape(P, -1))
    out["L0_down"] = c(down.T.reshape(n_i, P, D).transpose(1, 0, 2).reshape(P, -1))
    out["L0_sv_gu"] = c(np.stack([v["L0_ffn_gate_sv"], v["L0_ffn_up_sv"]]).transpose(1, 0, 2))
    out["L0_su_gu"] = c(np.stack([v["L0_ffn_gate_su"], v["L0_ffn_up_su"]]).reshape(2, n_i, P, -1).transpose(3, 1, 0, 2))
    out["L0_sv_d"] = v["L0_ffn_down_sv"]
    out["L0_su_d"] = c(v["L0_ffn_down_su"].T)
    n1 = v["L1_attn_b_qkv"].shape[0] // 3
    out["L1_w"] = c(v["L1_attn_w_qkv"].T)
    out["L1_wo"] = c(v["L1_attn_w_o"].T)
    out["L1_qk_bias"] = by_column(v["L1_attn_b_qkv"][:2 * n1])
    out["L1_v_bias"] = v["L1_attn_b_qkv"][2 * n1:]
    out["L1_o_bias"] = v["L1_attn_b_o"]
    out["L1_w24"] = c(cat([v["L1_ffn_W_res"], v["L1_ffn_W_pre"], v["L1_ffn_W_post"]]).T)
    out["L1_base"] = cat([v["L1_ffn_H_res_base"].ravel(), v["L1_ffn_H_pre_base"], v["L1_ffn_H_post_base"]])
    out["L1_gate"] = v["L1_ffn_gate"]
    out["L1_wb"] = v["L1_ffn_W_branch"]
    out["L2_w"] = c(cat([v["L2_attn_q_weight"], v["L2_attn_k_weight"], v["L2_attn_v_weight"], v["L2_attn_o_weight"]]).T)
    out["L2_qk_scale"] = by_column(cat([v["L2_attn_q_scale"], v["L2_attn_k_scale"]]))
    out["L2_row_scale"] = cat([v["L2_attn_v_scale"], v["L2_attn_o_scale"]])
    out["L2_w_ra"] = c(cat([v["L2_ffn_route_w"], v["L2_ffn_A"].reshape(P, D)]).T)
    out["L2_w_b"] = c(v["L2_ffn_Bw"].transpose(0, 2, 1).reshape(P, D))
    out["L3_w"] = v["L3_attn_qkv_w"]
    out["L3_qkv_bias"] = v["L3_attn_qkv_b"]
    out["L3_wo"] = v["L3_attn_out_w"]
    out["L3_o_bias"] = v["L3_attn_out_b"]
    out["L3_w_ra"] = c(cat([v["L3_ffn_W_router"], v["L3_ffn_lora_A"].reshape(P, D)]).T)
    out["L3_w_b"] = c(v["L3_ffn_lora_B"].transpose(0, 2, 1).reshape(P, D))
    out["L3_w_base"] = c(v["L3_ffn_W_base"].T)
    out["L3_base_bias"] = v["L3_ffn_b_base"]
    half = 8
    inv = (1.0 / 10000.0 ** (np.arange(half, dtype=f) / f(half))).astype(f)
    ang = np.arange(T, dtype=f)[:, None] * inv[None, :]
    for name, fn in (("cos", np.cos), ("sin", np.sin)):
        tab = fn(ang).astype(f).reshape(NI, P, half).transpose(1, 0, 2)
        out[name] = c(np.tile(tab, (1, NB, 2)))
    return {k: c(x) for k, x in out.items()}


def kernel(**inputs):
    import concourse.bacc as bacc
    from concourse.bass_utils import run_bass_kernel_spmd

    nc = bacc.Bacc("TRN2", target_bir_lowering=False, num_devices=1)
    arrays = lay_out({k: np.asarray(x) for k, x in inputs.items()})
    ins = {k: nc.dram_tensor(f"in_{k}", x.shape, mybir.dt.from_np(x.dtype), kind="ExternalInput").ap() for k, x in arrays.items()}
    shape = inputs["L0_attn_x"].shape
    out = nc.dram_tensor("out", shape, F32, kind="ExternalOutput").ap()
    build(nc, ins, out)
    return run_bass_kernel_spmd(nc, [{f"in_{k}": x for k, x in arrays.items()}], core_ids=[0]).results[0]["out"]
```

```python
from contextlib import ExitStack

import numpy as np

import concourse.bass as bass
from concourse import mybir

ALU = mybir.AluOpType
ACT = mybir.ActivationFunctionType
AX = mybir.AxisListType
F32 = mybir.dt.float32
F16 = mybir.dt.float16
BF16 = mybir.dt.bfloat16
ds = bass.ds

P = 128
D = 512
KC = D // P
NB = 2
T = 512
NI = T // P
NT = NB * NI
BANK = 512
PRODUCTS = ((0, 0), (1, 0), (0, 1))
MASKED = -1.0e30
LN_EPS = 1e-5


def wait_pos(eng, sem, value):
    if isinstance(value, int) and value <= 0:
        return
    eng.wait_ge(sem, value)


class Phase:

    held = []

    def __init__(self, nc, tag, names):
        self.nc, self.tag, self.names, self.stack = nc, tag, names.split(), ExitStack()

    def __enter__(self):
        sems = [self.nc.alloc_semaphore(f"{self.tag}_{n}") for n in self.names]
        Phase.held += sems
        return (self.stack.enter_context(self.nc.Block()), *sems)

    def __exit__(self, *exc):
        return self.stack.__exit__(*exc)


def product(pe, out, left, right, chunks, pairs=PRODUCTS, first=True, last=True):
    n = len(pairs) * len(chunks)
    k = 0
    for c in chunks:
        for a, b in pairs:
            mm = pe.matmul(out, left(a, c), right(b, c), start=first and k == 0, stop=last and k == n - 1)
            k += 1
    return mm


def load_constants(nc, g, ins):
    with Phase(nc, "const", "ident_here zeroed masked") as (block, ident_here, zeroed, masked):
        @block.sync
        def _(sp):
            sp.dma_start(g.ident[:, :], ins["ident"]).then_inc(ident_here, 16)
            sp.wait_ge(ident_here, 16)

        @block.vector
        def _(dve):
            dve.memset(g.ones[:, :], 1.0)
            dve.wait_ge(ident_here, 16)
            dve.tensor_copy(g.ident_b[:, :], g.ident[:, :])

        @block.gpsimd
        def _(pool):
            pool.memset(g.mask_qk[:, :], 0.0).then_inc(zeroed, 1)
            pool.memset(g.mask_kq[:, :], 0.0).then_inc(zeroed, 1)
            pool.wait_ge(zeroed, 2)
            pool.affine_select(out=g.mask_qk[:, :], in_=g.mask_qk[:, :], compare_op=ALU.is_ge, fill=MASKED,
                               base=0, pattern=[[-1, P]], channel_multiplier=1).then_inc(masked, 1)
            pool.affine_select(out=g.mask_kq[:, :], in_=g.mask_kq[:, :], compare_op=ALU.is_ge, fill=MASKED,
                               base=0, pattern=[[1, P]], channel_multiplier=-1).then_inc(masked, 1)
            pool.wait_ge(masked, 2)


def norm_and_split(nc, tag, g, weights, x_in=None, small=()):
    with Phase(nc, tag, "x_here stats aggr var std rstd normed turned hi lo w_hi w_lo small_here "
               + " ".join(f"w_here{i}" for i in range(len(weights)))) as (
            block, x_here, stats, aggr, var, std, rstd, normed, turned, hi, lo, w_hi, w_lo, small_here, *w_here), \
            nc.psum_tensor(f"{tag}_pt", [P, 8, BANK], F32) as pt, \
            nc.sbuf_tensor(f"{tag}_st", [P, NT, 6], F32) as st, \
            nc.sbuf_tensor(f"{tag}_mv", [P, NT, 2], F32) as mv, \
            nc.sbuf_tensor(f"{tag}_sd", [P, 3, NT], F32) as sd:
        splits = [(here, *part) for (_, _, parts), here in zip(weights, w_here) for part in parts]

        @block.sync
        def _(sp):
            if x_in is not None:
                sp.dma_start(g.x_res[:, :, :], x_in).then_inc(x_here, 16)
            for (dram, stage, _), here in zip(weights, w_here):
                sp.dma_start(stage, dram).then_inc(here, 16)
            for dst, src in small:
                sp.dma_start(dst, src).then_inc(small_here, 16)
            if small:
                sp.wait_ge(small_here, 16 * len(small))

        @block.vector
        def _(dve):
            if x_in is not None:
                dve.wait_ge(x_here, 16)
            for t in range(NT):
                dve.bn_stats(st[:, t, :], g.x_res[:, t, :]).then_inc(stats, 1)
            dve.wait_ge(stats, NT)
            for t in range(NT):
                dve.bn_aggr(mv[:, t, :], st[:, t, :]).then_inc(aggr, 1)
            dve.wait_ge(aggr, NT)
            dve.tensor_scalar(sd[:, 0, :], mv[:, :, 1], LN_EPS, None, ALU.add).then_inc(var, 1)
            dve.wait_ge(std, 1)
            dve.reciprocal(sd[:, 2, :], sd[:, 1, :]).then_inc(rstd, 1)
            dve.wait_ge(rstd, 1)
            for t in range(NT):
                dve.tensor_scalar(g.xn[:, t, :], g.x_res[:, t, :], mv[:, t, 0:1], sd[:, 2, t:t + 1],
                                  ALU.subtract, ALU.mult).then_inc(normed, 1)
            for n in range(NB * KC):
                b, c = divmod(n, KC)
                dve.wait_ge(hi, n + 1)
                dve.tensor_tensor(g.xt[:, 1, c, b * T:(b + 1) * T], pt[:, n, :], g.xt[:, 0, c, b * T:(b + 1) * T],
                                  ALU.subtract).then_inc(lo, 1)
            for k, (_, staged, h, l) in enumerate(splits):
                if k % 2 == 0:
                    dve.wait_ge(w_hi, k + 1)
                    dve.tensor_tensor(l, staged, h, ALU.subtract).then_inc(w_lo, 1)

        @block.gpsimd
        def _(pool):
            for k, (_, staged, h, l) in enumerate(splits):
                if k % 2:
                    pool.wait_ge(w_hi, k + 1)
                    pool.tensor_tensor(l, staged, h, ALU.subtract).then_inc(w_lo, 1)

        @block.tensor
        def _(pe):
            for n in range(NB * KC):
                b, c = divmod(n, KC)
                pe.wait_ge(normed, NI * (b + 1))
                for i in range(NI):
                    mm = pe.transpose(pt[:, n, i * P:(i + 1) * P], g.xn[:, b * NI + i, c * P:(c + 1) * P],
                                      g.ident[:, :])
                mm.then_inc(turned, 1)

        @block.scalar
        def _(act):
            act.wait_ge(var, 1)
            act.activation(sd[:, 1, :], sd[:, 0, :], ACT.Sqrt).then_inc(std, 1)
            for n in range(NB * KC):
                b, c = divmod(n, KC)
                act.wait_ge(turned, n + 1)
                act.activation(g.xt[:, 0, c, b * T:(b + 1) * T], pt[:, n, :], ACT.Copy).then_inc(hi, 1)
            for here, staged, h, l in splits:
                act.wait_ge(here, 16)
                act.activation(h, staged, ACT.Copy).then_inc(w_hi, 1)


def binary_weights(nc, tag, g, w_view, stage, sign, n_qk, n_v, n_o, cols, cols_src, rows, rows_src):
    nch, n_row = n_qk // P, n_v + n_o
    with Phase(nc, tag, "w_here small_here signed absd col_sum row_sum part") as (
            block, w_here, small_here, signed, absd, col_sum, row_sum, part), \
            nc.psum_tensor(f"{tag}_pc", [P, BANK], F32) as pc, \
            nc.psum_tensor(f"{tag}_pr", [P, 2, BANK], F32) as pr, \
            nc.sbuf_tensor(f"{tag}_cs", [P, nch], F32) as cs, \
            nc.sbuf_tensor(f"{tag}_rs", [P, n_row], F32) as rs:

        @block.sync
        def _(sp):
            for c in range(KC):
                sp.dma_start(stage[:, c, :], w_view[:, c, :]).then_inc(w_here, 16)
            sp.dma_start(cs[:, :], cols_src).then_inc(small_here, 16)
            sp.dma_start(rs[:, :], rows_src.partition_broadcast(P)).then_inc(small_here, 16)

        @block.scalar
        def _(act):
            act.wait_ge(w_here, 16 * KC)
            for c in range(KC):
                act.activation(sign[:, 0, c, :], stage[:, c, :], ACT.Sign).then_inc(signed, 1)
            for c in range(KC):
                act.wait_ge(signed, c + 1)
                act.activation(stage[:, c, :], stage[:, c, :], ACT.Abs).then_inc(absd, 1)

        @block.tensor
        def _(pe):
            pe.wait_ge(absd, KC)
            for j in range(nch):
                for c in range(KC):
                    mm = pe.matmul(pc[:, j:j + 1], stage[:, c, j * P:(j + 1) * P], g.ones[:, 0:1],
                                   start=c == 0, stop=c == KC - 1)
            mm.then_inc(col_sum, 1)
            for k, (a, n) in enumerate(((n_qk, n_v), (n_qk + n_v, n_o))):
                for c in range(KC):
                    mm = pe.matmul(pr[:, k, 0:n], g.ones[:, :], stage[:, c, a:a + n], start=c == 0, stop=c == KC - 1)
            mm.then_inc(row_sum, 1)

        @block.vector
        def _(dve):
            dve.wait_ge(small_here, 32)
            dve.wait_ge(col_sum, 1)
            dve.tensor_scalar(cols[:, :], pc[:, 0:nch], 1.0 / D, 1e-8, ALU.mult, ALU.max).then_inc(part, 1)
            dve.wait_ge(row_sum, 1)
            for k, (a, n) in enumerate(((0, n_v), (n_v, n_o))):
                dve.tensor_scalar(rows[:, a:a + n], pr[:, k, 0:n], 1.0 / D, 1e-8, ALU.mult, ALU.max).then_inc(part, 1)
            dve.wait_ge(part, 3)
            dve.tensor_tensor(cols[:, :], cols[:, :], cs[:, :], ALU.mult).then_inc(part, 1)
            dve.tensor_tensor(rows[:, :], rows[:, :], rs[:, :], ALU.mult).then_inc(part, 1)


def project(nc, tag, g, a, w, vz, col, v_row):
    full, left = divmod(a.n_qk, P)
    nch = full + (left > 0)
    op = ALU.mult if a.binary else ALU.add
    w_pairs = ((0, 0), (0, 1)) if a.binary else PRODUCTS
    x_pairs = ((0, 0), (1, 0)) if a.binary else PRODUCTS
    with Phase(nc, tag, "qk_made hi lo stored v_made v_out padded ones_set") as (
            block, qk_made, hi, lo, stored, v_made, v_out, padded, ones_set), \
            nc.psum_tensor(f"{tag}_pq", [P, 3, BANK], F32) as pq, \
            nc.psum_tensor(f"{tag}_pv", [P, 2, BANK], F32) as pv, \
            nc.sbuf_tensor(f"{tag}_qk", [P, NB * nch, 2, T], F16) as qk:

        def chunks(eng, step):
            for b in range(NB):
                with eng.Fori(0, full // 2) as jj:
                    for u in range(2):
                        j = eng.snap(jj * 2 + u)
                        step(b, j, eng.snap(j + b * nch), u, P)
                if left:
                    step(b, full, b * nch + full, 2, left)
                elif full % 2:
                    step(b, full - 1, b * nch + full - 1, 2, P)

        @block.tensor
        def _(pe):
            def step(b, j, n, u, rows):
                pe.wait_ge(lo, n + 1)
                product(pe, pq[0:rows, u, :], lambda part, c: w[:, part, c, ds(j * P, rows)],
                        lambda part, c: g.xt[:, part, c, b * T:(b + 1) * T], range(KC), w_pairs)\
                    .then_inc(qk_made, 1)
            chunks(pe, step)
            with pe.Fori(0, NT // 2) as tt:
                for u in range(2):
                    t = pe.snap(tt * 2 + u)
                    pe.wait_ge(v_out, t + 1)
                    product(pe, pv[:, u, 0:a.n_v], lambda part, c: g.xt[:, part, c, ds(t * P, P)],
                            lambda part, c: w[:, part, c, a.n_qk:a.n_qk + a.n_v], range(KC), x_pairs)\
                        .then_inc(v_made, 1)

        @block.scalar
        def _(act):
            def step(b, j, n, u, rows):
                act.wait_ge(qk_made, n + 1)
                out = qk[0:rows, ds(n, 1), 0, :]
                if a.binary:
                    act.activation(out, pq[0:rows, u:u + 1, :], ACT.Identity, scale=col[0:rows, ds(j, 1)]).then_inc(hi, 1)
                else:
                    act.activation(out, pq[0:rows, u:u + 1, :], ACT.Identity, bias=col[0:rows, ds(j, 1)]).then_inc(hi, 1)
            chunks(act, step)

        @block.gpsimd
        def _(pool):
            pool.memset(vz[:, :, :, :], 0.0).then_inc(padded, 1)
            pool.wait_ge(padded, 1)
            pool.memset(vz[:, :, :, a.hd:a.hd + 1], 1.0).then_inc(ones_set, 1)

        @block.vector
        def _(dve):
            dve.sem_inc(lo, 2)
            dve.sem_inc(v_out, 2)

            def step(b, j, n, u, rows):
                dve.wait_ge(hi, n + 1)
                dve.scalar_tensor_tensor(out=qk[0:rows, ds(n, 1), 1, :], in0=pq[0:rows, u:u + 1, :],
                                         scalar=col[0:rows, ds(j, 1)], in1=qk[0:rows, ds(n, 1), 0, :],
                                         op0=op, op1=ALU.subtract).then_inc(lo, 1)
            chunks(dve, step)
            dve.wait_ge(ones_set, 1)
            with dve.Fori(0, NT // 2) as tt:
                for u in range(2):
                    t = dve.snap(tt * 2 + u)
                    dve.wait_ge(v_made, t + 1)
                    dve.tensor_tensor(vz[:, ds(t, 1), :, 0:a.hd].rearrange("p o h d -> p (o h) d"),
                                      pv[:, u, 0:a.n_v].rearrange("p (h d) -> p h d", d=a.hd),
                                      v_row.rearrange("p (h d) -> p h d", d=a.hd), op).then_inc(v_out, 1)

        @block.sync
        def _(sp):
            def step(b, j, n, u, rows):
                sp.wait_ge(lo, n + 3)
                sp.dma_start(g.qk_dram[b, :, ds(j * P, rows), :].rearrange("two p t -> p two t"),
                             qk[0:rows, ds(n, 1), :, :].rearrange("p o two t -> p (o two) t")).then_inc(stored, 16)
            chunks(sp, step)
            sp.wait_ge(stored, 16 * NB * nch)


def attend(nc, tag, g, a, vz):
    body = 8
    per_batch = a.h // body
    items = NB * per_batch
    slots = min(4, items)
    kvi = max(1, body * a.kv // a.h)
    rows = 3 * a.hd
    hb = P // a.sw
    og_n = body // hb
    if a.causal:
        units = [([(0, 0), (3, T)], 0), ([(1, P), (2, T)], P)]
        width = T + P
        max_units = [(i, h0 + h, n, (i + 1) * P) for h0 in (0, 4) for i, n in enumerate((4, 2, 1, 1))
                     for h in range(0, 4, n)]
    else:
        units = [([(0, 0), (1, T)], 0), ([(2, 0), (3, T)], 0)]
        width = 2 * T
        max_units = [(i, h, 1, T) for h in range(body) for i in range(NI)]
    n_mu = len(max_units)
    ahead = 3
    late = 2
    spots = 4 * body
    loads = 2 * len(PRODUCTS) + 1
    vh = 4 if body // kvi == 1 else 1
    staged_v = items > 2
    one_pair = float(np.ones(2, np.float16).view(np.float32)[0])

    with Phase(nc, tag, "q_filled k_filled zeroed stacked m_scored maxed m_turned m_hi m_lo placed "
                        "scored exped summed taken turned inverted normed staged passed padded") as (
            block, q_filled, k_filled, zeroed, stacked, m_scored, maxed, m_turned, m_hi, m_lo, placed,
            scored, exped, summed, taken, turned, inverted, normed, staged, passed, padded), \
            nc.psum_tensor(f"{tag}_ps", [P, 2, 2 * BANK], F32) as ps, \
            nc.psum_tensor(f"{tag}_pm", [P, 2, BANK], F32) as pm, \
            nc.psum_tensor(f"{tag}_po", [P, BANK], F32) as po, \
            nc.psum_tensor(f"{tag}_pt", [P, BANK], F32) as pt, \
            nc.sbuf_tensor(f"{tag}_qs", [P, slots * body, T], F16) as qs, \
            nc.sbuf_tensor(f"{tag}_ks", [P, slots * kvi, T], F16) as ks, \
            nc.sbuf_tensor(f"{tag}_zt", [2, T], F16) as zt, \
            nc.sbuf_tensor(f"{tag}_mx", [P, NI, body], F32) as mx, \
            nc.sbuf_tensor(f"{tag}_mn", [body, 2, T], F16) as mn, \
            nc.sbuf_tensor(f"{tag}_pr", [P, body * 2, width], F32) as pr, \
            nc.sbuf_tensor(f"{tag}_vs", [P, 2, NI, vh, a.sw], F32) as vs, \
            nc.sbuf_tensor(f"{tag}_ou", [P, 2, BANK], F32) as ou, \
            nc.sbuf_tensor(f"{tag}_ri", [P, 2, NI, hb], F32) as ri:

        def all_items(eng, step):
            for n in range(items):
                if n in (0, items - 2, items - 1):
                    for k in range(body):
                        step(n, k, min(2, items - 1 - n))
                if n == 0 and items > 3:
                    with eng.Fori(1, items - 2) as i:
                        for k in range(body):
                            step(i, k, 2)

        def back(n, k, lag, fn):
            if k >= lag:
                fn(n, k - lag)
            elif not (isinstance(n, int) and n == 0):
                fn(n - 1, k - lag + body)

        def group_of(fn):
            return lambda n, k: fn(n, k // hb) if k % hb == hb - 1 else None

        def drain(*fns):
            for past in range(max(lag for lag, _ in fns)):
                for lag, fn in fns:
                    if past < lag:
                        fn(items - 1, body - lag + past)

        def fixed(eng, value):
            return value if isinstance(value, int) else eng.snap(value)

        def slot(eng, n, each, k):
            return fixed(eng, (n % slots if isinstance(n, int) else n & (slots - 1)) * each + k)

        def batch(n):
            return n // per_batch if isinstance(n, int) else (n >> (per_batch.bit_length() - 1)) & (NB - 1)

        def group(n):
            return n % per_batch if isinstance(n, int) else n & (per_batch - 1)

        def max_spots(maximum, n, k, follow):
            due, at = (n + 1, k + ahead) if k + ahead < body else (n + 2, k + ahead - body)

            def spot(s):
                if k + ahead < body and follow >= 1 or follow == 2:
                    for u in range(n_mu * (4 * at + s) // spots, n_mu * (4 * at + s + 1) // spots):
                        maximum(due)(u)
            return spot

        def first_maxima(unit, turn):
            for u in range(n_mu):
                unit(0)(u)
            turn()
            for u in range(n_mu * 4 * ahead // spots):
                unit(1)(u)

        def places_maxima(k, follow):
            return k + ahead == body and follow >= 1

        def region(u):
            _, _, heads, keys = max_units[u]
            return pm[:, u % 2, 0:heads * keys].rearrange("p (h k) -> p h k", k=keys)

        @block.gpsimd
        def _(pool):
            pool.memset(zt[:, :].bitcast(F32), 0.0).then_inc(zeroed, 1)
            pool.memset(vs[:, :, :, :, :], 0.0).then_inc(padded, 1)
            for s in range(slots):
                pool.memset(qs[:, s * body:(s + 1) * body, :].bitcast(F32), 0.0).then_inc(q_filled, 1)

        @block.sync
        def _(sp):
            def wait(sem, value):
                if not isinstance(value, int) or value > 0:
                    sp.wait_ge(sem, value)
                    sp.sem_inc(passed, 1)

            def stack(n):
                b, gr = fixed(sp, batch(n)), fixed(sp, group(n))
                q0, k0 = slot(sp, n, body, 0), slot(sp, n, kvi, 0)
                q_row = fixed(sp, gr * (body * a.hd))
                k_row = fixed(sp, a.n_q + (0 if a.kv == 1 else gr * (kvi * a.hd)))
                if isinstance(n, int):
                    sp.wait_ge(q_filled, min(n + 1, slots))
                    sp.wait_ge(k_filled, min(n + 1, slots))
                else:
                    wait(scored, (n - 3) * (2 * body))
                wait(stacked, n * (16 * loads))
                sp.dma_start(qs[rows:rows + 2, ds(q0, body), :],
                             zt[:, :].unsqueeze(1).to_broadcast([2, body, T])).then_inc(stacked, 16)
                for r, (qp, kp) in enumerate(PRODUCTS):
                    sp.dma_start(qs[r * a.hd:(r + 1) * a.hd, ds(q0, body), :],
                                 g.qk_dram[ds(b, 1), qp, ds(q_row, body * a.hd), :]
                                 .rearrange("o (h d) t -> d (o h) t", d=a.hd)).then_inc(stacked, 16)
                    sp.dma_start(ks[r * a.hd:(r + 1) * a.hd, ds(k0, kvi), :],
                                 g.qk_dram[ds(b, 1), kp, ds(k_row, kvi * a.hd), :]
                                 .rearrange("o (h d) t -> d (o h) t", d=a.hd)).then_inc(stacked, 16)

            def place(n):
                q0 = slot(sp, n, body, 0)
                wait(placed, n * 32)
                wait(m_lo, n + 1)
                for part in range(2):
                    sp.dma_start(qs[rows + part:rows + part + 1, ds(q0, body), :],
                                 mn[:, part:part + 1, :]).then_inc(placed, 16)

            sp.wait_ge(zeroed, 1)
            stack(0)
            stack(1)
            for n in (0, 1):
                place(n)
                if n + 2 < items:
                    stack(n + 2)
            if items > 2:
                with sp.Fori(2, items - 2) as n:
                    place(n)
                    stack(sp.snap(n + 2))
                for n in (items - 2, items - 1):
                    place(n)
            sp.wait_ge(stacked, items * 16 * loads)
            sp.wait_ge(placed, items * 32)

        @block.tensor
        def _(pe):
            def maximum(n):
                def unit(u):
                    i, h0, heads, keys = max_units[u]
                    pe.wait_ge(maxed, n * n_mu + u + 1)
                    if u == 0:
                        pe.wait_ge(stacked, (n + 1) * (16 * loads))
                    for k in range(heads):
                        mm = pe.matmul(region(u)[:, k, :],
                                       qs[:, ds(slot(pe, n, body, h0 + k), 1), i * P:(i + 1) * P]
                                       .rearrange("p o q -> p (o q)"),
                                       ks[:, ds(slot(pe, n, kvi, (h0 + k) * kvi // body), 1), 0:keys]
                                       .rearrange("p o k -> p (o k)"), start=True, stop=not a.causal)
                        if a.causal:
                            mm = pe.matmul(region(u)[:, k, keys - P:keys], g.ident_b[:, :], g.mask_qk[:, :],
                                           start=False, stop=True)
                    mm.then_inc(m_scored, 1)
                return unit

            def turn_maxima(n, turns):
                pe.wait_ge(maxed, (n + 1) * n_mu + 2)
                wait_pos(pe, normed, turns)
                wait_pos(pe, m_lo, n)
                for i in range(NI):
                    mm = pe.transpose(pt[0:body, i * P:(i + 1) * P], mx[:, i, :], g.ident[:, :])
                mm.then_inc(m_turned, 1)

            def scores(n, k, w):
                unit, _ = units[w]
                if k == 0 and w == 0:
                    pe.wait_ge(placed, (n + 1) * 32)
                wait_pos(pe, exped, (n * body + k) * 2 + w - 1)
                kv = slot(pe, n, kvi, k * kvi // body)
                h = slot(pe, n, body, k)
                for j, at in unit:
                    q0 = j * P if a.causal else 0
                    mm = pe.matmul(ps[:, w, at:at + T - q0],
                                   ks[:, ds(kv, 1), j * P:(j + 1) * P].rearrange("p o k -> p (o k)"),
                                   qs[:, ds(h, 1), q0:T].rearrange("p o q -> p (o q)"),
                                   start=True, stop=not a.causal)
                    if a.causal:
                        mm = pe.matmul(ps[:, w, at:at + P], g.ident_b[:, :], g.mask_kq[:, :],
                                       start=False, stop=True)
                mm.then_inc(scored, 1)

            def values(n, group, between=lambda s: None):
                heads = range(group * hb, (group + 1) * hb)
                pe.wait_ge(exped, (n * body + heads[-1] + 1) * 2)
                wait_pos(pe, taken, n * og_n + group)
                if staged_v:
                    pe.wait_ge(staged, n * 2 + group + 1)
                for j in range(NI):
                    w, at = next((w, at - first) for w, (unit, first) in enumerate(units)
                                 for jj, at in unit if jj == j)
                    q0 = j * P if a.causal else 0
                    for s, k in enumerate(heads):
                        if staged_v:
                            v = vs[:, k // 4, j, k % 4 if vh == 4 else 0, :]
                        else:
                            v = vz[:, n * NI + j, k * kvi // body, :]
                        mm = pe.matmul(po[s * a.sw:(s + 1) * a.sw, q0:T], v, pr[:, k * 2 + w, at:at + T - q0],
                                       start=j == 0, stop=j == NI - 1)
                    if j == NI - 1:
                        mm.then_inc(summed, 1)
                    if j < 3:
                        between(1 + j)

            def turn(maxima):
                def outputs(n, group):
                    og = n * og_n + group
                    pe.wait_ge(taken, og + 1)
                    wait_pos(pe, normed, og)
                    pe.wait_ge(m_lo, maxima)
                    for i in range(NI):
                        mm = pe.transpose(pt[:, i * P:(i + 1) * P], ou[:, group % 2, i * P:(i + 1) * P], g.ident[:, :])
                    mm.then_inc(turned, 1)
                return outputs

            first_maxima(maximum, lambda: turn_maxima(0, 0))

            def step(n, k, follow):
                spot = max_spots(maximum, n, k, follow)
                scores(n, k, 0)
                if places_maxima(k, follow):
                    scores(n, k, 1)
                    turn_maxima(n + 1, n * og_n + (k - late - 1) // hb)
                    spot(0)
                else:
                    spot(0)
                    scores(n, k, 1)
                if k % hb == (late - 1) % hb and not (isinstance(n, int) and n == 0 and k < late):
                    back(n, k, late, group_of(lambda m, group: values(m, group, spot)))
                else:
                    for s in (1, 2, 3):
                        spot(s)
                back(n, k, late + 1, group_of(turn(n + 2 if k + ahead >= body and follow >= 1 else n + 1)))

            all_items(pe, step)
            drain((late, group_of(values)), (late + 1, group_of(turn(items))))

        @block.scalar
        def _(act):
            def negate_high(n):
                act.wait_ge(m_turned, n + 1)
                wait_pos(act, placed, n * 32)
                act.activation(mn[:, 0, :], pt[0:body, :], ACT.Copy, scale=-1.0).then_inc(m_hi, 1)

            negate_high(0)

            act.wait_ge(padded, 1)

            def stage_v(n, k):
                kv = k * kvi // body + (0 if a.kv == 1 else group(n) * kvi)
                j, kv = fixed(act, batch(n) * NI), fixed(act, kv)
                act.activation(vs[:, k // 4, :, :, 0:a.vw], vz[:, ds(j, NI), ds(kv, vh), :], ACT.Copy).then_inc(staged, 1)

            def step(n, k, follow):
                for w, (_, first) in enumerate(units):
                    act.wait_ge(scored, (n * body + k) * 2 + w + 1)
                    if w == 0:
                        wait_pos(act, summed, (n - 1) * og_n + k // hb + 1)
                    act.activation(pr[:, k * 2 + w, :], ps[:, w, first:first + width], ACT.Exp,
                                   scale=a.scale).then_inc(exped, 1)
                    if staged_v and k % 4 == 0 and w == 0:
                        stage_v(n, k)
                if places_maxima(k, follow):
                    negate_high(n + 1)
            all_items(act, step)

        @block.vector
        def _(dve):
            dve.sem_inc(maxed, 2)
            for s in range(slots):
                dve.memset(ks[:, s * kvi:(s + 1) * kvi, :].bitcast(F32), one_pair).then_inc(k_filled, 1)

            def maximum(n):
                def unit(u):
                    i, h0, heads, keys = max_units[u]
                    if u == 0:
                        wait_pos(dve, m_turned, n)
                    dve.wait_ge(m_scored, n * n_mu + u + 1)
                    dve.tensor_reduce(mx[:, i, h0:h0 + heads], region(u), AX.X, ALU.max).then_inc(maxed, 1)
                return unit

            def negate_low(n):
                dve.wait_ge(m_hi, n + 1)
                dve.scalar_tensor_tensor(out=mn[:, 1, :], in0=pt[0:body, :], scalar=-1.0, in1=mn[:, 0, :],
                                         op0=ALU.mult, op1=ALU.subtract).then_inc(m_lo, 1)

            def take(n, group):
                og = n * og_n + group
                dve.wait_ge(summed, og + 1)
                wait_pos(dve, turned, og - 1)
                dve.tensor_copy(ou[:, group % 2, :], po[:, :]).then_inc(taken, 1)

            def normalise(n, outputs):
                og = n * og_n + outputs
                dve.wait_ge(turned, og + 1)
                out = pt[:, :].rearrange("p (i h d) -> p i h d", i=NI, d=a.sw)
                r = ri[:, outputs % 2, :, :]
                dve.reciprocal(r, out[:, :, :, a.hd]).then_inc(inverted, 1)
                dve.wait_ge(inverted, og + 1)
                col = fixed(dve, (group(n) * body + outputs * hb) * a.hd)
                dst = g.att[:, ds(fixed(dve, batch(n) * NI), NI), ds(col, hb * a.hd)]
                dve.tensor_tensor(dst.rearrange("p i (h d) -> p i h d", d=a.hd), out[:, :, :, 0:a.hd],
                                  r.unsqueeze(3).to_broadcast([P, NI, hb, a.hd]), ALU.mult).then_inc(normed, 1)

            first_maxima(maximum, lambda: negate_low(0))

            def step(n, k, follow):
                spot = max_spots(maximum, n, k, follow)
                spot(0)
                spot(1)
                back(n, k, late + 2, group_of(normalise))
                if places_maxima(k, follow):
                    negate_low(n + 1)
                spot(2)
                spot(3)
                back(n, k, late, group_of(take))
            all_items(dve, step)
            drain((late + 2, group_of(normalise)), (late, group_of(take)))


def project_out(nc, tag, g, a, b, wo, row):
    kc = a.n_q // P
    pairs = ((0, 0), (1, 0)) if a.binary else PRODUCTS
    with Phase(nc, tag, "turned hi lo made out") as (block, turned, hi, lo, made, out), \
            nc.psum_tensor(f"{tag}_pt", [P, kc, BANK], F32) as pt, \
            nc.psum_tensor(f"{tag}_po", [P, NI, BANK], F32) as po, \
            nc.sbuf_tensor(f"{tag}_ot", [P, 2, kc, T], F16) as ot:

        @block.tensor
        def _(pe):
            for c in range(kc):
                for i in range(NI):
                    mm = pe.transpose(pt[:, c, i * P:(i + 1) * P], g.att[:, b * NI + i, c * P:(c + 1) * P], g.ident[:, :])
                mm.then_inc(turned, 1)
            pe.wait_ge(lo, kc)
            for i in range(NI):
                product(pe, po[:, i, :], lambda part, c: ot[:, part, c, i * P:(i + 1) * P],
                        lambda part, c: wo[:, part, c, :], range(kc), pairs).then_inc(made, 1)

        @block.scalar
        def _(act):
            for c in range(kc):
                act.wait_ge(turned, c + 1)
                act.activation(ot[:, 0, c, :], pt[:, c, :], ACT.Copy).then_inc(hi, 1)

        @block.vector
        def _(dve):
            for c in range(kc):
                dve.wait_ge(hi, c + 1)
                dve.tensor_tensor(ot[:, 1, c, :], pt[:, c, :], ot[:, 0, c, :], ALU.subtract).then_inc(lo, 1)
            for i in range(NI):
                dve.wait_ge(made, i + 1)
                dve.tensor_tensor(g.att[:, b * NI + i, :], po[:, i, :], row,
                                  ALU.mult if a.binary else ALU.add).then_inc(out, 1)


def attention(nc, tag, g, a, vz, wo, o_row):
    attend(nc, f"{tag}a", g, a, vz)
    for b in range(NB):
        project_out(nc, f"{tag}o{b}", g, a, b, wo, o_row)


def clear_semaphores(nc):
    nc.clear_and_free_semaphores(Phase.held)
    nc.all_engine_barrier()
    Phase.held = []


class Heads:

    def __init__(self, h, kv, hd, causal, scale, binary=False):
        self.h, self.kv, self.hd, self.causal, self.scale, self.binary = h, kv, hd, causal, scale, binary
        self.n_q, self.n_v = h * hd, kv * hd
        self.sw = 32 if hd < 32 else 64
        self.vw = hd + 1 if h > 8 else self.sw
        self.n_qk = self.n_q + kv * hd
        self.n_all = self.n_qk + self.n_v


def project_rotary(nc, tag, g, a, w, vz, brow, cos, sin):
    half = a.hd // 2
    with Phase(nc, tag, "made biased sined cosed rotated turned hi lo v_out padded ones_set stored") as (
            block, made, biased, sined, cosed, rotated, turned, hi, lo, v_out, padded, ones_set, stored), \
            nc.psum_tensor(f"{tag}_pq", [P, 3, BANK], F32) as pq, \
            nc.psum_tensor(f"{tag}_pt", [P, 2, BANK], F32) as pt, \
            nc.sbuf_tensor(f"{tag}_qb", [P, 2, a.n_q], F32) as qb, \
            nc.sbuf_tensor(f"{tag}_qc", [P, 2, a.n_q], F32) as qc, \
            nc.sbuf_tensor(f"{tag}_qsn", [P, 2, a.n_q], F32) as qsn, \
            nc.sbuf_tensor(f"{tag}_rot", [P, 2, a.n_q], F32) as rot, \
            nc.sbuf_tensor(f"{tag}_qk", [P, 2, KC, 2, NT * P], F16) as qk:

        def heads(ap):
            return ap.rearrange("p (h d) -> p h d", d=a.hd)

        def table(tab, t):
            return tab[:, ds(t, 1), :].to_broadcast([P, a.h, a.hd])

        def tiles(eng, step):
            with eng.Fori(0, NT) as t:
                step(eng.snap(t))

        @block.tensor
        def _(pe):
            pe.sem_inc(turned, 2)

            def step(t):
                for m in range(3):
                    if m < 2:
                        pe.wait_ge(biased, t * 2 + m + 1)
                    else:
                        pe.wait_ge(v_out, t + 1)
                    product(pe, pq[:, m, :], lambda part, c: g.xt[:, part, c, ds(t * P, P)],
                            lambda part, c: w[:, part, c, m * a.n_q:(m + 1) * a.n_q], range(KC)).then_inc(made, 1)
                for m in range(2):
                    pe.wait_ge(rotated, t * 4 + 2 * m + 6)
                    pe.wait_ge(lo, t * 2 + m + 1)
                    for c in range(KC):
                        mm = pe.transpose(pt[:, m, c * P:(c + 1) * P], rot[:, m, c * P:(c + 1) * P], g.ident[:, :])
                    mm.then_inc(turned, 1)
            tiles(pe, step)

        @block.vector
        def _(dve):
            dve.sem_inc(biased, 2)
            dve.sem_inc(rotated, 4)
            dve.sem_inc(lo, 2)
            dve.sem_inc(v_out, 1)
            dve.wait_ge(ones_set, 1)

            def step(t):
                for m in range(2):
                    dve.wait_ge(made, t * 3 + m + 1)
                    dve.tensor_tensor(qb[:, m, :], pq[:, m, :], brow[:, m * a.n_q:(m + 1) * a.n_q],
                                      ALU.add).then_inc(biased, 1)
                    dve.wait_ge(biased, t * 2 + m + 3)
                    dve.tensor_tensor(heads(qc[:, m, :]), heads(qb[:, m, :]), table(cos, t), ALU.mult).then_inc(cosed, 1)
                    dve.wait_ge(cosed, t * 2 + m + 1)
                    dve.wait_ge(sined, t * 2 + m + 1)
                    dve.wait_ge(turned, t * 2 + m + 1)
                    out, c_, s_ = heads(rot[:, m, :]), heads(qc[:, m, :]), heads(qsn[:, m, :])
                    dve.tensor_tensor(out[:, :, 0:half], c_[:, :, 0:half], s_[:, :, half:], ALU.subtract).then_inc(rotated, 1)
                    dve.tensor_tensor(out[:, :, half:], c_[:, :, half:], s_[:, :, 0:half], ALU.add).then_inc(rotated, 1)
                dve.wait_ge(made, t * 3 + 3)
                dve.tensor_tensor(vz[:, ds(t, 1), :, 0:a.hd].rearrange("p o h d -> p (o h) d"), heads(pq[:, 2, :]),
                                  heads(brow[:, 2 * a.n_q:3 * a.n_q]), ALU.add).then_inc(v_out, 1)
                for m in range(2):
                    dve.wait_ge(hi, t * 2 + m + 1)
                    dve.tensor_tensor(qk[:, m, :, 1, ds(t * P, P)], pt[:, m, :].rearrange("p (c t) -> p c t", t=P),
                                      qk[:, m, :, 0, ds(t * P, P)], ALU.subtract).then_inc(lo, 1)
            tiles(dve, step)

        @block.gpsimd
        def _(pool):
            pool.memset(vz[:, :, :, :], 0.0).then_inc(padded, 1)
            pool.wait_ge(padded, 1)
            pool.memset(vz[:, :, :, a.hd:a.hd + 1], 1.0).then_inc(ones_set, 1)

            def step(t):
                for m in range(2):
                    pool.wait_ge(biased, t * 2 + m + 3)
                    pool.wait_ge(rotated, t * 4 + 2 * m + 2)
                    pool.tensor_tensor(heads(qsn[:, m, :]), heads(qb[:, m, :]), table(sin, t), ALU.mult).then_inc(sined, 1)
            for t in range(NT):
                step(t)

        @block.scalar
        def _(act):
            def step(t):
                for m in range(2):
                    act.wait_ge(turned, t * 2 + m + 3)
                    act.activation(qk[:, m, :, 0, ds(t * P, P)], pt[:, m, :].rearrange("p (c t) -> p c t", t=P),
                                   ACT.Copy).then_inc(hi, 1)
            tiles(act, step)

        @block.sync
        def _(sp):
            for b in range(NB):
                sp.wait_ge(lo, 2 * NI * (b + 1) + 2)
                for m in range(2):
                    for c in range(KC):
                        sp.dma_start(g.qk_dram[b, :, m * a.n_q + c * P:m * a.n_q + (c + 1) * P, :]
                                     .rearrange("two p t -> p two t"), qk[:, m, c, :, b * T:(b + 1) * T]).then_inc(stored, 16)
            sp.wait_ge(stored, 16 * NB * 2 * KC)


def gated_residual(nc, tag, g, multiply, row=None):
    with Phase(nc, tag, "made free biased silued gated added") as (block, made, free, biased, silued, gated, added), \
            nc.psum_tensor(f"{tag}_pf", [P, 2, BANK], F32) as pf, \
            nc.sbuf_tensor(f"{tag}_gl", [P, 2, D], F32) as gl:

        def tiles(eng, step):
            with eng.Fori(0, NT // 2) as tt:
                for u in range(2):
                    step(eng.snap(tt * 2 + u), u)

        @block.tensor
        def _(pe):
            def step(t, u):
                pe.wait_ge(free, t + 1)
                multiply(pe, pf[:, u, :], t).then_inc(made, 1)
            tiles(pe, step)

        @block.scalar
        def _(act):
            def step(t, u):
                if row is None:
                    act.wait_ge(added, t + 1)
                    act.wait_ge(made, t + 1)
                    act.activation(gl[:, u, :], pf[:, u, :], ACT.Silu).then_inc(silued, 1)
                else:
                    act.wait_ge(biased, t + 1)
                    act.activation(gl[:, u, :], gl[:, u, :], ACT.Silu).then_inc(silued, 1)
            tiles(act, step)

        @block.vector
        def _(dve):
            dve.sem_inc(added, 2)
            dve.sem_inc(free, 2)

            def step(t, u):
                if row is not None:
                    dve.wait_ge(added, t + 1)
                    dve.wait_ge(made, t + 1)
                    dve.tensor_tensor(gl[:, u, :], pf[:, u, :], row, ALU.add).then_inc(biased, 1)
                dve.wait_ge(silued, t + 1)
                dve.sem_inc(free, 1)
                dve.tensor_tensor(gl[:, u, :], gl[:, u, :], g.att[:, ds(t, 1), :].rearrange("p o d -> p (o d)"),
                                  ALU.mult).then_inc(gated, 1)
                dve.wait_ge(gated, t + 1)
                x = g.x_res[:, ds(t, 1), :].rearrange("p o d -> p (o d)")
                dve.tensor_tensor(x, x, gl[:, u, :], ALU.add).then_inc(added, 1)
            tiles(dve, step)



def swiglu_low_rank(nc, g, ins):
    rank, width = ins["L0_sv_d"].shape
    n_i = width // P
    gu = KC * 2 * P
    down = D
    with nc.sbuf_tensor("f0_dt", [P, 2, n_i, NT * P], F16) as dt, \
            nc.sbuf_tensor("f0_wd", [P, 2, n_i, D], F16) as wd:
        with nc.sbuf_tensor("f0_ws", [P, 2, gu + down], F32) as ws, \
                nc.sbuf_tensor("f0_wgu", [P, 2, 2, gu], F16) as wgu, \
                nc.sbuf_tensor("f0_sd", [P, NB, T], F32) as sd, \
                nc.sbuf_tensor("f0_svg", [rank, 2, D], F32) as svg, \
                nc.sbuf_tensor("f0_sug", [rank, n_i, 2, P], F32) as sug, \
                nc.sbuf_tensor("f0_svd", [rank, 2, P], F32) as svd, \
                nc.sbuf_tensor("f0_sud", [rank, D], F32) as sud, \
                nc.psum_tensor("f0_pr", [P, 3 * BANK], F32) as pr, \
                nc.psum_tensor("f0_pp", [P, NB, 2, BANK], F32) as pp, \
                Phase(nc, "f0", "small_here w_here0 w_here1 low weffed hi lo paired silued gated d_hi d_lo") as (
                block, small_here, w_here0, w_here1, low, weffed, hi, lo, paired, silued, gated, d_hi, d_lo):
            w_here = (w_here0, w_here1)

            def pipeline(eng, prepare, use):
                prepare(0, 0, 0)
                for i in range(2):
                    prepare(i + 1, (i + 1) % 2, (i + 1) // 2)
                    use(i, i)
                with eng.Fori(1, n_i // 2 - 1) as ii:
                    i = eng.snap(ii * 2)
                    after = eng.snap(ii * 2 + 1)
                    prepare(after, 1, ii)
                    use(i, 0)
                    prepare(eng.snap(ii * 2 + 2), 0, ii + 1)
                    use(after, 1)
                prepare(n_i - 1, 1, n_i // 2 - 1)
                use(n_i - 2, 0)
                use(n_i - 1, 1)

            @block.sync
            def _(sp):
                for dst, name in ((svg, "L0_sv_gu"), (sug, "L0_su_gu"), (sud, "L0_su_d")):
                    sp.dma_start(dst[:], ins[name]).then_inc(small_here, 16)

                def load(i, u, k):
                    wait_pos(sp, lo, i - 1)
                    sp.dma_start(ws[:, u, 0:gu].rearrange("p (c n) -> p c n", c=KC),
                                 ins["L0_gu"][:, ds(i * KC * 2 * P, KC * 2 * P)].rearrange("p (c n) -> p c n", c=KC))\
                        .then_inc(w_here[u], 16)
                    sp.dma_start(ws[:, u, gu:gu + down], ins["L0_down"][:, ds(i * D, D)]).then_inc(w_here[u], 16)
                    sp.dma_start(svd[:, u, :], ins["L0_sv_d"][:, ds(i * P, P)]).then_inc(w_here[u], 16)
                pipeline(sp, load, lambda i, u: None)

            @block.tensor
            def _(pe):
                pe.wait_ge(small_here, 48)

                def low_rank(i, u, k):
                    wait_pos(pe, weffed, i)
                    pe.wait_ge(w_here[u], (k + 1) * 48)
                    for c in range(KC):
                        for m in range(2):
                            at = (c * 2 + m) * P
                            pe.matmul(pr[:, at:at + P], svg[:, m, c * P:(c + 1) * P],
                                      sug[:, ds(i, 1), m, :].rearrange("r o n -> r (o n)"), start=True, stop=True)
                    pe.matmul(pr[:, gu:gu + down], svd[:, u, :], sud[:, :], start=True, stop=True).then_inc(low, 1)

                def gate_and_up(i, u):
                    pe.wait_ge(lo, i + 1)
                    for b in range(NB):
                        wait_pos(pe, gated, i * 2 - 1 + b)
                        for m in range(2):
                            mm = product(pe, pp[:, b, m, :],
                                         lambda part, c: wgu[:, u, part, (c * 2 + m) * P:(c * 2 + m + 1) * P],
                                         lambda part, c: g.xt[:, part, c, b * T:(b + 1) * T], range(KC))
                        mm.then_inc(paired, 1)
                pipeline(pe, low_rank, gate_and_up)

            @block.vector
            def _(dve):
                def effective(i, u, k):
                    dve.wait_ge(low, i + 1)
                    dve.wait_ge(w_here[u], (k + 1) * 48)
                    dve.tensor_tensor(ws[:, u, :], ws[:, u, :], pr[:, :], ALU.mult).then_inc(weffed, 1)

                def gate(i, u):
                    for b in range(NB):
                        dve.wait_ge(silued, i * 2 + b + 1)
                        dve.tensor_tensor(sd[:, b, :], sd[:, b, :], pp[:, b, 1, :], ALU.mult).then_inc(gated, 1)
                pipeline(dve, effective, gate)

            @block.scalar
            def _(act):
                def high(i, u, k):
                    act.wait_ge(weffed, i + 1)
                    wait_pos(act, paired, (i - 1) * 2)
                    act.activation(wgu[:, u, 0, :], ws[:, u, 0:gu], ACT.Copy).then_inc(hi, 1)
                    act.activation(wd[:, 0, ds(i, 1), :], ws[:, u:u + 1, gu:gu + down], ACT.Copy).then_inc(hi, 1)

                def silu(i, u):
                    for b in range(NB):
                        wait_pos(act, d_lo, i * 2 - 1 + b)
                        act.wait_ge(paired, i * 2 + b + 1)
                        act.activation(sd[:, b, :], pp[:, b, 0, :], ACT.Silu).then_inc(silued, 1)
                        act.wait_ge(gated, i * 2 + b + 1)
                        act.activation(dt[:, 0, ds(i, 1), b * T:(b + 1) * T], sd[:, b:b + 1, :], ACT.Copy).then_inc(d_hi, 1)
                pipeline(act, high, silu)

            @block.gpsimd
            def _(pool):
                def low_part(i, u, k):
                    pool.wait_ge(hi, (i + 1) * 2)
                    pool.tensor_tensor(wd[:, 1, ds(i, 1), :], ws[:, u:u + 1, gu:gu + down], wd[:, 0, ds(i, 1), :],
                                       ALU.subtract)
                    pool.tensor_tensor(wgu[:, u, 1, :], ws[:, u, 0:gu], wgu[:, u, 0, :], ALU.subtract).then_inc(lo, 1)

                def gated_low(i, u):
                    for b in range(NB):
                        pool.wait_ge(d_hi, i * 2 + b + 1)
                        pool.tensor_tensor(dt[:, 1, ds(i, 1), b * T:(b + 1) * T], sd[:, b:b + 1, :],
                                           dt[:, 0, ds(i, 1), b * T:(b + 1) * T], ALU.subtract).then_inc(d_lo, 1)
                pipeline(pool, low_part, gated_low)

        gated_residual(nc, "g0", g, lambda pe, out, t: product(
            pe, out, lambda part, j: dt[:, part, j, ds(t * P, P)], lambda part, j: wd[:, part, j, :], range(n_i)))


def hyper_connections(nc, g, ins, w24, wb, base, gate):
    n, iters, inv_tau, eps = 4, 50, 10.0, 1.1920929e-07
    nl = n * n + 2 * n
    with nc.sbuf_tensor("h_mix", [P, NT, n * n], F32) as mix, \
            nc.sbuf_tensor("h_pp", [P, NT, 2 * n], F32) as pp:
        with nc.psum_tensor("h_pl", [P, NT * nl], F32) as pl, \
                nc.sbuf_tensor("h_sq", [P, 2, D], F32) as sq, \
                nc.sbuf_tensor("h_ss", [P, NT], F32) as ss, \
                nc.sbuf_tensor("h_rr", [P, NT], F32) as rr, \
                nc.sbuf_tensor("h_lg", [P, NT, nl], F32) as lg, \
                nc.sbuf_tensor("h_m4", [P, NT * n], F32) as m4, \
                nc.sbuf_tensor("h_i4", [P, NT * n], F32) as i4, \
                nc.sbuf_tensor("h_m2", [P, NT, 2], F32) as m2, \
                nc.sbuf_tensor("h_i2", [P, NT * 2], F32) as i2, \
                nc.sbuf_tensor("h_gt", [P, 3], F32) as gt, \
                Phase(nc, "hs", "made squared meaned rooted centred exped gate_exped done balanced") as (
                block, made, squared, meaned, rooted, centred, exped, gate_exped, done, balanced):

            @block.tensor
            def _(pe):
                for t in range(NT):
                    mm = product(pe, pl[:, t * nl:(t + 1) * nl], lambda part, c: g.xt[:, part, c, t * P:(t + 1) * P],
                                 lambda part, c: w24[:, part, c, :], range(KC))
                mm.then_inc(made, 1)

            @block.scalar
            def _(act):
                for t in range(NT):
                    wait_pos(act, squared, t - 1)
                    act.activation(sq[:, t % 2, :], g.xn[:, t, :], ACT.Square, accum_out=ss[:, t:t + 1]).then_inc(squared, 1)
                act.activation(gt[:, 0:1], gate[:, :], ACT.Exp, scale=-1.0).then_inc(gate_exped, 1)
                act.wait_ge(meaned, 1)
                act.activation(ss[:, :], ss[:, :], ACT.Sqrt).then_inc(rooted, 1)
                act.wait_ge(centred, 2)
                act.activation(mix[:, :, :], mix[:, :, :], ACT.Exp, scale=inv_tau).then_inc(exped, 1)
                act.activation(pp[:, :, :], pp[:, :, :], ACT.Exp).then_inc(exped, 1)

            @block.vector
            def _(dve):
                count = 0

                def chain(ins_):
                    nonlocal count
                    count += 1
                    ins_.then_inc(done, 1)
                    dve.wait_ge(done, count)

                dve.wait_ge(squared, NT)
                dve.tensor_scalar(ss[:, :], ss[:, :], 1.0 / D, eps, ALU.mult, ALU.add).then_inc(meaned, 1)
                dve.wait_ge(rooted, 1)
                chain(dve.reciprocal(rr[:, :], ss[:, :]))
                dve.wait_ge(made, 1)
                chain(dve.tensor_tensor(lg[:, :, :], pl.rearrange("p (t n) -> p t n", n=nl),
                                        rr[:, :].unsqueeze(2).to_broadcast([P, NT, nl]), ALU.mult))
                chain(dve.tensor_tensor(lg[:, :, :], lg[:, :, :], base[:, :].unsqueeze(1).to_broadcast([P, NT, nl]), ALU.add))
                res = lg[:, :, 0:n * n].rearrange("p t (i j) -> p t i j", j=n)
                two = lg[:, :, n * n:].rearrange("p t (i j) -> p t i j", j=n)
                chain(dve.tensor_reduce(m4[:, :], res, AX.X, ALU.max))
                chain(dve.tensor_reduce(m2[:, :, :], two, AX.X, ALU.max))
                two_p = pp[:, :, :].rearrange("p t (i j) -> p (t i) j", j=n)
                dve.tensor_tensor(mix[:, :, :].rearrange("p t (i j) -> p t i j", j=n), res,
                                  m4[:, :].rearrange("p (t i) -> p t i", i=n).unsqueeze(3).to_broadcast([P, NT, n, n]),
                                  ALU.subtract).then_inc(centred, 1)
                dve.tensor_tensor(pp[:, :, :].rearrange("p t (i j) -> p t i j", j=n), two,
                                  m2[:, :, :].unsqueeze(3).to_broadcast([P, NT, 2, n]), ALU.subtract).then_inc(centred, 1)
                dve.wait_ge(exped, 2)
                chain(dve.tensor_reduce(m2[:, :, :].rearrange("p t i -> p (t i)"), two_p, AX.X, ALU.add))
                chain(dve.reciprocal(i2[:, :], m2[:, :, :].rearrange("p t i -> p (t i)")))
                chain(dve.tensor_tensor(two_p, two_p, i2[:, :].unsqueeze(2).to_broadcast([P, NT * 2, n]), ALU.mult))
                dve.sem_inc(balanced, 2)
                with dve.Fori(0, iters) as it:
                    for k in range(6):
                        for half in range(2):
                            tiles = slice(half * NI, (half + 1) * NI)
                            own = slice(half * NI * n, (half + 1) * NI * n)
                            dve.wait_ge(balanced, it * 12 + (2 * k + half + 1))
                            byrow = mix[:, tiles, :].rearrange("p t (i j) -> p (t i) j", j=n)
                            bycol = mix[:, tiles, :].rearrange("p t (i j) -> p t j i", j=n)
                            sums, inverse = m4[:, own], i4[:, own]
                            if k == 0:
                                op = dve.tensor_reduce(sums, byrow, AX.X, ALU.add)
                            elif k == 3:
                                op = dve.tensor_reduce(sums.rearrange("p (t j) -> p t j", j=n), bycol, AX.X, ALU.add)
                            elif k == 2:
                                op = dve.tensor_tensor(byrow, byrow, inverse.unsqueeze(2).to_broadcast([P, NI * n, n]),
                                                       ALU.mult)
                            elif k == 5:
                                op = dve.tensor_tensor(bycol, bycol, inverse.rearrange("p (t j) -> p t j", j=n)
                                                       .unsqueeze(3).to_broadcast([P, NI, n, n]), ALU.mult)
                            else:
                                op = dve.reciprocal(inverse, sums)
                            op.then_inc(balanced, 1)
                dve.wait_ge(balanced, 12 * iters + 2)
                dve.wait_ge(gate_exped, 1)
                chain(dve.tensor_scalar(gt[:, 0:1], gt[:, 0:1], 1.0, None, ALU.add))
                chain(dve.reciprocal(gt[:, 1:2], gt[:, 0:1]))
                chain(dve.tensor_scalar(gt[:, 2:3], gt[:, 1:2], -1.0, 1.0, ALU.mult, ALU.add))
                chain(dve.tensor_scalar(mix[:, :, :], mix[:, :, :], gt[:, 1:2], None, ALU.mult))
                chain(dve.tensor_scalar(mix[:, :, 0:n * n:n + 1], mix[:, :, 0:n * n:n + 1], gt[:, 2:3], None, ALU.add))

        with nc.sbuf_tensor("h_xp", [P, NT, P], F32) as xp, \
                nc.sbuf_tensor("h_xpt", [P, 2, NT * P], F16) as xpt, \
                nc.sbuf_tensor("h_om", [P, 2, D], F32) as om, \
                nc.psum_tensor("h_pt", [P, 2, BANK], F32) as pt, \
                nc.psum_tensor("h_py", [P, NT, P], F32) as py, \
                Phase(nc, "hm", "pre turned hi lo branched mixed silued gated added") as (
                block, pre, turned, hi, lo, branched, mixed, silued, gated, added):

            @block.vector
            def _(dve):
                for s in range(n):
                    for t in range(NT):
                        x_s = g.xn[:, t, s * P:(s + 1) * P]
                        if s == 0:
                            dve.tensor_scalar(xp[:, t, :], x_s, pp[:, t, 0:1], None, ALU.mult).then_inc(pre, 1)
                        else:
                            dve.wait_ge(pre, (s - 1) * NT + t + 1)
                            dve.scalar_tensor_tensor(out=xp[:, t, :], in0=x_s, scalar=pp[:, t, s:s + 1], in1=xp[:, t, :],
                                                     op0=ALU.mult, op1=ALU.add).then_inc(pre, 1)
                for k in range(2):
                    dve.wait_ge(hi, k + 1)
                    dve.tensor_tensor(xpt[:, 1, k * BANK:(k + 1) * BANK], pt[:, k, :], xpt[:, 0, k * BANK:(k + 1) * BANK],
                                      ALU.subtract).then_inc(lo, 1)
                dve.wait_ge(branched, 1)
                dve.sem_inc(added, 2)
                with dve.Fori(0, NT // 2) as tt:
                    for u in range(2):
                        t = dve.snap(tt * 2 + u)
                        dve.wait_ge(added, t + 1)
                        xt_ = g.xn[:, ds(t, 1), :].rearrange("p o d -> p (o d)")
                        y = py[:, ds(t, 1), :].rearrange("p o d -> p (o d)")
                        h_ = mix[:, ds(t, 1), :].rearrange("p o d -> p (o d)")
                        w_ = pp[:, ds(t, 1), :].rearrange("p o d -> p (o d)")
                        for i in range(n):
                            dve.tensor_scalar(om[:, u, i * P:(i + 1) * P], y, w_[:, n + i:n + i + 1], None, ALU.mult)\
                                .then_inc(mixed, 1)
                        for j in range(n):
                            for i in range(n):
                                o = om[:, u, i * P:(i + 1) * P]
                                dve.wait_ge(mixed, t * (n * n + n) + j * n + i + 1)
                                dve.scalar_tensor_tensor(out=o, in0=xt_[:, j * P:(j + 1) * P],
                                                         scalar=h_[:, i * n + j:i * n + j + 1], in1=o,
                                                         op0=ALU.mult, op1=ALU.add).then_inc(mixed, 1)
                        dve.wait_ge(silued, t + 1)
                        dve.tensor_tensor(om[:, u, :], om[:, u, :], g.att[:, ds(t, 1), :].rearrange("p o d -> p (o d)"),
                                          ALU.mult).then_inc(gated, 1)
                        dve.wait_ge(gated, t + 1)
                        x = g.x_res[:, ds(t, 1), :].rearrange("p o d -> p (o d)")
                        dve.tensor_tensor(x, x, om[:, u, :], ALU.add).then_inc(added, 1)

            @block.tensor
            def _(pe):
                for t in range(NT):
                    pe.wait_ge(pre, (n - 1) * NT + t + 1)
                    pe.transpose(pt[:, t // NI, (t % NI) * P:(t % NI + 1) * P], xp[:, t, :], g.ident[:, :]).then_inc(turned, 1)
                pe.wait_ge(lo, 2)
                for t in range(NT):
                    mm = product(pe, py[:, t, :], lambda part, c: xpt[:, part, t * P:(t + 1) * P],
                                 lambda part, c: wb[:, part, :], range(1))
                mm.then_inc(branched, 1)

            @block.scalar
            def _(act):
                for k in range(2):
                    act.wait_ge(turned, (k + 1) * NI)
                    act.activation(xpt[:, 0, k * BANK:(k + 1) * BANK], pt[:, k, :], ACT.Copy).then_inc(hi, 1)
                with act.Fori(0, NT // 2) as tt:
                    for u in range(2):
                        t = act.snap(tt * 2 + u)
                        act.wait_ge(mixed, (t + 1) * (n * n + n))
                        act.activation(om[:, u, :], om[:, u, :], ACT.Silu).then_inc(silued, 1)


def routed_lora(nc, tag, g, w_ra, top, wt, e, r):
    er = e * r
    with nc.psum_tensor(f"{tag}_ph", [P, 2, BANK], F32) as ph, \
            nc.psum_tensor(f"{tag}_pt", [P, 2, BANK], F32) as pt, \
            nc.sbuf_tensor(f"{tag}_lg", [P, NT, e], F32) as lg, \
            nc.sbuf_tensor(f"{tag}_hh", [P, NT, er], F32) as hh, \
            nc.sbuf_tensor(f"{tag}_m", [P, NT], F32) as m, \
            nc.sbuf_tensor(f"{tag}_s", [P, NT], F32) as s, \
            nc.sbuf_tensor(f"{tag}_e", [P, NT, e], F32) as eq, \
            nc.sbuf_tensor(f"{tag}_o", [P, 2, NT, e], F32) as one, \
            nc.sbuf_tensor(f"{tag}_p", [P, NT, e], F32) as pb, \
            nc.sbuf_tensor(f"{tag}_w", [P, NT, e], F32) as wgt, \
            Phase(nc, tag, "made h_out l_out centred exped done weighted turned hi lo") as (
            block, made, h_out, l_out, centred, exped, done, weighted, turned, hi, lo):

        @block.tensor
        def _(pe):
            with pe.Fori(0, NT // 2) as tt:
                for u in range(2):
                    t = pe.snap(tt * 2 + u)
                    pe.wait_ge(l_out, t + 1)
                    pe.wait_ge(h_out, t + 1)
                    product(pe, ph[:, u, 0:e + er], lambda part, c: g.xt[:, part, c, ds(t * P, P)],
                            lambda part, c: w_ra[:, part, c, :], range(KC)).then_inc(made, 1)
            pe.wait_ge(weighted, 1)
            for t in range(NT):
                pe.transpose(pt[:, t // NI, (t % NI) * P:(t % NI + 1) * P], hh[:, t, :], g.ident[:, :]).then_inc(turned, 1)

        @block.scalar
        def _(act):
            act.sem_inc(h_out, 2)
            with act.Fori(0, NT // 2) as tt:
                for u in range(2):
                    t = act.snap(tt * 2 + u)
                    act.wait_ge(made, t + 1)
                    act.wait_ge(l_out, t + 3)
                    act.activation(hh[:, ds(t, 1), :], ph[:, u:u + 1, e:e + er], ACT.Copy).then_inc(h_out, 1)
            if top == 2:
                act.wait_ge(centred, 1)
                act.activation(pb[:, :, :], pb[:, :, :], ACT.Exp).then_inc(exped, 1)
            for k in range(2):
                act.wait_ge(turned, (k + 1) * NI)
                act.activation(wt[:, 0, k * BANK:(k + 1) * BANK], pt[:, k, :], ACT.Copy).then_inc(hi, 1)

        @block.vector
        def _(dve):
            count = 0

            def chain(ins_):
                nonlocal count
                count += 1
                ins_.then_inc(done, 1)
                dve.wait_ge(done, count)

            def over(v):
                return v.unsqueeze(2).to_broadcast([P, NT, e])

            def largest(values, mark):
                chain(dve.tensor_reduce(m[:, :], values, AX.X, ALU.max))
                chain(dve.tensor_tensor(eq[:, :, :], values, over(m[:, :]), ALU.is_equal))
                chain(dve.tensor_tensor(eq[:, :, :], eq[:, :, :], g.rank[:, :].unsqueeze(1).to_broadcast([P, NT, e]), ALU.mult))
                chain(dve.tensor_reduce(s[:, :], eq[:, :, :], AX.X, ALU.max))
                chain(dve.tensor_tensor(mark, eq[:, :, :], over(s[:, :]), ALU.is_equal))

            dve.sem_inc(l_out, 2)
            with dve.Fori(0, NT // 2) as tt:
                for u in range(2):
                    t = dve.snap(tt * 2 + u)
                    dve.wait_ge(made, t + 1)
                    dve.tensor_copy(lg[:, ds(t, 1), :], ph[:, u:u + 1, 0:e]).then_inc(l_out, 1)
            dve.wait_ge(l_out, NT + 2)
            if top == 1:
                largest(lg[:, :, :], one[:, 0, :, :])
                chain(dve.tensor_tensor(wgt[:, :, :], one[:, 0, :, :], over(m[:, :]), ALU.mult))
            else:
                chain(dve.tensor_reduce(m[:, :], lg[:, :, :], AX.X, ALU.max))
                dve.tensor_tensor(pb[:, :, :], lg[:, :, :], over(m[:, :]), ALU.subtract).then_inc(centred, 1)
                dve.wait_ge(exped, 1)
                chain(dve.tensor_reduce(s[:, :], pb[:, :, :], AX.X, ALU.add))
                chain(dve.reciprocal(m[:, :], s[:, :]))
                chain(dve.tensor_tensor(pb[:, :, :], pb[:, :, :], over(m[:, :]), ALU.mult))
                largest(pb[:, :, :], one[:, 0, :, :])
                chain(dve.scalar_tensor_tensor(out=lg[:, :, :], in0=one[:, 0, :, :], scalar=-2.0, in1=pb[:, :, :],
                                               op0=ALU.mult, op1=ALU.add))
                largest(lg[:, :, :], one[:, 1, :, :])
                chain(dve.tensor_tensor(eq[:, :, :], one[:, 0, :, :], one[:, 1, :, :], ALU.add))
                chain(dve.tensor_tensor(wgt[:, :, :], pb[:, :, :], eq[:, :, :], ALU.mult))
                chain(dve.tensor_reduce(s[:, :], wgt[:, :, :], AX.X, ALU.add))
                chain(dve.reciprocal(m[:, :], s[:, :]))
                chain(dve.tensor_tensor(wgt[:, :, :], wgt[:, :, :], over(m[:, :]), ALU.mult))
                chain(dve.tensor_scalar(wgt[:, :, :], wgt[:, :, :], 2.0, None, ALU.mult))
            dve.wait_ge(h_out, NT + 2)
            h4 = hh[:, :, :].rearrange("p t (e r) -> p (t e) r", r=r)
            dve.tensor_tensor(h4, h4, wgt[:, :, :].rearrange("p t e -> p (t e)").unsqueeze(2)
                              .to_broadcast([P, NT * e, r]), ALU.mult).then_inc(weighted, 1)
            for k in range(2):
                dve.wait_ge(hi, k + 1)
                dve.tensor_tensor(wt[:, 1, k * BANK:(k + 1) * BANK], pt[:, k, :], wt[:, 0, k * BANK:(k + 1) * BANK],
                                  ALU.subtract).then_inc(lo, 1)


class Shared:
    pass


def split_weight(stage, parts, chunks):
    return [(stage[:, c, :], parts[:, 0, c, :], parts[:, 1, c, :]) for c in range(chunks)]


def build(nc, ins, out, layers=4):
    g = Shared()
    Phase.held = []
    with ExitStack() as top:
        def sb(name, shape, dtype, stack=top):
            return stack.enter_context(nc.sbuf_tensor(name, shape, dtype))

        g.ident = sb("ident", [P, P], F32)
        g.ident_b = sb("ident_b", [P, P], BF16)
        g.mask_qk = sb("mask_qk", [P, P], BF16)
        g.mask_kq = sb("mask_kq", [P, P], BF16)
        g.ones = sb("ones", [P, P], F32)
        g.x_res = sb("x_res", [P, NT, D], F32)
        g.att = sb("att", [P, NT, D], F32)
        g.xt = sb("xt", [P, 2, KC, NT * P], F16)
        g.qk_dram = nc.dram_tensor("qk_scratch", [NB, 2, 2 * D, T], F16).ap()
        load_constants(nc, g, ins)

        def by_chunk(name, chunks=KC):
            return ins[name].rearrange("(c p) n -> p c n", c=chunks)

        x_tiles = ins["x"].rearrange("b (i p) d -> p (b i) d", p=P)
        for layer in range(layers):
            with ExitStack() as st:
                def lsb(name, shape, dtype, st=st):
                    return sb(f"l{layer}_{name}", shape, dtype, st)

                if layer == 0:
                    a = Heads(32, 1, 16, True, 0.25)
                elif layer == 1:
                    a = Heads(8, 8, 32, True, 1.0)
                elif layer == 2:
                    a = Heads(32, 8, 16, False, 0.25, binary=True)
                else:
                    a = Heads(32, 32, 16, True, 0.25)
                nch = -(-a.n_qk // P)
                kc_o = a.n_q // P
                if layer == 1:
                    g.xn = lsb("xn", [P, NT, D], F32)
                    w24 = lsb("w24", [P, 2, KC, 24], F16)
                    wb = lsb("wb", [P, 2, P], F16)
                    base = lsb("base", [P, 24], F32)
                    gate = lsb("gate", [P, 1], F32)
                if layer >= 2:
                    w_ra = lsb("w_ra", [P, 2, KC, 8 + P], F16)
                    w_b = lsb("w_b", [P, 2, 1, D], F16)
                    g.rank = lsb("rank", [P, 8], F32)
                if layer == 3:
                    w_base = lsb("w_base", [P, 2, KC, D], F16)
                    base_row = lsb("base_row", [P, D], F32)
                with ExitStack() as at:
                    def asb(name, shape, dtype, at=at):
                        return sb(f"a{layer}_{name}", shape, dtype, at)
                    pj = at.enter_context(ExitStack())

                    def psb(name, shape, dtype, pj=pj):
                        return sb(f"p{layer}_{name}", shape, dtype, pj)
                    vz = asb("vz", [P, NT, a.kv, a.vw], F32)
                    o_row = asb("o_row", [P, D], F32)
                    wts, small = [], []
                    if a.binary:
                        sign = asb("sign", [P, 1, KC, a.n_all + D], F16)
                        w, wo = sign, sign[:, :, :, a.n_all:]
                        col = asb("col", [P, nch], F32)
                        rows = asb("rows", [P, a.n_v + D], F32)
                        v_row, o_row = rows[:, 0:a.n_v], rows[:, a.n_v:]
                    else:
                        wo = asb("wo", [P, 2, kc_o, D], F16)
                        w = psb("w", [P, 2, KC, a.n_all], F16)
                        small.append((o_row[:, :], ins[f"L{layer}_o_bias"].partition_broadcast(P)))
                        if layer == 3:
                            v_row = psb("qkv_row", [P, a.n_all], F32)
                            small.append((v_row[:, :], ins["L3_qkv_bias"].partition_broadcast(P)))
                            cos = psb("cos", [P, NT, a.hd], F32)
                            sin = psb("sin", [P, NT, a.hd], F32)
                            small += [(cos[:, :, :], ins["cos"]), (sin[:, :, :], ins["sin"])]
                            col = None
                        else:
                            v_row = psb("v_row", [P, a.n_v], F32)
                            col = psb("col", [P, nch], F32)
                            small += [(col[:, :], ins[f"L{layer}_qk_bias"]),
                                      (v_row[:, :], ins[f"L{layer}_v_bias"].partition_broadcast(P))]
                            col, v_row = col[:, :], v_row[:, :]
                        o_row = o_row[:, :]
                    if layer == 1:
                        small += [(base[:, :], ins["L1_base"].partition_broadcast(P)),
                                  (gate[:, :], ins["L1_gate"].partition_broadcast(P))]
                    if layer >= 2:
                        small.append((g.rank[:, :], ins["rank"].partition_broadcast(P)))
                    if layer == 3:
                        small.append((base_row[:, :], ins["L3_base_bias"].partition_broadcast(P)))
                    with ExitStack() as stg:
                        def ssb(name, shape, stg=stg):
                            return sb(f"s{layer}_{name}", shape, F32, stg)
                        if not a.binary:
                            for nm, parts, chunks, n in (("w", w, KC, a.n_all), ("wo", wo, kc_o, D)):
                                s_ = ssb(nm, [P, chunks, n])
                                wts.append((by_chunk(f"L{layer}_{nm}", chunks), s_[:, :, :], split_weight(s_, parts, chunks)))
                        if layer == 1:
                            s_ = ssb("w24", [P, KC, 24])
                            wts.append((by_chunk("L1_w24"), s_[:, :, :],
                                        [(s_[:, :, :], w24[:, 0], w24[:, 1])]))
                            s_ = ssb("wb", [P, P])
                            wts.append((ins["L1_wb"], s_[:, :], [(s_[:, :], wb[:, 0], wb[:, 1])]))
                        if layer >= 2:
                            s_ = ssb("w_ra", [P, KC, 8 + P])
                            wts.append((by_chunk(f"L{layer}_w_ra"), s_[:, :, :], [(s_[:, :, :], w_ra[:, 0], w_ra[:, 1])]))
                            s_ = ssb("w_b", [P, 1, D])
                            wts.append((by_chunk(f"L{layer}_w_b", 1), s_[:, :, :], [(s_[:, :, :], w_b[:, 0], w_b[:, 1])]))
                        if layer == 3:
                            s_ = ssb("w_base", [P, KC, D])
                            wts.append((by_chunk("L3_w_base"), s_[:, :, :], split_weight(s_, w_base, KC)))
                        if layer != 1:
                            g.xn = ssb("xn", [P, NT, D])
                        norm_and_split(nc, f"n{layer}", g, wts, x_in=x_tiles if layer == 0 else None, small=small)
                    if a.binary:
                        with nc.sbuf_tensor("s2_all", [P, KC, a.n_all + D], F32) as stage:
                            binary_weights(nc, "bw", g, by_chunk("L2_w"), stage, sign, a.n_qk, a.n_v, D,
                                           col, ins["L2_qk_scale"], rows, ins["L2_row_scale"])
                        col, v_row, o_row = col[:, :], v_row, o_row
                    if layer == 3:
                        project_rotary(nc, "p3", g, a, w, vz, v_row[:, :], cos, sin)
                    else:
                        project(nc, f"p{layer}", g, a, w, vz, col, v_row)
                    pj.close()
                    attention(nc, f"a{layer}", g, a, vz, wo, o_row)
                if layer == 0:
                    swiglu_low_rank(nc, g, ins)
                elif layer == 1:
                    hyper_connections(nc, g, ins, w24, wb, base, gate)
                else:
                    wt = lsb("wt", [P, 2, NT * P], F16)
                    routed_lora(nc, f"r{layer}", g, w_ra, layer - 1, wt, 8, 16)

                    def multiply(pe, psum, t):
                        if layer == 3:
                            product(pe, psum, lambda part, c: g.xt[:, part, c, ds(t * P, P)],
                                    lambda part, c: w_base[:, part, c, :], range(KC), last=False)
                        return product(pe, psum, lambda part, c: wt[:, part, ds(t * P, P)],
                                       lambda part, c: w_b[:, part, 0, :], range(1), first=layer != 3)
                    gated_residual(nc, f"g{layer}", g, multiply, base_row[:, :] if layer == 3 else None)

            clear_semaphores(nc)

        with Phase(nc, "store", "stored") as (block, stored):
            @block.sync
            def _(sp):
                sp.dma_start(out.rearrange("b (i p) d -> p (b i) d", p=P), g.x_res[:, :, :]).then_inc(stored, 16)
                sp.wait_ge(stored, 16)


def lay_out(v):
    c = np.ascontiguousarray
    f = np.float32

    def by_column(bias):
        n = -(-bias.shape[0] // P)
        full = np.zeros((n * P,), f)
        full[:bias.shape[0]] = bias
        return c(full.reshape(n, P).T)

    cat = np.concatenate
    out = {"x": v["L0_attn_x"], "ident": np.eye(P, dtype=f), "rank": np.arange(8, 0, -1).astype(f)}
    out["L0_w"] = c(cat([v["L0_attn_wq_w"], v["L0_attn_wk_w"], v["L0_attn_wv_w"]]).T)
    out["L0_wo"] = c(v["L0_attn_wo_w"].T)
    out["L0_qk_bias"] = by_column(cat([v["L0_attn_wq_b"], v["L0_attn_wk_b"]]))
    out["L0_v_bias"] = v["L0_attn_wv_b"]
    out["L0_o_bias"] = v["L0_attn_wo_b"]
    gate, up, down = v["L0_ffn_gate_w"], v["L0_ffn_up_w"], v["L0_ffn_down_w"]
    width = gate.shape[0]
    n_i = width // P
    gu = np.stack([gate, up]).reshape(2, n_i, P, KC, P).transpose(4, 1, 3, 0, 2)
    out["L0_gu"] = c(gu.reshape(P, -1))
    out["L0_down"] = c(down.T.reshape(n_i, P, D).transpose(1, 0, 2).reshape(P, -1))
    out["L0_sv_gu"] = c(np.stack([v["L0_ffn_gate_sv"], v["L0_ffn_up_sv"]]).transpose(1, 0, 2))
    out["L0_su_gu"] = c(np.stack([v["L0_ffn_gate_su"], v["L0_ffn_up_su"]]).reshape(2, n_i, P, -1).transpose(3, 1, 0, 2))
    out["L0_sv_d"] = v["L0_ffn_down_sv"]
    out["L0_su_d"] = c(v["L0_ffn_down_su"].T)
    n1 = v["L1_attn_b_qkv"].shape[0] // 3
    out["L1_w"] = c(v["L1_attn_w_qkv"].T)
    out["L1_wo"] = c(v["L1_attn_w_o"].T)
    out["L1_qk_bias"] = by_column(v["L1_attn_b_qkv"][:2 * n1])
    out["L1_v_bias"] = v["L1_attn_b_qkv"][2 * n1:]
    out["L1_o_bias"] = v["L1_attn_b_o"]
    out["L1_w24"] = c(cat([v["L1_ffn_W_res"], v["L1_ffn_W_pre"], v["L1_ffn_W_post"]]).T)
    out["L1_base"] = cat([v["L1_ffn_H_res_base"].ravel(), v["L1_ffn_H_pre_base"], v["L1_ffn_H_post_base"]])
    out["L1_gate"] = v["L1_ffn_gate"]
    out["L1_wb"] = v["L1_ffn_W_branch"]
    out["L2_w"] = c(cat([v["L2_attn_q_weight"], v["L2_attn_k_weight"], v["L2_attn_v_weight"], v["L2_attn_o_weight"]]).T)
    out["L2_qk_scale"] = by_column(cat([v["L2_attn_q_scale"], v["L2_attn_k_scale"]]))
    out["L2_row_scale"] = cat([v["L2_attn_v_scale"], v["L2_attn_o_scale"]])
    out["L2_w_ra"] = c(cat([v["L2_ffn_route_w"], v["L2_ffn_A"].reshape(P, D)]).T)
    out["L2_w_b"] = c(v["L2_ffn_Bw"].transpose(0, 2, 1).reshape(P, D))
    out["L3_w"] = v["L3_attn_qkv_w"]
    out["L3_qkv_bias"] = v["L3_attn_qkv_b"]
    out["L3_wo"] = v["L3_attn_out_w"]
    out["L3_o_bias"] = v["L3_attn_out_b"]
    out["L3_w_ra"] = c(cat([v["L3_ffn_W_router"], v["L3_ffn_lora_A"].reshape(P, D)]).T)
    out["L3_w_b"] = c(v["L3_ffn_lora_B"].transpose(0, 2, 1).reshape(P, D))
    out["L3_w_base"] = c(v["L3_ffn_W_base"].T)
    out["L3_base_bias"] = v["L3_ffn_b_base"]
    half = 8
    inv = (1.0 / 10000.0 ** (np.arange(half, dtype=f) / f(half))).astype(f)
    ang = np.arange(T, dtype=f)[:, None] * inv[None, :]
    for name, fn in (("cos", np.cos), ("sin", np.sin)):
        tab = fn(ang).astype(f).reshape(NI, P, half).transpose(1, 0, 2)
        out[name] = c(np.tile(tab, (1, NB, 2)))
    return {k: c(x) for k, x in out.items()}


def kernel(**inputs):
    import concourse.bacc as bacc
    from concourse.bass_utils import run_bass_kernel_spmd

    nc = bacc.Bacc("TRN2", target_bir_lowering=False, num_devices=1)
    arrays = lay_out({k: np.asarray(x) for k, x in inputs.items()})
    ins = {k: nc.dram_tensor(f"in_{k}", x.shape, mybir.dt.from_np(x.dtype), kind="ExternalInput").ap() for k, x in arrays.items()}
    shape = inputs["L0_attn_x"].shape
    out = nc.dram_tensor("out", shape, F32, kind="ExternalOutput").ap()
    build(nc, ins, out)
    return run_bass_kernel_spmd(nc, [{f"in_{k}": x for k, x in arrays.items()}], core_ids=[0]).results[0]["out"]
```

```python
from contextlib import ExitStack

import numpy as np

import concourse.bass as bass
from concourse import mybir

ALU = mybir.AluOpType
ACT = mybir.ActivationFunctionType
AX = mybir.AxisListType
F32 = mybir.dt.float32
F16 = mybir.dt.float16
BF16 = mybir.dt.bfloat16
ds = bass.ds

P = 128
D = 512
KC = D // P
NB = 2
T = 512
NI = T // P
NT = NB * NI
BANK = 512
PRODUCTS = ((0, 0), (1, 0), (0, 1))
MASKED = -1.0e30
LN_EPS = 1e-5


def wait_pos(eng, sem, value):
    if isinstance(value, int) and value <= 0:
        return
    eng.wait_ge(sem, value)


class Phase:

    held = []

    def __init__(self, nc, tag, names):
        self.nc, self.tag, self.names, self.stack = nc, tag, names.split(), ExitStack()

    def __enter__(self):
        sems = [self.nc.alloc_semaphore(f"{self.tag}_{n}") for n in self.names]
        Phase.held += sems
        return (self.stack.enter_context(self.nc.Block()), *sems)

    def __exit__(self, *exc):
        return self.stack.__exit__(*exc)


def product(pe, out, left, right, chunks, pairs=PRODUCTS, first=True, last=True):
    n = len(pairs) * len(chunks)
    k = 0
    for c in chunks:
        for a, b in pairs:
            mm = pe.matmul(out, left(a, c), right(b, c), start=first and k == 0, stop=last and k == n - 1)
            k += 1
    return mm


def load_constants(nc, g, ins):
    with Phase(nc, "const", "ident_here zeroed masked") as (block, ident_here, zeroed, masked):
        @block.sync
        def _(sp):
            sp.dma_start(g.ident[:, :], ins["ident"]).then_inc(ident_here, 16)
            sp.wait_ge(ident_here, 16)

        @block.vector
        def _(dve):
            dve.memset(g.ones[:, :], 1.0)
            dve.wait_ge(ident_here, 16)
            dve.tensor_copy(g.ident_b[:, :], g.ident[:, :])

        @block.gpsimd
        def _(pool):
            pool.memset(g.mask_qk[:, :], 0.0).then_inc(zeroed, 1)
            pool.memset(g.mask_kq[:, :], 0.0).then_inc(zeroed, 1)
            pool.wait_ge(zeroed, 2)
            pool.affine_select(out=g.mask_qk[:, :], in_=g.mask_qk[:, :], compare_op=ALU.is_ge, fill=MASKED,
                               base=0, pattern=[[-1, P]], channel_multiplier=1).then_inc(masked, 1)
            pool.affine_select(out=g.mask_kq[:, :], in_=g.mask_kq[:, :], compare_op=ALU.is_ge, fill=MASKED,
                               base=0, pattern=[[1, P]], channel_multiplier=-1).then_inc(masked, 1)
            pool.wait_ge(masked, 2)


def norm_and_split(nc, tag, g, weights, x_in=None, small=()):
    with Phase(nc, tag, "x_here stats aggr var std rstd normed turned hi lo w_hi w_lo small_here "
               + " ".join(f"w_here{i}" for i in range(len(weights)))) as (
            block, x_here, stats, aggr, var, std, rstd, normed, turned, hi, lo, w_hi, w_lo, small_here, *w_here), \
            nc.psum_tensor(f"{tag}_pt", [P, 8, BANK], F32) as pt, \
            nc.sbuf_tensor(f"{tag}_st", [P, NT, 6], F32) as st, \
            nc.sbuf_tensor(f"{tag}_mv", [P, NT, 2], F32) as mv, \
            nc.sbuf_tensor(f"{tag}_sd", [P, 3, NT], F32) as sd:
        splits = [(here, *part) for (_, _, parts), here in zip(weights, w_here) for part in parts]

        @block.sync
        def _(sp):
            if x_in is not None:
                sp.dma_start(g.x_res[:, :, :], x_in).then_inc(x_here, 16)
            for (dram, stage, _), here in zip(weights, w_here):
                sp.dma_start(stage, dram).then_inc(here, 16)
            for dst, src in small:
                sp.dma_start(dst, src).then_inc(small_here, 16)
            if small:
                sp.wait_ge(small_here, 16 * len(small))

        @block.vector
        def _(dve):
            if x_in is not None:
                dve.wait_ge(x_here, 16)
            for t in range(NT):
                dve.bn_stats(st[:, t, :], g.x_res[:, t, :]).then_inc(stats, 1)
            dve.wait_ge(stats, NT)
            for t in range(NT):
                dve.bn_aggr(mv[:, t, :], st[:, t, :]).then_inc(aggr, 1)
            dve.wait_ge(aggr, NT)
            dve.tensor_scalar(sd[:, 0, :], mv[:, :, 1], LN_EPS, None, ALU.add).then_inc(var, 1)
            dve.wait_ge(std, 1)
            dve.reciprocal(sd[:, 2, :], sd[:, 1, :]).then_inc(rstd, 1)
            dve.wait_ge(rstd, 1)
            for t in range(NT):
                dve.tensor_scalar(g.xn[:, t, :], g.x_res[:, t, :], mv[:, t, 0:1], sd[:, 2, t:t + 1],
                                  ALU.subtract, ALU.mult).then_inc(normed, 1)
            for n in range(NB * KC):
                b, c = divmod(n, KC)
                dve.wait_ge(hi, n + 1)
                dve.tensor_tensor(g.xt[:, 1, c, b * T:(b + 1) * T], pt[:, n, :], g.xt[:, 0, c, b * T:(b + 1) * T],
                                  ALU.subtract).then_inc(lo, 1)
            for k, (_, staged, h, l) in enumerate(splits):
                if k % 2 == 0:
                    dve.wait_ge(w_hi, k + 1)
                    dve.tensor_tensor(l, staged, h, ALU.subtract).then_inc(w_lo, 1)

        @block.gpsimd
        def _(pool):
            for k, (_, staged, h, l) in enumerate(splits):
                if k % 2:
                    pool.wait_ge(w_hi, k + 1)
                    pool.tensor_tensor(l, staged, h, ALU.subtract).then_inc(w_lo, 1)

        @block.tensor
        def _(pe):
            for n in range(NB * KC):
                b, c = divmod(n, KC)
                pe.wait_ge(normed, NI * (b + 1))
                for i in range(NI):
                    mm = pe.transpose(pt[:, n, i * P:(i + 1) * P], g.xn[:, b * NI + i, c * P:(c + 1) * P],
                                      g.ident[:, :])
                mm.then_inc(turned, 1)

        @block.scalar
        def _(act):
            act.wait_ge(var, 1)
            act.activation(sd[:, 1, :], sd[:, 0, :], ACT.Sqrt).then_inc(std, 1)
            for n in range(NB * KC):
                b, c = divmod(n, KC)
                act.wait_ge(turned, n + 1)
                act.activation(g.xt[:, 0, c, b * T:(b + 1) * T], pt[:, n, :], ACT.Copy).then_inc(hi, 1)
            for here, staged, h, l in splits:
                act.wait_ge(here, 16)
                act.activation(h, staged, ACT.Copy).then_inc(w_hi, 1)


class BinaryWeights:

    def __init__(self, nc, stack, g, a, w_view, cols_src, rows_src):
        self.nc, self.g, self.w_view, self.cols_src, self.rows_src = nc, g, w_view, cols_src, rows_src
        self.n_qk, self.n_v, self.n_o = a.n_qk, a.n_v, D
        self.sign = stack.enter_context(nc.sbuf_tensor("bw_sign", [P, 1, KC, a.n_all + D], F16))
        self.cols = stack.enter_context(nc.sbuf_tensor("bw_cols", [P, a.n_qk // P], F32))
        self.rows = stack.enter_context(nc.sbuf_tensor("bw_rows", [P, a.n_v + D], F32))

    def __enter__(self):
        nc, nch = self.nc, self.n_qk // P
        self.stack = stack = ExitStack()
        names = ("w_here", "small_here", "signed", "absd", "col_sum", "row_sum", "part")
        sems = [nc.alloc_semaphore(f"bw_{n}") for n in names]
        Phase.held += sems
        self.w_here, self.small_here, self.signed, self.absd, self.col_sum, self.row_sum, self.part = sems
        self.pc = stack.enter_context(nc.psum_tensor("bw_pc", [P, BANK], F32))
        self.pr = stack.enter_context(nc.psum_tensor("bw_pr", [P, 2, BANK], F32))
        self.stage = stack.enter_context(nc.sbuf_tensor("bw_stage", [P, KC, self.n_qk + self.n_v + self.n_o], F32))
        self.cs = stack.enter_context(nc.sbuf_tensor("bw_cs", [P, nch], F32))
        self.rs = stack.enter_context(nc.sbuf_tensor("bw_rs", [P, self.n_v + self.n_o], F32))

    def __exit__(self, *exc):
        return self.stack.__exit__(*exc)

    def load(self, sp):
        for c in range(KC):
            sp.dma_start(self.stage[:, c, :], self.w_view[:, c, :]).then_inc(self.w_here, 16)
        sp.dma_start(self.cs[:, :], self.cols_src).then_inc(self.small_here, 16)
        sp.dma_start(self.rs[:, :], self.rows_src.partition_broadcast(P)).then_inc(self.small_here, 16)

    def signs(self, act):
        act.wait_ge(self.w_here, 16 * KC)
        for c in range(KC):
            act.activation(self.sign[:, 0, c, :], self.stage[:, c, :], ACT.Sign).then_inc(self.signed, 1)
        for c in range(KC):
            act.wait_ge(self.signed, c + 1)
            act.activation(self.stage[:, c, :], self.stage[:, c, :], ACT.Abs).then_inc(self.absd, 1)

    def sums(self, pe):
        stage, pc, pr, ones = self.stage, self.pc, self.pr, self.g.ones
        pe.wait_ge(self.absd, KC)
        for j in range(self.n_qk // P):
            for c in range(KC):
                mm = pe.matmul(pc[:, j:j + 1], stage[:, c, j * P:(j + 1) * P], ones[:, 0:1],
                               start=c == 0, stop=c == KC - 1)
        mm.then_inc(self.col_sum, 1)
        for k, (at, n) in enumerate(((self.n_qk, self.n_v), (self.n_qk + self.n_v, self.n_o))):
            for c in range(KC):
                mm = pe.matmul(pr[:, k, 0:n], ones[:, :], stage[:, c, at:at + n], start=c == 0, stop=c == KC - 1)
        mm.then_inc(self.row_sum, 1)

    def scales(self, dve):
        cols, rows, n_v, n_o = self.cols, self.rows, self.n_v, self.n_o
        dve.wait_ge(self.small_here, 32)
        dve.wait_ge(self.col_sum, 1)
        dve.tensor_scalar(cols[:, :], self.pc[:, 0:self.n_qk // P], 1.0 / D, 1e-8, ALU.mult, ALU.max).then_inc(self.part, 1)
        dve.wait_ge(self.row_sum, 1)
        for k, (at, n) in enumerate(((0, n_v), (n_v, n_o))):
            dve.tensor_scalar(rows[:, at:at + n], self.pr[:, k, 0:n], 1.0 / D, 1e-8, ALU.mult, ALU.max)\
                .then_inc(self.part, 1)
        dve.wait_ge(self.part, 3)
        dve.tensor_tensor(cols[:, :], cols[:, :], self.cs[:, :], ALU.mult).then_inc(self.part, 1)
        dve.tensor_tensor(rows[:, :], rows[:, :], self.rs[:, :], ALU.mult).then_inc(self.part, 1)


def project(nc, tag, g, a, w, vz, col, v_row):
    full, left = divmod(a.n_qk, P)
    nch = full + (left > 0)
    op = ALU.mult if a.binary else ALU.add
    w_pairs = ((0, 0), (0, 1)) if a.binary else PRODUCTS
    x_pairs = ((0, 0), (1, 0)) if a.binary else PRODUCTS
    with Phase(nc, tag, "qk_made hi lo stored v_made v_out padded ones_set") as (
            block, qk_made, hi, lo, stored, v_made, v_out, padded, ones_set), \
            nc.psum_tensor(f"{tag}_pq", [P, 3, BANK], F32) as pq, \
            nc.psum_tensor(f"{tag}_pv", [P, 2, BANK], F32) as pv, \
            nc.sbuf_tensor(f"{tag}_qk", [P, NB * nch, 2, T], F16) as qk:

        def chunks(eng, step):
            for b in range(NB):
                with eng.Fori(0, full // 2) as jj:
                    for u in range(2):
                        j = eng.snap(jj * 2 + u)
                        step(b, j, eng.snap(j + b * nch), u, P)
                if left:
                    step(b, full, b * nch + full, 2, left)
                elif full % 2:
                    step(b, full - 1, b * nch + full - 1, 2, P)

        @block.tensor
        def _(pe):
            def step(b, j, n, u, rows):
                pe.wait_ge(lo, n + 1)
                product(pe, pq[0:rows, u, :], lambda part, c: w[:, part, c, ds(j * P, rows)],
                        lambda part, c: g.xt[:, part, c, b * T:(b + 1) * T], range(KC), w_pairs)\
                    .then_inc(qk_made, 1)
            chunks(pe, step)
            with pe.Fori(0, NT // 2) as tt:
                for u in range(2):
                    t = pe.snap(tt * 2 + u)
                    pe.wait_ge(v_out, t + 1)
                    product(pe, pv[:, u, 0:a.n_v], lambda part, c: g.xt[:, part, c, ds(t * P, P)],
                            lambda part, c: w[:, part, c, a.n_qk:a.n_qk + a.n_v], range(KC), x_pairs)\
                        .then_inc(v_made, 1)

        @block.scalar
        def _(act):
            def step(b, j, n, u, rows):
                act.wait_ge(qk_made, n + 1)
                out = qk[0:rows, ds(n, 1), 0, :]
                if a.binary:
                    act.activation(out, pq[0:rows, u:u + 1, :], ACT.Identity, scale=col[0:rows, ds(j, 1)]).then_inc(hi, 1)
                else:
                    act.activation(out, pq[0:rows, u:u + 1, :], ACT.Identity, bias=col[0:rows, ds(j, 1)]).then_inc(hi, 1)
            chunks(act, step)

        @block.gpsimd
        def _(pool):
            pool.memset(vz[:, :, :, :], 0.0).then_inc(padded, 1)
            pool.wait_ge(padded, 1)
            pool.memset(vz[:, :, :, a.hd:a.hd + 1], 1.0).then_inc(ones_set, 1)

        @block.vector
        def _(dve):
            dve.sem_inc(lo, 2)
            dve.sem_inc(v_out, 2)

            def step(b, j, n, u, rows):
                dve.wait_ge(hi, n + 1)
                dve.scalar_tensor_tensor(out=qk[0:rows, ds(n, 1), 1, :], in0=pq[0:rows, u:u + 1, :],
                                         scalar=col[0:rows, ds(j, 1)], in1=qk[0:rows, ds(n, 1), 0, :],
                                         op0=op, op1=ALU.subtract).then_inc(lo, 1)
            chunks(dve, step)
            dve.wait_ge(ones_set, 1)
            with dve.Fori(0, NT // 2) as tt:
                for u in range(2):
                    t = dve.snap(tt * 2 + u)
                    dve.wait_ge(v_made, t + 1)
                    dve.tensor_tensor(vz[:, ds(t, 1), :, 0:a.hd].rearrange("p o h d -> p (o h) d"),
                                      pv[:, u, 0:a.n_v].rearrange("p (h d) -> p h d", d=a.hd),
                                      v_row.rearrange("p (h d) -> p h d", d=a.hd), op).then_inc(v_out, 1)

        @block.sync
        def _(sp):
            def step(b, j, n, u, rows):
                sp.wait_ge(lo, n + 3)
                sp.dma_start(g.qk_dram[b, :, ds(j * P, rows), :].rearrange("two p t -> p two t"),
                             qk[0:rows, ds(n, 1), :, :].rearrange("p o two t -> p (o two) t")).then_inc(stored, 16)
            chunks(sp, step)
            sp.wait_ge(stored, 16 * NB * nch)


def attend(nc, tag, g, a, vz, beside):
    body = 8
    per_batch = a.h // body
    items = NB * per_batch
    slots = min(4, items)
    kvi = max(1, body * a.kv // a.h)
    rows = 3 * a.hd
    hb = P // a.sw
    og_n = body // hb
    if a.causal:
        units = [([(0, 0), (3, T)], 0), ([(1, P), (2, T)], P)]
        width = T + P
        max_units = [(i, h0 + h, n, (i + 1) * P) for h0 in (0, 4) for i, n in enumerate((4, 2, 1, 1))
                     for h in range(0, 4, n)]
    else:
        units = [([(0, 0), (1, T)], 0), ([(2, 0), (3, T)], 0)]
        width = 2 * T
        max_units = [(i, h, 1, T) for h in range(body) for i in range(NI)]
    n_mu = len(max_units)
    ahead = 3
    late = 2
    spots = 4 * body
    loads = 2 * len(PRODUCTS) + 1
    vh = 4 if body // kvi == 1 else 1
    staged_v = items > 2
    one_pair = float(np.ones(2, np.float16).view(np.float32)[0])

    with Phase(nc, tag, "q_filled k_filled zeroed stacked m_scored maxed m_turned m_hi m_lo placed "
                        "scored exped summed taken turned inverted normed staged passed padded") as (
            block, q_filled, k_filled, zeroed, stacked, m_scored, maxed, m_turned, m_hi, m_lo, placed,
            scored, exped, summed, taken, turned, inverted, normed, staged, passed, padded), \
            nc.psum_tensor(f"{tag}_ps", [P, 2, 2 * BANK], F32) as ps, \
            nc.psum_tensor(f"{tag}_pm", [P, 2, BANK], F32) as pm, \
            nc.psum_tensor(f"{tag}_po", [P, BANK], F32) as po, \
            nc.psum_tensor(f"{tag}_pt", [P, BANK], F32) as pt, \
            nc.sbuf_tensor(f"{tag}_qs", [P, slots * body, T], F16) as qs, \
            nc.sbuf_tensor(f"{tag}_ks", [P, slots * kvi, T], F16) as ks, \
            nc.sbuf_tensor(f"{tag}_zt", [2, T], F16) as zt, \
            nc.sbuf_tensor(f"{tag}_mx", [P, NI, body], F32) as mx, \
            nc.sbuf_tensor(f"{tag}_mn", [body, 2, T], F16) as mn, \
            nc.sbuf_tensor(f"{tag}_pr", [P, body * 2, width], F32) as pr, \
            nc.sbuf_tensor(f"{tag}_vs", [P, 2, NI, vh, a.sw], F32) as vs, \
            nc.sbuf_tensor(f"{tag}_ou", [P, 2, BANK], F32) as ou, \
            nc.sbuf_tensor(f"{tag}_ri", [P, 2, NI, hb], F32) as ri:

        def all_items(eng, step):
            for n in range(items):
                if n in (0, items - 2, items - 1):
                    for k in range(body):
                        step(n, k, min(2, items - 1 - n))
                if n == 0 and items > 3:
                    with eng.Fori(1, items - 2) as i:
                        for k in range(body):
                            step(i, k, 2)

        def back(n, k, lag, fn):
            if k >= lag:
                fn(n, k - lag)
            elif not (isinstance(n, int) and n == 0):
                fn(n - 1, k - lag + body)

        def group_of(fn):
            return lambda n, k: fn(n, k // hb) if k % hb == hb - 1 else None

        def drain(*fns):
            for past in range(max(lag for lag, _ in fns)):
                for lag, fn in fns:
                    if past < lag:
                        fn(items - 1, body - lag + past)

        def fixed(eng, value):
            return value if isinstance(value, int) else eng.snap(value)

        def slot(eng, n, each, k):
            return fixed(eng, (n % slots if isinstance(n, int) else n & (slots - 1)) * each + k)

        def batch(n):
            return n // per_batch if isinstance(n, int) else (n >> (per_batch.bit_length() - 1)) & (NB - 1)

        def group(n):
            return n % per_batch if isinstance(n, int) else n & (per_batch - 1)

        def max_spots(maximum, n, k, follow):
            due, at = (n + 1, k + ahead) if k + ahead < body else (n + 2, k + ahead - body)

            def spot(s):
                if k + ahead < body and follow >= 1 or follow == 2:
                    for u in range(n_mu * (4 * at + s) // spots, n_mu * (4 * at + s + 1) // spots):
                        maximum(due)(u)
            return spot

        def first_maxima(unit, turn):
            for u in range(n_mu):
                unit(0)(u)
            turn()
            for u in range(n_mu * 4 * ahead // spots):
                unit(1)(u)

        def places_maxima(k, follow):
            return k + ahead == body and follow >= 1

        def region(u):
            _, _, heads, keys = max_units[u]
            return pm[:, u % 2, 0:heads * keys].rearrange("p (h k) -> p h k", k=keys)

        @block.gpsimd
        def _(pool):
            pool.memset(zt[:, :].bitcast(F32), 0.0).then_inc(zeroed, 1)
            pool.memset(vs[:, :, :, :, :], 0.0).then_inc(padded, 1)
            for s in range(slots):
                pool.memset(qs[:, s * body:(s + 1) * body, :].bitcast(F32), 0.0).then_inc(q_filled, 1)
            if beside is not None:
                beside(pool)

        @block.sync
        def _(sp):
            def wait(sem, value):
                if not isinstance(value, int) or value > 0:
                    sp.wait_ge(sem, value)
                    sp.sem_inc(passed, 1)

            def stack(n):
                b, gr = fixed(sp, batch(n)), fixed(sp, group(n))
                q0, k0 = slot(sp, n, body, 0), slot(sp, n, kvi, 0)
                q_row = fixed(sp, gr * (body * a.hd))
                k_row = fixed(sp, a.n_q + (0 if a.kv == 1 else gr * (kvi * a.hd)))
                if isinstance(n, int):
                    sp.wait_ge(q_filled, min(n + 1, slots))
                    sp.wait_ge(k_filled, min(n + 1, slots))
                else:
                    wait(scored, (n - 3) * (2 * body))
                wait(stacked, n * (16 * loads))
                sp.dma_start(qs[rows:rows + 2, ds(q0, body), :],
                             zt[:, :].unsqueeze(1).to_broadcast([2, body, T])).then_inc(stacked, 16)
                for r, (qp, kp) in enumerate(PRODUCTS):
                    sp.dma_start(qs[r * a.hd:(r + 1) * a.hd, ds(q0, body), :],
                                 g.qk_dram[ds(b, 1), qp, ds(q_row, body * a.hd), :]
                                 .rearrange("o (h d) t -> d (o h) t", d=a.hd)).then_inc(stacked, 16)
                    sp.dma_start(ks[r * a.hd:(r + 1) * a.hd, ds(k0, kvi), :],
                                 g.qk_dram[ds(b, 1), kp, ds(k_row, kvi * a.hd), :]
                                 .rearrange("o (h d) t -> d (o h) t", d=a.hd)).then_inc(stacked, 16)

            def place(n):
                q0 = slot(sp, n, body, 0)
                wait(placed, n * 32)
                wait(m_lo, n + 1)
                for part in range(2):
                    sp.dma_start(qs[rows + part:rows + part + 1, ds(q0, body), :],
                                 mn[:, part:part + 1, :]).then_inc(placed, 16)

            sp.wait_ge(zeroed, 1)
            stack(0)
            stack(1)
            for n in (0, 1):
                place(n)
                if n + 2 < items:
                    stack(n + 2)
            if items > 2:
                with sp.Fori(2, items - 2) as n:
                    place(n)
                    stack(sp.snap(n + 2))
                for n in (items - 2, items - 1):
                    place(n)
            sp.wait_ge(stacked, items * 16 * loads)
            sp.wait_ge(placed, items * 32)

        @block.tensor
        def _(pe):
            def maximum(n):
                def unit(u):
                    i, h0, heads, keys = max_units[u]
                    pe.wait_ge(maxed, n * n_mu + u + 1)
                    if u == 0:
                        pe.wait_ge(stacked, (n + 1) * (16 * loads))
                    for k in range(heads):
                        mm = pe.matmul(region(u)[:, k, :],
                                       qs[:, ds(slot(pe, n, body, h0 + k), 1), i * P:(i + 1) * P]
                                       .rearrange("p o q -> p (o q)"),
                                       ks[:, ds(slot(pe, n, kvi, (h0 + k) * kvi // body), 1), 0:keys]
                                       .rearrange("p o k -> p (o k)"), start=True, stop=not a.causal)
                        if a.causal:
                            mm = pe.matmul(region(u)[:, k, keys - P:keys], g.ident_b[:, :], g.mask_qk[:, :],
                                           start=False, stop=True)
                    mm.then_inc(m_scored, 1)
                return unit

            def turn_maxima(n, turns):
                pe.wait_ge(maxed, (n + 1) * n_mu + 2)
                wait_pos(pe, normed, turns)
                wait_pos(pe, m_lo, n)
                for i in range(NI):
                    mm = pe.transpose(pt[0:body, i * P:(i + 1) * P], mx[:, i, :], g.ident[:, :])
                mm.then_inc(m_turned, 1)

            def scores(n, k, w):
                unit, _ = units[w]
                if k == 0 and w == 0:
                    pe.wait_ge(placed, (n + 1) * 32)
                wait_pos(pe, exped, (n * body + k) * 2 + w - 1)
                kv = slot(pe, n, kvi, k * kvi // body)
                h = slot(pe, n, body, k)
                for j, at in unit:
                    q0 = j * P if a.causal else 0
                    mm = pe.matmul(ps[:, w, at:at + T - q0],
                                   ks[:, ds(kv, 1), j * P:(j + 1) * P].rearrange("p o k -> p (o k)"),
                                   qs[:, ds(h, 1), q0:T].rearrange("p o q -> p (o q)"),
                                   start=True, stop=not a.causal)
                    if a.causal:
                        mm = pe.matmul(ps[:, w, at:at + P], g.ident_b[:, :], g.mask_kq[:, :],
                                       start=False, stop=True)
                mm.then_inc(scored, 1)

            def values(n, group, between=lambda s: None):
                heads = range(group * hb, (group + 1) * hb)
                pe.wait_ge(exped, (n * body + heads[-1] + 1) * 2)
                wait_pos(pe, taken, n * og_n + group)
                if staged_v:
                    pe.wait_ge(staged, n * 2 + group + 1)
                for j in range(NI):
                    w, at = next((w, at - first) for w, (unit, first) in enumerate(units)
                                 for jj, at in unit if jj == j)
                    q0 = j * P if a.causal else 0
                    for s, k in enumerate(heads):
                        if staged_v:
                            v = vs[:, k // 4, j, k % 4 if vh == 4 else 0, :]
                        else:
                            v = vz[:, n * NI + j, k * kvi // body, :]
                        mm = pe.matmul(po[s * a.sw:(s + 1) * a.sw, q0:T], v, pr[:, k * 2 + w, at:at + T - q0],
                                       start=j == 0, stop=j == NI - 1)
                    if j == NI - 1:
                        mm.then_inc(summed, 1)
                    if j < 3:
                        between(1 + j)

            def turn(maxima):
                def outputs(n, group):
                    og = n * og_n + group
                    pe.wait_ge(taken, og + 1)
                    wait_pos(pe, normed, og)
                    pe.wait_ge(m_lo, maxima)
                    for i in range(NI):
                        mm = pe.transpose(pt[:, i * P:(i + 1) * P], ou[:, group % 2, i * P:(i + 1) * P], g.ident[:, :])
                    mm.then_inc(turned, 1)
                return outputs

            first_maxima(maximum, lambda: turn_maxima(0, 0))

            def step(n, k, follow):
                spot = max_spots(maximum, n, k, follow)
                scores(n, k, 0)
                if places_maxima(k, follow):
                    scores(n, k, 1)
                    turn_maxima(n + 1, n * og_n + (k - late - 1) // hb)
                    spot(0)
                else:
                    spot(0)
                    scores(n, k, 1)
                if k % hb == (late - 1) % hb and not (isinstance(n, int) and n == 0 and k < late):
                    back(n, k, late, group_of(lambda m, group: values(m, group, spot)))
                else:
                    for s in (1, 2, 3):
                        spot(s)
                back(n, k, late + 1, group_of(turn(n + 2 if k + ahead >= body and follow >= 1 else n + 1)))

            all_items(pe, step)
            drain((late, group_of(values)), (late + 1, group_of(turn(items))))

        @block.scalar
        def _(act):
            def negate_high(n):
                act.wait_ge(m_turned, n + 1)
                wait_pos(act, placed, n * 32)
                act.activation(mn[:, 0, :], pt[0:body, :], ACT.Copy, scale=-1.0).then_inc(m_hi, 1)

            negate_high(0)

            act.wait_ge(padded, 1)

            def stage_v(n, k):
                kv = k * kvi // body + (0 if a.kv == 1 else group(n) * kvi)
                j, kv = fixed(act, batch(n) * NI), fixed(act, kv)
                act.activation(vs[:, k // 4, :, :, 0:a.vw], vz[:, ds(j, NI), ds(kv, vh), :], ACT.Copy).then_inc(staged, 1)

            def step(n, k, follow):
                for w, (_, first) in enumerate(units):
                    act.wait_ge(scored, (n * body + k) * 2 + w + 1)
                    if w == 0:
                        wait_pos(act, summed, (n - 1) * og_n + k // hb + 1)
                    act.activation(pr[:, k * 2 + w, :], ps[:, w, first:first + width], ACT.Exp,
                                   scale=a.scale).then_inc(exped, 1)
                    if staged_v and k % 4 == 0 and w == 0:
                        stage_v(n, k)
                if places_maxima(k, follow):
                    negate_high(n + 1)
            all_items(act, step)

        @block.vector
        def _(dve):
            dve.sem_inc(maxed, 2)
            for s in range(slots):
                dve.memset(ks[:, s * kvi:(s + 1) * kvi, :].bitcast(F32), one_pair).then_inc(k_filled, 1)

            def maximum(n):
                def unit(u):
                    i, h0, heads, keys = max_units[u]
                    if u == 0:
                        wait_pos(dve, m_turned, n)
                    dve.wait_ge(m_scored, n * n_mu + u + 1)
                    dve.tensor_reduce(mx[:, i, h0:h0 + heads], region(u), AX.X, ALU.max).then_inc(maxed, 1)
                return unit

            def negate_low(n):
                dve.wait_ge(m_hi, n + 1)
                dve.scalar_tensor_tensor(out=mn[:, 1, :], in0=pt[0:body, :], scalar=-1.0, in1=mn[:, 0, :],
                                         op0=ALU.mult, op1=ALU.subtract).then_inc(m_lo, 1)

            def take(n, group):
                og = n * og_n + group
                dve.wait_ge(summed, og + 1)
                wait_pos(dve, turned, og - 1)
                dve.tensor_copy(ou[:, group % 2, :], po[:, :]).then_inc(taken, 1)

            def normalise(n, outputs):
                og = n * og_n + outputs
                dve.wait_ge(turned, og + 1)
                out = pt[:, :].rearrange("p (i h d) -> p i h d", i=NI, d=a.sw)
                r = ri[:, outputs % 2, :, :]
                dve.reciprocal(r, out[:, :, :, a.hd]).then_inc(inverted, 1)
                dve.wait_ge(inverted, og + 1)
                col = fixed(dve, (group(n) * body + outputs * hb) * a.hd)
                dst = g.att[:, ds(fixed(dve, batch(n) * NI), NI), ds(col, hb * a.hd)]
                dve.tensor_tensor(dst.rearrange("p i (h d) -> p i h d", d=a.hd), out[:, :, :, 0:a.hd],
                                  r.unsqueeze(3).to_broadcast([P, NI, hb, a.hd]), ALU.mult).then_inc(normed, 1)

            first_maxima(maximum, lambda: negate_low(0))

            def step(n, k, follow):
                spot = max_spots(maximum, n, k, follow)
                spot(0)
                spot(1)
                back(n, k, late + 2, group_of(normalise))
                if places_maxima(k, follow):
                    negate_low(n + 1)
                spot(2)
                spot(3)
                back(n, k, late, group_of(take))
            all_items(dve, step)
            drain((late + 2, group_of(normalise)), (late, group_of(take)))


def project_out(nc, tag, g, a, wo, row):
    kc = a.n_q // P
    pairs = ((0, 0), (1, 0)) if a.binary else PRODUCTS
    with Phase(nc, tag, "turned hi lo made out") as (block, turned, hi, lo, made, out), \
            nc.psum_tensor(f"{tag}_pt", [P, kc, BANK], F32) as pt, \
            nc.psum_tensor(f"{tag}_po", [P, NI, BANK], F32) as po, \
            nc.sbuf_tensor(f"{tag}_ot", [P, NB, 2, kc, T], F16) as ot:

        @block.tensor
        def _(pe):
            for b in range(NB):
                for c in range(kc):
                    wait_pos(pe, lo, (b - 1) * kc + c + 1)
                    for i in range(NI):
                        mm = pe.transpose(pt[:, c, i * P:(i + 1) * P], g.att[:, b * NI + i, c * P:(c + 1) * P],
                                          g.ident[:, :])
                    mm.then_inc(turned, 1)
            for b in range(NB):
                pe.wait_ge(lo, (b + 1) * kc)
                for i in range(NI):
                    wait_pos(pe, out, (b - 1) * NI + i + 1)
                    product(pe, po[:, i, :], lambda part, c: ot[:, b, part, c, i * P:(i + 1) * P],
                            lambda part, c: wo[:, part, c, :], range(kc), pairs).then_inc(made, 1)

        @block.scalar
        def _(act):
            for b in range(NB):
                for c in range(kc):
                    act.wait_ge(turned, b * kc + c + 1)
                    act.activation(ot[:, b, 0, c, :], pt[:, c, :], ACT.Copy).then_inc(hi, 1)

        @block.vector
        def _(dve):
            for b in range(NB):
                for c in range(kc):
                    dve.wait_ge(hi, b * kc + c + 1)
                    dve.tensor_tensor(ot[:, b, 1, c, :], pt[:, c, :], ot[:, b, 0, c, :], ALU.subtract).then_inc(lo, 1)
            for t in range(NT):
                dve.wait_ge(made, t + 1)
                dve.tensor_tensor(g.att[:, t, :], po[:, t % NI, :], row, ALU.mult if a.binary else ALU.add).then_inc(out, 1)


def attention(nc, tag, g, a, vz, wo, o_row, beside=None):
    attend(nc, f"{tag}a", g, a, vz, beside)
    project_out(nc, f"{tag}o", g, a, wo, o_row)


def split_beside(nc, pool, tag, stage, weights):
    here, hi, lo = (nc.alloc_semaphore(f"{tag}_{n}") for n in ("here", "hi", "lo"))
    Phase.held += [here, hi, lo]
    width = stage.shape[-1]
    pieces = [tuple(ap[:, at:min(at + width, ap.shape[-1])] for ap in weight)
              for weight in weights for at in range(0, weight[0].shape[-1], width)]
    for k, (dram, high, low) in enumerate(pieces):
        n = dram.shape[-1]
        wait_pos(pool, lo, k)
        pool.dma_start(stage[:, 0:n], dram).then_inc(here, 16)
        pool.wait_ge(here, 16 * (k + 1))
        pool.tensor_copy(high, stage[:, 0:n]).then_inc(hi, 1)
        pool.wait_ge(hi, k + 1)
        pool.tensor_tensor(low, stage[:, 0:n], high, ALU.subtract).then_inc(lo, 1)


def clear_semaphores(nc):
    nc.clear_and_free_semaphores(Phase.held)
    nc.all_engine_barrier()
    Phase.held = []


class Heads:

    def __init__(self, h, kv, hd, causal, scale, binary=False):
        self.h, self.kv, self.hd, self.causal, self.scale, self.binary = h, kv, hd, causal, scale, binary
        self.n_q, self.n_v = h * hd, kv * hd
        self.sw = 32 if hd < 32 else 64
        self.vw = hd + 1 if h > 8 else self.sw
        self.n_qk = self.n_q + kv * hd
        self.n_all = self.n_qk + self.n_v


def project_rotary(nc, tag, g, a, w, vz, brow, cos, sin):
    half = a.hd // 2
    with Phase(nc, tag, "made biased sined cosed rotated turned hi lo v_out padded ones_set stored") as (
            block, made, biased, sined, cosed, rotated, turned, hi, lo, v_out, padded, ones_set, stored), \
            nc.psum_tensor(f"{tag}_pq", [P, 3, BANK], F32) as pq, \
            nc.psum_tensor(f"{tag}_pt", [P, 2, BANK], F32) as pt, \
            nc.sbuf_tensor(f"{tag}_qb", [P, 2, a.n_q], F32) as qb, \
            nc.sbuf_tensor(f"{tag}_qc", [P, 2, a.n_q], F32) as qc, \
            nc.sbuf_tensor(f"{tag}_qsn", [P, 2, a.n_q], F32) as qsn, \
            nc.sbuf_tensor(f"{tag}_rot", [P, 2, a.n_q], F32) as rot, \
            nc.sbuf_tensor(f"{tag}_qk", [P, 2, KC, 2, NT * P], F16) as qk:

        def heads(ap):
            return ap.rearrange("p (h d) -> p h d", d=a.hd)

        def table(tab, t):
            return tab[:, ds(t, 1), :].to_broadcast([P, a.h, a.hd])

        def tiles(eng, step):
            with eng.Fori(0, NT) as t:
                step(eng.snap(t))

        def tiles_and_last(eng, step, last):
            step(0)
            with eng.Fori(1, NT) as t:
                step(eng.snap(t))
                last(eng.snap(t - 1))
            last(NT - 1)

        @block.tensor
        def _(pe):
            pe.sem_inc(turned, 2)

            def step(t):
                for m in range(3):
                    if m < 2:
                        pe.wait_ge(biased, t * 2 + m + 1)
                    else:
                        pe.wait_ge(v_out, t + 1)
                    product(pe, pq[:, m, :], lambda part, c: g.xt[:, part, c, ds(t * P, P)],
                            lambda part, c: w[:, part, c, m * a.n_q:(m + 1) * a.n_q], range(KC)).then_inc(made, 1)

            def turn(t):
                for m in range(2):
                    pe.wait_ge(rotated, t * 4 + 2 * m + 6)
                    pe.wait_ge(lo, t * 2 + m + 1)
                    for c in range(KC):
                        mm = pe.transpose(pt[:, m, c * P:(c + 1) * P], rot[:, m, c * P:(c + 1) * P], g.ident[:, :])
                    mm.then_inc(turned, 1)
            tiles_and_last(pe, step, turn)

        @block.vector
        def _(dve):
            dve.sem_inc(biased, 2)
            dve.sem_inc(rotated, 4)
            dve.sem_inc(lo, 2)
            dve.sem_inc(v_out, 1)
            dve.wait_ge(ones_set, 1)

            def step(t):
                for m in range(2):
                    dve.wait_ge(made, t * 3 + m + 1)
                    dve.tensor_tensor(qb[:, m, :], pq[:, m, :], brow[:, m * a.n_q:(m + 1) * a.n_q],
                                      ALU.add).then_inc(biased, 1)
                    dve.wait_ge(biased, t * 2 + m + 3)
                    dve.tensor_tensor(heads(qc[:, m, :]), heads(qb[:, m, :]), table(cos, t), ALU.mult).then_inc(cosed, 1)
                    dve.wait_ge(cosed, t * 2 + m + 1)
                    dve.wait_ge(sined, t * 2 + m + 1)
                    dve.wait_ge(turned, t * 2 + m + 1)
                    out, c_, s_ = heads(rot[:, m, :]), heads(qc[:, m, :]), heads(qsn[:, m, :])
                    dve.tensor_tensor(out[:, :, 0:half], c_[:, :, 0:half], s_[:, :, half:], ALU.subtract).then_inc(rotated, 1)
                    dve.tensor_tensor(out[:, :, half:], c_[:, :, half:], s_[:, :, 0:half], ALU.add).then_inc(rotated, 1)
                dve.wait_ge(made, t * 3 + 3)
                dve.tensor_tensor(vz[:, ds(t, 1), :, 0:a.hd].rearrange("p o h d -> p (o h) d"), heads(pq[:, 2, :]),
                                  heads(brow[:, 2 * a.n_q:3 * a.n_q]), ALU.add).then_inc(v_out, 1)

            def low(t):
                for m in range(2):
                    dve.wait_ge(hi, t * 2 + m + 1)
                    dve.tensor_tensor(qk[:, m, :, 1, ds(t * P, P)], pt[:, m, :].rearrange("p (c t) -> p c t", t=P),
                                      qk[:, m, :, 0, ds(t * P, P)], ALU.subtract).then_inc(lo, 1)
            tiles_and_last(dve, step, low)

        @block.gpsimd
        def _(pool):
            pool.memset(vz[:, :, :, :], 0.0).then_inc(padded, 1)
            pool.wait_ge(padded, 1)
            pool.memset(vz[:, :, :, a.hd:a.hd + 1], 1.0).then_inc(ones_set, 1)

            def step(t):
                for m in range(2):
                    pool.wait_ge(biased, t * 2 + m + 3)
                    pool.wait_ge(rotated, t * 4 + 2 * m + 2)
                    pool.tensor_tensor(heads(qsn[:, m, :]), heads(qb[:, m, :]), table(sin, t), ALU.mult).then_inc(sined, 1)
            for t in range(NT):
                step(t)

        @block.scalar
        def _(act):
            def step(t):
                for m in range(2):
                    act.wait_ge(turned, t * 2 + m + 3)
                    act.activation(qk[:, m, :, 0, ds(t * P, P)], pt[:, m, :].rearrange("p (c t) -> p c t", t=P),
                                   ACT.Copy).then_inc(hi, 1)
            tiles(act, step)

        @block.sync
        def _(sp):
            for b in range(NB):
                sp.wait_ge(lo, 2 * NI * (b + 1) + 2)
                for m in range(2):
                    for c in range(KC):
                        sp.dma_start(g.qk_dram[b, :, m * a.n_q + c * P:m * a.n_q + (c + 1) * P, :]
                                     .rearrange("two p t -> p two t"), qk[:, m, c, :, b * T:(b + 1) * T]).then_inc(stored, 16)
            sp.wait_ge(stored, 16 * NB * 2 * KC)


def gated_residual(nc, tag, g, multiply, row=None, store=None):
    with Phase(nc, tag, "made free biased silued gated added stored") as (
            block, made, free, biased, silued, gated, added, stored), \
            nc.psum_tensor(f"{tag}_pf", [P, 2, BANK], F32) as pf, \
            nc.sbuf_tensor(f"{tag}_gl", [P, 2, D], F32) as gl:

        def tiles(eng, step):
            with eng.Fori(0, NT // 2) as tt:
                for u in range(2):
                    step(eng.snap(tt * 2 + u), u)

        if store is not None:
            @block.sync
            def _(sp):
                for part in range(0, NT, 2):
                    sp.wait_ge(added, part + 2 + 2)
                    sp.dma_start(store[:, part:part + 2, :], g.x_res[:, part:part + 2, :]).then_inc(stored, 16)
                sp.wait_ge(stored, 16 * (NT // 2))

        @block.tensor
        def _(pe):
            def step(t, u):
                pe.wait_ge(free, t + 1)
                multiply(pe, pf[:, u, :], t).then_inc(made, 1)
            tiles(pe, step)

        @block.scalar
        def _(act):
            def step(t, u):
                if row is None:
                    act.wait_ge(added, t + 1)
                    act.wait_ge(made, t + 1)
                    act.activation(gl[:, u, :], pf[:, u, :], ACT.Silu).then_inc(silued, 1)
                else:
                    act.wait_ge(biased, t + 1)
                    act.activation(gl[:, u, :], gl[:, u, :], ACT.Silu).then_inc(silued, 1)
            tiles(act, step)

        @block.vector
        def _(dve):
            dve.sem_inc(added, 2)
            dve.sem_inc(free, 2)

            def step(t, u):
                if row is not None:
                    dve.wait_ge(added, t + 1)
                    dve.wait_ge(made, t + 1)
                    dve.tensor_tensor(gl[:, u, :], pf[:, u, :], row, ALU.add).then_inc(biased, 1)
                dve.wait_ge(silued, t + 1)
                dve.sem_inc(free, 1)
                dve.tensor_tensor(gl[:, u, :], gl[:, u, :], g.att[:, ds(t, 1), :].rearrange("p o d -> p (o d)"),
                                  ALU.mult).then_inc(gated, 1)
                dve.wait_ge(gated, t + 1)
                x = g.x_res[:, ds(t, 1), :].rearrange("p o d -> p (o d)")
                dve.tensor_tensor(x, x, gl[:, u, :], ALU.add).then_inc(added, 1)
            tiles(dve, step)



def stack_low_rank(nc, pool, low, stage, parts, stack):
    rank, columns = low.shape
    sv = 2 * D + (columns - 3 * D) // 3
    here, split, stacked = (nc.alloc_semaphore(f"low_{n}") for n in ("here", "split", "stacked"))
    Phase.held += [here, split, stacked]
    for half in range(2):
        own = slice(half * columns // 2, (half + 1) * columns // 2)
        pool.dma_start(stage[:, :], low[:, own]).then_inc(here, 16)
        pool.wait_ge(here, 16 * (half + 1))
        pool.tensor_copy(parts[:, 0, own], stage[:, :]).then_inc(split, 1)
        pool.wait_ge(split, 2 * half + 1)
        pool.tensor_tensor(parts[:, 1, own], stage[:, :], parts[:, 0, own], ALU.subtract).then_inc(split, 1)
        pool.wait_ge(split, 2 * half + 2)
    for cols, which in ((slice(0, sv), (0, 1, 0)), (slice(sv, columns), (0, 0, 1))):
        for r, part in enumerate(which):
            pool.dma_start(stack[r * rank:(r + 1) * rank, cols], parts[:, part, cols]).then_inc(stacked, 16)
    pool.wait_ge(stacked, 16 * 6)


def swiglu_low_rank(nc, g, ins, stack):
    rows = stack.shape[0]
    width = ins["L0_down"].shape[1] // D * P
    sv_gu, sv_d = stack[:, 0:2 * D], stack[:, 2 * D:2 * D + width]
    su_gu, su_d = stack[:, 2 * D + width:2 * D + 3 * width], stack[:, 2 * D + 3 * width:]
    n_i = width // P
    gu = KC * 2 * P
    down = D
    with nc.sbuf_tensor("f0_dt", [P, 2, n_i, NT * P], F16) as dt, \
            nc.sbuf_tensor("f0_wd", [P, 2, n_i, D], F16) as wd:
        with nc.sbuf_tensor("f0_ws", [P, 2, gu + down], F32) as ws, \
                nc.sbuf_tensor("f0_wgu", [P, 2, 2, gu], F16) as wgu, \
                nc.sbuf_tensor("f0_sd", [P, NB, T], F32) as sd, \
                nc.sbuf_tensor("f0_svd", [rows, 2, P], F16) as svd, \
                nc.psum_tensor("f0_pr", [P, 3 * BANK], F32) as pr, \
                nc.psum_tensor("f0_pp", [P, NB, 2, BANK], F32) as pp, \
                Phase(nc, "f0", "w_here0 w_here1 low weffed hi lo paired silued gated d_hi d_lo") as (
                block, w_here0, w_here1, low, weffed, hi, lo, paired, silued, gated, d_hi, d_lo):
            w_here = (w_here0, w_here1)

            def pipeline(eng, prepare, use):
                prepare(0, 0, 0)
                for i in range(2):
                    prepare(i + 1, (i + 1) % 2, (i + 1) // 2)
                    use(i, i)
                with eng.Fori(1, n_i // 2 - 1) as ii:
                    i = eng.snap(ii * 2)
                    after = eng.snap(ii * 2 + 1)
                    prepare(after, 1, ii)
                    use(i, 0)
                    prepare(eng.snap(ii * 2 + 2), 0, ii + 1)
                    use(after, 1)
                prepare(n_i - 1, 1, n_i // 2 - 1)
                use(n_i - 2, 0)
                use(n_i - 1, 1)

            @block.sync
            def _(sp):
                def load(i, u, k):
                    wait_pos(sp, lo, i - 1)
                    sp.dma_start(ws[:, u, 0:gu].rearrange("p (c n) -> p c n", c=KC),
                                 ins["L0_gu"][:, ds(i * KC * 2 * P, KC * 2 * P)].rearrange("p (c n) -> p c n", c=KC))\
                        .then_inc(w_here[u], 16)
                    sp.dma_start(ws[:, u, gu:gu + down], ins["L0_down"][:, ds(i * D, D)]).then_inc(w_here[u], 16)
                    sp.dma_start(svd[:, u, :], sv_d[:, ds(i * P, P)]).then_inc(w_here[u], 16)
                pipeline(sp, load, lambda i, u: None)

            @block.tensor
            def _(pe):
                def low_rank(i, u, k):
                    wait_pos(pe, weffed, i)
                    pe.wait_ge(w_here[u], (k + 1) * 48)
                    for c in range(KC):
                        for m in range(2):
                            at = (c * 2 + m) * P
                            pe.matmul(pr[:, at:at + P], sv_gu[:, m * D + c * P:m * D + (c + 1) * P],
                                      su_gu[:, ds(i * 2 * P + m * P, P)], start=True, stop=True)
                    pe.matmul(pr[:, gu:gu + down], svd[:, u, :], su_d, start=True, stop=True).then_inc(low, 1)

                def gate_and_up(i, u):
                    pe.wait_ge(lo, i + 1)
                    for b in range(NB):
                        wait_pos(pe, gated, i * 2 - 1 + b)
                        for m in range(2):
                            mm = product(pe, pp[:, b, m, :],
                                         lambda part, c: wgu[:, u, part, (c * 2 + m) * P:(c * 2 + m + 1) * P],
                                         lambda part, c: g.xt[:, part, c, b * T:(b + 1) * T], range(KC))
                        mm.then_inc(paired, 1)
                pipeline(pe, low_rank, gate_and_up)

            @block.vector
            def _(dve):
                def effective(i, u, k):
                    dve.wait_ge(low, i + 1)
                    dve.wait_ge(w_here[u], (k + 1) * 48)
                    dve.tensor_tensor(ws[:, u, :], ws[:, u, :], pr[:, :], ALU.mult).then_inc(weffed, 1)

                def gate(i, u):
                    for b in range(NB):
                        dve.wait_ge(silued, i * 2 + b + 1)
                        dve.tensor_tensor(sd[:, b, :], sd[:, b, :], pp[:, b, 1, :], ALU.mult).then_inc(gated, 1)
                pipeline(dve, effective, gate)

            @block.scalar
            def _(act):
                def high(i, u, k):
                    act.wait_ge(weffed, i + 1)
                    wait_pos(act, paired, (i - 1) * 2)
                    act.activation(wgu[:, u, 0, :], ws[:, u, 0:gu], ACT.Copy).then_inc(hi, 1)
                    act.activation(wd[:, 0, ds(i, 1), :], ws[:, u:u + 1, gu:gu + down], ACT.Copy).then_inc(hi, 1)

                def silu(i, u):
                    for b in range(NB):
                        wait_pos(act, d_lo, i * 2 - 1 + b)
                        act.wait_ge(paired, i * 2 + b + 1)
                        act.activation(sd[:, b, :], pp[:, b, 0, :], ACT.Silu).then_inc(silued, 1)
                        act.wait_ge(gated, i * 2 + b + 1)
                        act.activation(dt[:, 0, ds(i, 1), b * T:(b + 1) * T], sd[:, b:b + 1, :], ACT.Copy).then_inc(d_hi, 1)
                pipeline(act, high, silu)

            @block.gpsimd
            def _(pool):
                def low_part(i, u, k):
                    pool.wait_ge(hi, (i + 1) * 2)
                    pool.tensor_tensor(wd[:, 1, ds(i, 1), :], ws[:, u:u + 1, gu:gu + down], wd[:, 0, ds(i, 1), :],
                                       ALU.subtract)
                    pool.tensor_tensor(wgu[:, u, 1, :], ws[:, u, 0:gu], wgu[:, u, 0, :], ALU.subtract).then_inc(lo, 1)

                def gated_low(i, u):
                    for b in range(NB):
                        pool.wait_ge(d_hi, i * 2 + b + 1)
                        pool.tensor_tensor(dt[:, 1, ds(i, 1), b * T:(b + 1) * T], sd[:, b:b + 1, :],
                                           dt[:, 0, ds(i, 1), b * T:(b + 1) * T], ALU.subtract).then_inc(d_lo, 1)
                pipeline(pool, low_part, gated_low)

        gated_residual(nc, "g0", g, lambda pe, out, t: product(
            pe, out, lambda part, j: dt[:, part, j, ds(t * P, P)], lambda part, j: wd[:, part, j, :], range(n_i)))


def hyper_connections(nc, g, ins, w24, wb, base, gate, binary):
    n, iters, inv_tau, eps = 4, 50, 10.0, 1.1920929e-07
    nl = n * n + 2 * n
    with nc.sbuf_tensor("h_mix", [P, NT, n * n], F32) as mix, \
            nc.sbuf_tensor("h_pp", [P, NT, 2 * n], F32) as pp:
        with binary, nc.psum_tensor("h_pl", [P, NT * nl], F32) as pl, \
                nc.sbuf_tensor("h_sq", [P, 2, D], F32) as sq, \
                nc.sbuf_tensor("h_ss", [P, NT], F32) as ss, \
                nc.sbuf_tensor("h_rr", [P, NT], F32) as rr, \
                nc.sbuf_tensor("h_lg", [P, NT, nl], F32) as lg, \
                nc.sbuf_tensor("h_m4", [P, NT * n], F32) as m4, \
                nc.sbuf_tensor("h_i4", [P, NT * n], F32) as i4, \
                nc.sbuf_tensor("h_m2", [P, NT, 2], F32) as m2, \
                nc.sbuf_tensor("h_i2", [P, NT * 2], F32) as i2, \
                nc.sbuf_tensor("h_gt", [P, 3], F32) as gt, \
                Phase(nc, "hs", "made squared meaned rooted centred exped gate_exped done balanced") as (
                block, made, squared, meaned, rooted, centred, exped, gate_exped, done, balanced):

            @block.sync
            def _(sp):
                binary.load(sp)

            @block.tensor
            def _(pe):
                for t in range(NT):
                    mm = product(pe, pl[:, t * nl:(t + 1) * nl], lambda part, c: g.xt[:, part, c, t * P:(t + 1) * P],
                                 lambda part, c: w24[:, part, c, :], range(KC))
                mm.then_inc(made, 1)
                binary.sums(pe)

            @block.scalar
            def _(act):
                for t in range(NT):
                    wait_pos(act, squared, t - 1)
                    act.activation(sq[:, t % 2, :], g.xn[:, t, :], ACT.Square, accum_out=ss[:, t:t + 1]).then_inc(squared, 1)
                act.activation(gt[:, 0:1], gate[:, :], ACT.Exp, scale=-1.0).then_inc(gate_exped, 1)
                act.wait_ge(meaned, 1)
                act.activation(ss[:, :], ss[:, :], ACT.Sqrt).then_inc(rooted, 1)
                act.wait_ge(centred, 2)
                act.activation(mix[:, :, :], mix[:, :, :], ACT.Exp, scale=inv_tau).then_inc(exped, 1)
                act.activation(pp[:, :, :], pp[:, :, :], ACT.Exp).then_inc(exped, 1)
                binary.signs(act)

            @block.vector
            def _(dve):
                count = 0

                def chain(ins_):
                    nonlocal count
                    count += 1
                    ins_.then_inc(done, 1)
                    dve.wait_ge(done, count)

                dve.wait_ge(squared, NT)
                dve.tensor_scalar(ss[:, :], ss[:, :], 1.0 / D, eps, ALU.mult, ALU.add).then_inc(meaned, 1)
                dve.wait_ge(rooted, 1)
                chain(dve.reciprocal(rr[:, :], ss[:, :]))
                dve.wait_ge(made, 1)
                chain(dve.tensor_tensor(lg[:, :, :], pl.rearrange("p (t n) -> p t n", n=nl),
                                        rr[:, :].unsqueeze(2).to_broadcast([P, NT, nl]), ALU.mult))
                chain(dve.tensor_tensor(lg[:, :, :], lg[:, :, :], base[:, :].unsqueeze(1).to_broadcast([P, NT, nl]), ALU.add))
                res = lg[:, :, 0:n * n].rearrange("p t (i j) -> p t i j", j=n)
                two = lg[:, :, n * n:].rearrange("p t (i j) -> p t i j", j=n)
                chain(dve.tensor_reduce(m4[:, :], res, AX.X, ALU.max))
                chain(dve.tensor_reduce(m2[:, :, :], two, AX.X, ALU.max))
                two_p = pp[:, :, :].rearrange("p t (i j) -> p (t i) j", j=n)
                dve.tensor_tensor(mix[:, :, :].rearrange("p t (i j) -> p t i j", j=n), res,
                                  m4[:, :].rearrange("p (t i) -> p t i", i=n).unsqueeze(3).to_broadcast([P, NT, n, n]),
                                  ALU.subtract).then_inc(centred, 1)
                dve.tensor_tensor(pp[:, :, :].rearrange("p t (i j) -> p t i j", j=n), two,
                                  m2[:, :, :].unsqueeze(3).to_broadcast([P, NT, 2, n]), ALU.subtract).then_inc(centred, 1)
                dve.wait_ge(exped, 2)
                chain(dve.tensor_reduce(m2[:, :, :].rearrange("p t i -> p (t i)"), two_p, AX.X, ALU.add))
                chain(dve.reciprocal(i2[:, :], m2[:, :, :].rearrange("p t i -> p (t i)")))
                chain(dve.tensor_tensor(two_p, two_p, i2[:, :].unsqueeze(2).to_broadcast([P, NT * 2, n]), ALU.mult))
                dve.sem_inc(balanced, 2)
                with dve.Fori(0, iters) as it:
                    for k in range(6):
                        for half in range(2):
                            tiles = slice(half * NI, (half + 1) * NI)
                            own = slice(half * NI * n, (half + 1) * NI * n)
                            dve.wait_ge(balanced, it * 12 + (2 * k + half + 1))
                            byrow = mix[:, tiles, :].rearrange("p t (i j) -> p (t i) j", j=n)
                            bycol = mix[:, tiles, :].rearrange("p t (i j) -> p t j i", j=n)
                            sums, inverse = m4[:, own], i4[:, own]
                            if k == 0:
                                op = dve.tensor_reduce(sums, byrow, AX.X, ALU.add)
                            elif k == 3:
                                op = dve.tensor_reduce(sums.rearrange("p (t j) -> p t j", j=n), bycol, AX.X, ALU.add)
                            elif k == 2:
                                op = dve.tensor_tensor(byrow, byrow, inverse.unsqueeze(2).to_broadcast([P, NI * n, n]),
                                                       ALU.mult)
                            elif k == 5:
                                op = dve.tensor_tensor(bycol, bycol, inverse.rearrange("p (t j) -> p t j", j=n)
                                                       .unsqueeze(3).to_broadcast([P, NI, n, n]), ALU.mult)
                            else:
                                op = dve.reciprocal(inverse, sums)
                            op.then_inc(balanced, 1)
                dve.wait_ge(balanced, 12 * iters + 2)
                binary.scales(dve)
                dve.wait_ge(gate_exped, 1)
                chain(dve.tensor_scalar(gt[:, 0:1], gt[:, 0:1], 1.0, None, ALU.add))
                chain(dve.reciprocal(gt[:, 1:2], gt[:, 0:1]))
                chain(dve.tensor_scalar(gt[:, 2:3], gt[:, 1:2], -1.0, 1.0, ALU.mult, ALU.add))
                chain(dve.tensor_scalar(mix[:, :, :], mix[:, :, :], gt[:, 1:2], None, ALU.mult))
                chain(dve.tensor_scalar(mix[:, :, 0:n * n:n + 1], mix[:, :, 0:n * n:n + 1], gt[:, 2:3], None, ALU.add))

        with nc.sbuf_tensor("h_xp", [P, NT, P], F32) as xp, \
                nc.sbuf_tensor("h_xpt", [P, 2, NT * P], F16) as xpt, \
                nc.sbuf_tensor("h_om", [P, NI, D], F32) as om, \
                nc.psum_tensor("h_pt", [P, 2, BANK], F32) as pt, \
                nc.psum_tensor("h_py", [P, NT, P], F32) as py, \
                Phase(nc, "hm", "pre turned hi lo branched posted mixed silued gated added passed") as (
                block, pre, turned, hi, lo, branched, posted, mixed, silued, gated, added, passed):

            @block.vector
            def _(dve):
                for s in range(n):
                    for t in range(NT):
                        x_s = g.xn[:, t, s * P:(s + 1) * P]
                        if s == 0:
                            dve.tensor_scalar(xp[:, t, :], x_s, pp[:, t, 0:1], None, ALU.mult).then_inc(pre, 1)
                        else:
                            dve.wait_ge(pre, (s - 1) * NT + t + 1)
                            dve.scalar_tensor_tensor(out=xp[:, t, :], in0=x_s, scalar=pp[:, t, s:s + 1], in1=xp[:, t, :],
                                                     op0=ALU.mult, op1=ALU.add).then_inc(pre, 1)
                for k in range(2):
                    dve.wait_ge(hi, k + 1)
                    dve.tensor_tensor(xpt[:, 1, k * BANK:(k + 1) * BANK], pt[:, k, :], xpt[:, 0, k * BANK:(k + 1) * BANK],
                                      ALU.subtract).then_inc(lo, 1)
                def mix_streams(t, u):
                    dve.wait_ge(posted, t + 1)
                    xt_ = g.xn[:, ds(t, 1), :].rearrange("p o d -> p (o d)")
                    h_ = mix[:, ds(t, 1), :].rearrange("p o d -> p (o d)")
                    for j in range(n):
                        for i in range(n):
                            o = om[:, u, i * P:(i + 1) * P]
                            if j > 0:
                                dve.wait_ge(mixed, t * (n * n) + (j - 1) * n + i + 1)
                            dve.scalar_tensor_tensor(out=o, in0=xt_[:, j * P:(j + 1) * P],
                                                     scalar=h_[:, i * n + j:i * n + j + 1], in1=o,
                                                     op0=ALU.mult, op1=ALU.add).then_inc(mixed, 1)
                with dve.Fori(0, NT // NI) as tt:
                    for u in range(NI):
                        mix_streams(dve.snap(tt * NI + u), u)

            @block.gpsimd
            def _(pool):
                pool.sem_inc(added, NI)
                with pool.Fori(0, NT // NI) as tt:
                    for u in range(NI):
                        t = pool.snap(tt * NI + u)
                        pool.wait_ge(silued, t + 1)
                        pool.sem_inc(passed, 1)
                        pool.tensor_tensor(om[:, u, :], om[:, u, :], g.att[:, ds(t, 1), :].rearrange("p o d -> p (o d)"),
                                           ALU.mult).then_inc(gated, 1)
                        pool.wait_ge(gated, t + 1)
                        pool.sem_inc(passed, 1)
                        x = g.x_res[:, ds(t, 1), :].rearrange("p o d -> p (o d)")
                        pool.tensor_tensor(x, x, om[:, u, :], ALU.add).then_inc(added, 1)

            @block.tensor
            def _(pe):
                for t in range(NT):
                    pe.wait_ge(pre, (n - 1) * NT + t + 1)
                    pe.transpose(pt[:, t // NI, (t % NI) * P:(t % NI + 1) * P], xp[:, t, :], g.ident[:, :]).then_inc(turned, 1)
                pe.wait_ge(lo, 2)
                for t in range(NT):
                    mm = product(pe, py[:, t, :], lambda part, c: xpt[:, part, t * P:(t + 1) * P],
                                 lambda part, c: wb[:, part, :], range(1))
                mm.then_inc(branched, 1)

            @block.scalar
            def _(act):
                for k in range(2):
                    act.wait_ge(turned, (k + 1) * NI)
                    act.activation(xpt[:, 0, k * BANK:(k + 1) * BANK], pt[:, k, :], ACT.Copy).then_inc(hi, 1)
                act.wait_ge(branched, 1)
                with act.Fori(0, NT // NI) as tt:
                    for u in range(NI):
                        t = act.snap(tt * NI + u)
                        act.wait_ge(added, t + 1)
                        w_ = pp[:, ds(t, 1), :].rearrange("p o d -> p (o d)")
                        for i in range(n):
                            op = act.activation(om[:, u, i * P:(i + 1) * P], py[:, ds(t, 1), :].rearrange("p o d -> p (o d)"),
                                                ACT.Copy, scale=w_[:, n + i:n + i + 1])
                        op.then_inc(posted, 1)
                    for u in range(NI):
                        act.wait_ge(mixed, (tt * NI + u + 1) * (n * n))
                        act.activation(om[:, u, :], om[:, u, :], ACT.Silu).then_inc(silued, 1)


def routed_lora(nc, tag, g, w_ra, top, wt, e, r):
    er = e * r
    with nc.psum_tensor(f"{tag}_ph", [P, 2, BANK], F32) as ph, \
            nc.psum_tensor(f"{tag}_pt", [P, 2, BANK], F32) as pt, \
            nc.sbuf_tensor(f"{tag}_lg", [P, NT, e], F32) as lg, \
            nc.sbuf_tensor(f"{tag}_hh", [P, NT, er], F32) as hh, \
            nc.sbuf_tensor(f"{tag}_m", [P, NT], F32) as m, \
            nc.sbuf_tensor(f"{tag}_s", [P, NT], F32) as s, \
            nc.sbuf_tensor(f"{tag}_e", [P, NT, e], F32) as eq, \
            nc.sbuf_tensor(f"{tag}_o", [P, 2, NT, e], F32) as one, \
            nc.sbuf_tensor(f"{tag}_p", [P, NT, e], F32) as pb, \
            nc.sbuf_tensor(f"{tag}_w", [P, NT, e], F32) as wgt, \
            Phase(nc, tag, "made h_out l_out centred exped done weighted turned hi lo") as (
            block, made, h_out, l_out, centred, exped, done, weighted, turned, hi, lo):

        @block.tensor
        def _(pe):
            with pe.Fori(0, NT // 2) as tt:
                for u in range(2):
                    t = pe.snap(tt * 2 + u)
                    pe.wait_ge(l_out, t + 1)
                    pe.wait_ge(h_out, t + 1)
                    product(pe, ph[:, u, 0:e + er], lambda part, c: g.xt[:, part, c, ds(t * P, P)],
                            lambda part, c: w_ra[:, part, c, :], range(KC)).then_inc(made, 1)
            pe.wait_ge(weighted, 1)
            for t in range(NT):
                pe.transpose(pt[:, t // NI, (t % NI) * P:(t % NI + 1) * P], hh[:, t, :], g.ident[:, :]).then_inc(turned, 1)

        @block.scalar
        def _(act):
            act.sem_inc(h_out, 2)
            with act.Fori(0, NT // 2) as tt:
                for u in range(2):
                    t = act.snap(tt * 2 + u)
                    act.wait_ge(made, t + 1)
                    act.wait_ge(l_out, t + 3)
                    act.activation(hh[:, ds(t, 1), :], ph[:, u:u + 1, e:e + er], ACT.Copy).then_inc(h_out, 1)
            if top == 2:
                act.wait_ge(centred, 1)
                act.activation(pb[:, :, :], pb[:, :, :], ACT.Exp).then_inc(exped, 1)
            for k in range(2):
                act.wait_ge(turned, (k + 1) * NI)
                act.activation(wt[:, 0, k * BANK:(k + 1) * BANK], pt[:, k, :], ACT.Copy).then_inc(hi, 1)

        @block.vector
        def _(dve):
            count = 0

            def chain(ins_):
                nonlocal count
                count += 1
                ins_.then_inc(done, 1)
                dve.wait_ge(done, count)

            def over(v):
                return v.unsqueeze(2).to_broadcast([P, NT, e])

            def largest(values, mark):
                chain(dve.tensor_reduce(m[:, :], values, AX.X, ALU.max))
                chain(dve.tensor_tensor(eq[:, :, :], values, over(m[:, :]), ALU.is_equal))
                chain(dve.tensor_tensor(eq[:, :, :], eq[:, :, :], g.rank[:, :].unsqueeze(1).to_broadcast([P, NT, e]), ALU.mult))
                chain(dve.tensor_reduce(s[:, :], eq[:, :, :], AX.X, ALU.max))
                chain(dve.tensor_tensor(mark, eq[:, :, :], over(s[:, :]), ALU.is_equal))

            dve.sem_inc(l_out, 2)
            with dve.Fori(0, NT // 2) as tt:
                for u in range(2):
                    t = dve.snap(tt * 2 + u)
                    dve.wait_ge(made, t + 1)
                    dve.tensor_copy(lg[:, ds(t, 1), :], ph[:, u:u + 1, 0:e]).then_inc(l_out, 1)
            dve.wait_ge(l_out, NT + 2)
            if top == 1:
                largest(lg[:, :, :], one[:, 0, :, :])
                chain(dve.tensor_tensor(wgt[:, :, :], one[:, 0, :, :], over(m[:, :]), ALU.mult))
            else:
                chain(dve.tensor_reduce(m[:, :], lg[:, :, :], AX.X, ALU.max))
                dve.tensor_tensor(pb[:, :, :], lg[:, :, :], over(m[:, :]), ALU.subtract).then_inc(centred, 1)
                dve.wait_ge(exped, 1)
                chain(dve.tensor_reduce(s[:, :], pb[:, :, :], AX.X, ALU.add))
                chain(dve.reciprocal(m[:, :], s[:, :]))
                chain(dve.tensor_tensor(pb[:, :, :], pb[:, :, :], over(m[:, :]), ALU.mult))
                largest(pb[:, :, :], one[:, 0, :, :])
                chain(dve.scalar_tensor_tensor(out=lg[:, :, :], in0=one[:, 0, :, :], scalar=-2.0, in1=pb[:, :, :],
                                               op0=ALU.mult, op1=ALU.add))
                largest(lg[:, :, :], one[:, 1, :, :])
                chain(dve.tensor_tensor(eq[:, :, :], one[:, 0, :, :], one[:, 1, :, :], ALU.add))
                chain(dve.tensor_tensor(wgt[:, :, :], pb[:, :, :], eq[:, :, :], ALU.mult))
                chain(dve.tensor_reduce(s[:, :], wgt[:, :, :], AX.X, ALU.add))
                chain(dve.reciprocal(m[:, :], s[:, :]))
                chain(dve.tensor_tensor(wgt[:, :, :], wgt[:, :, :], over(m[:, :]), ALU.mult))
                chain(dve.tensor_scalar(wgt[:, :, :], wgt[:, :, :], 2.0, None, ALU.mult))
            dve.wait_ge(h_out, NT + 2)
            h4 = hh[:, :, :].rearrange("p t (e r) -> p (t e) r", r=r)
            dve.tensor_tensor(h4, h4, wgt[:, :, :].rearrange("p t e -> p (t e)").unsqueeze(2)
                              .to_broadcast([P, NT * e, r]), ALU.mult).then_inc(weighted, 1)
            for k in range(2):
                dve.wait_ge(hi, k + 1)
                dve.tensor_tensor(wt[:, 1, k * BANK:(k + 1) * BANK], pt[:, k, :], wt[:, 0, k * BANK:(k + 1) * BANK],
                                  ALU.subtract).then_inc(lo, 1)


class Shared:
    pass


def build(nc, ins, out):
    g = Shared()
    Phase.held = []
    with ExitStack() as top:
        def sb(name, shape, dtype, stack=top):
            return stack.enter_context(nc.sbuf_tensor(name, shape, dtype))

        g.ident = sb("ident", [P, P], F32)
        g.ident_b = sb("ident_b", [P, P], BF16)
        g.mask_qk = sb("mask_qk", [P, P], BF16)
        g.mask_kq = sb("mask_kq", [P, P], BF16)
        g.ones = sb("ones", [P, P], F32)
        g.x_res = sb("x_res", [P, NT, D], F32)
        g.att = sb("att", [P, NT, D], F32)
        g.xt = sb("xt", [P, 2, KC, NT * P], F16)
        g.qk_dram = nc.dram_tensor("qk_scratch", [NB, 2, 2 * D, T], F16).ap()
        load_constants(nc, g, ins)

        def by_chunk(name, chunks=KC):
            return ins[name].rearrange("(c p) n -> p c n", c=chunks)

        x_tiles = ins["x"].rearrange("b (i p) d -> p (b i) d", p=P)
        layer_2 = Heads(32, 8, 16, False, 0.25, binary=True)
        for layer in range(4):
            if layer == 1:
                signs = ExitStack()
                binary = BinaryWeights(nc, signs, g, layer_2, by_chunk("L2_w"), ins["L2_qk_scale"], ins["L2_row_scale"])
            with ExitStack() as st:
                def lsb(name, shape, dtype, st=st):
                    return sb(f"l{layer}_{name}", shape, dtype, st)

                if layer == 0:
                    a = Heads(32, 1, 16, True, 0.25)
                elif layer == 1:
                    a = Heads(8, 8, 32, True, 1.0)
                elif layer == 2:
                    a = layer_2
                else:
                    a = Heads(32, 32, 16, True, 0.25)
                nch = -(-a.n_qk // P)
                kc_o = a.n_q // P
                if layer == 1:
                    g.xn = lsb("xn", [P, NT, D], F32)
                    w24 = lsb("w24", [P, 2, KC, 24], F16)
                    wb = lsb("wb", [P, 2, P], F16)
                    base = lsb("base", [P, 24], F32)
                    gate = lsb("gate", [P, 1], F32)
                if layer >= 2:
                    w_ra = lsb("w_ra", [P, 2, KC, 8 + P], F16)
                    w_b = lsb("w_b", [P, 2, 1, D], F16)
                    g.rank = lsb("rank", [P, 8], F32)
                if layer == 3:
                    w_base = lsb("w_base", [P, 2, KC, D], F16)
                    base_row = lsb("base_row", [P, D], F32)
                if layer == 0:
                    rank, columns = ins["L0_low"].shape
                    low_stack = lsb("low_stack", [3 * rank, columns], F16)
                with ExitStack() as at:
                    def asb(name, shape, dtype, at=at):
                        return sb(f"a{layer}_{name}", shape, dtype, at)
                    pj = at.enter_context(ExitStack())

                    def psb(name, shape, dtype, pj=pj):
                        return sb(f"p{layer}_{name}", shape, dtype, pj)
                    vz = asb("vz", [P, NT, a.kv, a.vw], F32)
                    o_row = asb("o_row", [P, D], F32)
                    wts, small = [], []
                    if a.binary:
                        w, wo = binary.sign, binary.sign[:, :, :, a.n_all:]
                        col, v_row, o_row = binary.cols[:, :], binary.rows[:, 0:a.n_v], binary.rows[:, a.n_v:]
                    else:
                        wo = asb("wo", [P, 2, kc_o, D], F16)
                        w = psb("w", [P, 2, KC, a.n_all], F16)
                        small.append((o_row[:, :], ins[f"L{layer}_o_bias"].partition_broadcast(P)))
                        if layer == 3:
                            v_row = psb("qkv_row", [P, a.n_all], F32)
                            small.append((v_row[:, :], ins["L3_qkv_bias"].partition_broadcast(P)))
                            cos = psb("cos", [P, NT, a.hd], F32)
                            sin = psb("sin", [P, NT, a.hd], F32)
                            small += [(cos[:, :, :], ins["cos"]), (sin[:, :, :], ins["sin"])]
                            col = None
                        else:
                            v_row = psb("v_row", [P, a.n_v], F32)
                            col = psb("col", [P, nch], F32)
                            small += [(col[:, :], ins[f"L{layer}_qk_bias"]),
                                      (v_row[:, :], ins[f"L{layer}_v_bias"].partition_broadcast(P))]
                            col, v_row = col[:, :], v_row[:, :]
                        o_row = o_row[:, :]
                    if layer == 1:
                        small += [(base[:, :], ins["L1_base"].partition_broadcast(P)),
                                  (gate[:, :], ins["L1_gate"].partition_broadcast(P))]
                    if layer >= 2:
                        small.append((g.rank[:, :], ins["rank"].partition_broadcast(P)))
                    if layer == 3:
                        small.append((base_row[:, :], ins["L3_base_bias"].partition_broadcast(P)))
                    after = []
                    if not a.binary:
                        after += [(by_chunk(f"L{layer}_wo", kc_o)[:, c, :], wo[:, 0, c, :], wo[:, 1, c, :])
                                  for c in range(kc_o)]
                    if layer == 1:
                        after += [(by_chunk("L1_w24")[:, c, :], w24[:, 0, c, :], w24[:, 1, c, :]) for c in range(KC)]
                        after.append((ins["L1_wb"], wb[:, 0], wb[:, 1]))
                    if layer >= 2:
                        after += [(by_chunk(f"L{layer}_w_ra")[:, c, :], w_ra[:, 0, c, :], w_ra[:, 1, c, :])
                                  for c in range(KC)]
                        after.append((ins[f"L{layer}_w_b"], w_b[:, 0, 0, :], w_b[:, 1, 0, :]))
                    if layer == 3:
                        after += [(by_chunk("L3_w_base")[:, c, :], w_base[:, 0, c, :], w_base[:, 1, c, :])
                                  for c in range(KC)]
                    with ExitStack() as stg:
                        def ssb(name, shape, stg=stg):
                            return sb(f"s{layer}_{name}", shape, F32, stg)
                        if not a.binary:
                            s_ = ssb("w", [P, KC, a.n_all])
                            for c in range(KC):
                                wts.append((by_chunk(f"L{layer}_w")[:, c, :], s_[:, c, :],
                                            [(s_[:, c, :], w[:, 0, c, :], w[:, 1, c, :])]))
                        if layer != 1:
                            g.xn = ssb("xn", [P, NT, D])
                        norm_and_split(nc, f"n{layer}", g, wts, x_in=x_tiles if layer == 0 else None, small=small)
                    if layer == 3:
                        project_rotary(nc, "p3", g, a, w, vz, v_row[:, :], cos, sin)
                    else:
                        project(nc, f"p{layer}", g, a, w, vz, col, v_row)
                    pj.close()
                    after_stage = asb("after_stage", [P, D // 2], F32)
                    if layer == 0:
                        low = ins["L0_low"]
                        low_stage = asb("low_stage", [rank, columns // 2], F32)
                        low_parts = asb("low_parts", [rank, 2, columns], F16)

                    def beside(pool):
                        split_beside(nc, pool, f"after{layer}", after_stage, after)
                        if layer == 0:
                            stack_low_rank(nc, pool, low, low_stage, low_parts, low_stack)
                    attention(nc, f"a{layer}", g, a, vz, wo, o_row, beside)
                if layer == 0:
                    swiglu_low_rank(nc, g, ins, low_stack)
                elif layer == 1:
                    hyper_connections(nc, g, ins, w24, wb, base, gate, binary)
                else:
                    wt = lsb("wt", [P, 2, NT * P], F16)
                    routed_lora(nc, f"r{layer}", g, w_ra, layer - 1, wt, 8, 16)

                    def multiply(pe, psum, t):
                        if layer == 3:
                            product(pe, psum, lambda part, c: g.xt[:, part, c, ds(t * P, P)],
                                    lambda part, c: w_base[:, part, c, :], range(KC), last=False)
                        return product(pe, psum, lambda part, c: wt[:, part, ds(t * P, P)],
                                       lambda part, c: w_b[:, part, 0, :], range(1), first=layer != 3)
                    if layer == 3:
                        gated_residual(nc, "g3", g, multiply, base_row[:, :],
                                       out.rearrange("b (i p) d -> p (b i) d", p=P))
                    else:
                        gated_residual(nc, "g2", g, multiply)

            if layer == 2:
                signs.close()
            clear_semaphores(nc)


def lay_out(v):
    c = np.ascontiguousarray
    f = np.float32

    def by_column(bias):
        n = -(-bias.shape[0] // P)
        full = np.zeros((n * P,), f)
        full[:bias.shape[0]] = bias
        return c(full.reshape(n, P).T)

    cat = np.concatenate
    out = {"x": v["L0_attn_x"], "ident": np.eye(P, dtype=f), "rank": np.arange(8, 0, -1).astype(f)}
    out["L0_w"] = c(cat([v["L0_attn_wq_w"], v["L0_attn_wk_w"], v["L0_attn_wv_w"]]).T)
    out["L0_wo"] = c(v["L0_attn_wo_w"].T)
    out["L0_qk_bias"] = by_column(cat([v["L0_attn_wq_b"], v["L0_attn_wk_b"]]))
    out["L0_v_bias"] = v["L0_attn_wv_b"]
    out["L0_o_bias"] = v["L0_attn_wo_b"]
    gate, up, down = v["L0_ffn_gate_w"], v["L0_ffn_up_w"], v["L0_ffn_down_w"]
    width = gate.shape[0]
    n_i = width // P
    gu = np.stack([gate, up]).reshape(2, n_i, P, KC, P).transpose(4, 1, 3, 0, 2)
    out["L0_gu"] = c(gu.reshape(P, -1))
    out["L0_down"] = c(down.T.reshape(n_i, P, D).transpose(1, 0, 2).reshape(P, -1))
    out["L0_low"] = cat([v["L0_ffn_gate_sv"], v["L0_ffn_up_sv"], v["L0_ffn_down_sv"],
                         np.stack([v["L0_ffn_gate_su"], v["L0_ffn_up_su"]]).reshape(2, n_i, P, -1)
                         .transpose(3, 1, 0, 2).reshape(-1, 2 * width), v["L0_ffn_down_su"].T], axis=1)
    n1 = v["L1_attn_b_qkv"].shape[0] // 3
    out["L1_w"] = c(v["L1_attn_w_qkv"].T)
    out["L1_wo"] = c(v["L1_attn_w_o"].T)
    out["L1_qk_bias"] = by_column(v["L1_attn_b_qkv"][:2 * n1])
    out["L1_v_bias"] = v["L1_attn_b_qkv"][2 * n1:]
    out["L1_o_bias"] = v["L1_attn_b_o"]
    out["L1_w24"] = c(cat([v["L1_ffn_W_res"], v["L1_ffn_W_pre"], v["L1_ffn_W_post"]]).T)
    out["L1_base"] = cat([v["L1_ffn_H_res_base"].ravel(), v["L1_ffn_H_pre_base"], v["L1_ffn_H_post_base"]])
    out["L1_gate"] = v["L1_ffn_gate"]
    out["L1_wb"] = v["L1_ffn_W_branch"]
    out["L2_w"] = c(cat([v["L2_attn_q_weight"], v["L2_attn_k_weight"], v["L2_attn_v_weight"], v["L2_attn_o_weight"]]).T)
    out["L2_qk_scale"] = by_column(cat([v["L2_attn_q_scale"], v["L2_attn_k_scale"]]))
    out["L2_row_scale"] = cat([v["L2_attn_v_scale"], v["L2_attn_o_scale"]])
    out["L2_w_ra"] = c(cat([v["L2_ffn_route_w"], v["L2_ffn_A"].reshape(P, D)]).T)
    out["L2_w_b"] = c(v["L2_ffn_Bw"].transpose(0, 2, 1).reshape(P, D))
    out["L3_w"] = v["L3_attn_qkv_w"]
    out["L3_qkv_bias"] = v["L3_attn_qkv_b"]
    out["L3_wo"] = v["L3_attn_out_w"]
    out["L3_o_bias"] = v["L3_attn_out_b"]
    out["L3_w_ra"] = c(cat([v["L3_ffn_W_router"], v["L3_ffn_lora_A"].reshape(P, D)]).T)
    out["L3_w_b"] = c(v["L3_ffn_lora_B"].transpose(0, 2, 1).reshape(P, D))
    out["L3_w_base"] = c(v["L3_ffn_W_base"].T)
    out["L3_base_bias"] = v["L3_ffn_b_base"]
    half = 8
    inv = (1.0 / 10000.0 ** (np.arange(half, dtype=f) / f(half))).astype(f)
    ang = np.arange(T, dtype=f)[:, None] * inv[None, :]
    for name, fn in (("cos", np.cos), ("sin", np.sin)):
        tab = fn(ang).astype(f).reshape(NI, P, half).transpose(1, 0, 2)
        out[name] = c(np.tile(tab, (1, NB, 2)))
    return {k: c(x) for k, x in out.items()}


def kernel(**inputs):
    import concourse.bacc as bacc
    from concourse.bass_utils import run_bass_kernel_spmd

    nc = bacc.Bacc("TRN2", target_bir_lowering=False, num_devices=1)
    arrays = lay_out({k: np.asarray(x) for k, x in inputs.items()})
    ins = {k: nc.dram_tensor(f"in_{k}", x.shape, mybir.dt.from_np(x.dtype), kind="ExternalInput").ap() for k, x in arrays.items()}
    shape = inputs["L0_attn_x"].shape
    out = nc.dram_tensor("out", shape, F32, kind="ExternalOutput").ap()
    build(nc, ins, out)
    return run_bass_kernel_spmd(nc, [{f"in_{k}": x for k, x in arrays.items()}], core_ids=[0]).results[0]["out"]
```
